# Optimizing a Trainium2 kernel written in Bass

```python
import numpy as np
import jax
import jax.numpy as jnp

def _softmax(x, axis=-1):
    return jax.nn.softmax(x, axis=axis)

def _gelu(x):
    return jax.nn.gelu(x, approximate=True)

def _silu(x):
    return jax.nn.silu(x)

def _sigmoid(x):
    return jax.nn.sigmoid(x)

def _layernorm(x, axis=-1, eps=1e-05):
    m = jnp.mean(x, axis=axis, keepdims=True)
    v = jnp.var(x, axis=axis, keepdims=True)
    return (x - m) / jnp.sqrt(v + eps)

def _scatter_add(tgt, idx, src, axis=0):
    return tgt.at[idx].add(src)

def _segment_sum(src, seg, n):
    return jax.ops.segment_sum(src, seg, n)
kernel_name = 'mk_seq_preln_d2_jaxref_r4_af98d5'

def setup_inputs(seed: int=0):
    np.random.seed(seed)
    _w = jnp.asarray

    def _L0_attn_setup():
        import jax, jax.numpy as jnp
        import numpy as np
        B, L, H, NH = (2, 512, 512, 16)
        K = H // NH
        EPS = 1e-05
        SCALE = K ** (-0.5)

        def _gla(q, k, v, g):

            def step(S, xs):
                q_t, k_t, v_t, g_t = xs
                S = jnp.exp(g_t)[:, :, None] * S + k_t[:, :, None] * v_t[:, None, :]
                o_t = jnp.einsum('bk,bkv->bv', q_t, S)
                return (S, o_t)
            S0 = jnp.zeros((q.shape[0], q.shape[2], v.shape[2]), dtype=q.dtype)
            xs = (jnp.swapaxes(q, 0, 1), jnp.swapaxes(k, 0, 1), jnp.swapaxes(v, 0, 1), jnp.swapaxes(g, 0, 1))
            _, o = jax.lax.scan(step, S0, xs)
            return jnp.swapaxes(o, 0, 1)
        key = jax.random.key(seed)
        k0, k1, k2, k3, k4 = jax.random.split(key, 5)
        std = 0.02
        return {'hidden_states': jax.random.normal(k0, (B, L, H), dtype=jnp.float32), 'Wq': jax.random.normal(k1, (K, H), dtype=jnp.float32) * std, 'Wk': jax.random.normal(k2, (K, H), dtype=jnp.float32) * std, 'Wog': jax.random.normal(k3, (H, H), dtype=jnp.float32) * std, 'Wig': jax.random.normal(k4, (H, H), dtype=jnp.float32) * std, 'g_weight': jnp.ones((H,), dtype=jnp.float32)}
    _L0_attn_in = _L0_attn_setup()

    def _L0_ffn_setup():
        import jax, jax.numpy as jnp
        import numpy as np
        E = 16
        K = 2
        D = 512
        I = 352
        CAP = 256
        VOCAB = 32320
        key = jax.random.key(seed)
        ks = jax.random.split(key, 11)
        B, S = (4, 256)
        sd = 1.0 / np.sqrt(D)
        si = 1.0 / np.sqrt(I)
        return {'x': jax.random.normal(ks[0], (B, S, D), jnp.float32), 'input_ids': jax.random.randint(ks[1], (B, S), 0, VOCAB, dtype=jnp.int64), 'gate_w': jax.random.normal(ks[2], (E, D), jnp.float32) * sd, 'gate_b': jax.random.normal(ks[3], (E,), jnp.float32) * 0.01, 'W1': jax.random.normal(ks[4], (E, I, D), jnp.float32) * sd, 'W3': jax.random.normal(ks[5], (E, I, D), jnp.float32) * sd, 'W2': jax.random.normal(ks[6], (E, D, I), jnp.float32) * si, 'Ws1': jax.random.normal(ks[7], (I, D), jnp.float32) * sd, 'Ws3': jax.random.normal(ks[8], (I, D), jnp.float32) * sd, 'Ws2': jax.random.normal(ks[9], (D, I), jnp.float32) * si}
    _L0_ffn_in = _L0_ffn_setup()

    def _L1_attn_setup():
        import jax, jax.numpy as jnp
        import numpy as np
        D_MODEL = 512
        N_HEADS = 16
        D_K = D_MODEL // N_HEADS
        EPS = 1e-06
        key = jax.random.key(seed)
        ks = jax.random.split(key, 9)
        s = 1.0 / np.sqrt(D_MODEL)
        return {'x': jax.random.normal(ks[0], (4, 1024, D_MODEL), dtype=jnp.float32), 'Wq': jax.random.normal(ks[1], (D_MODEL, D_MODEL), dtype=jnp.float32) * s, 'bq': jnp.zeros((D_MODEL,), dtype=jnp.float32), 'Wk': jax.random.normal(ks[2], (D_MODEL, D_MODEL), dtype=jnp.float32) * s, 'bk': jnp.zeros((D_MODEL,), dtype=jnp.float32), 'Wv': jax.random.normal(ks[3], (D_MODEL, D_MODEL), dtype=jnp.float32) * s, 'bv': jnp.zeros((D_MODEL,), dtype=jnp.float32), 'Wo': jax.random.normal(ks[4], (D_MODEL, D_MODEL), dtype=jnp.float32) * s, 'bo': jnp.zeros((D_MODEL,), dtype=jnp.float32)}
    _L1_attn_in = _L1_attn_setup()

    def _L1_ffn_setup():
        import jax, jax.numpy as jnp
        import numpy as np
        CAPACITY = 0.125
        HEAD_DIM = 128
        N_HEADS = 16
        N_KV_HEADS = 8
        ROPE_THETA = 10000.0
        EPS = 1e-06

        def _rms_norm(x, w):
            return x * jax.lax.rsqrt(jnp.mean(x * x, axis=-1, keepdims=True) + EPS) * w

        def _rotate_half(t):
            h = t.shape[-1] // 2
            return jnp.concatenate([-t[..., h:], t[..., :h]], axis=-1)
        key = jax.random.key(seed)
        ks = jax.random.split(key, 12)
        B, T, D = (4, 1024, 512)
        I = 2048
        s = 0.02
        return {'hidden_states': jax.random.normal(ks[0], (B, T, D), jnp.float32), 'w_router': jax.random.normal(ks[1], (D,), jnp.float32) * s, 'wq': jax.random.normal(ks[2], (D, N_HEADS * HEAD_DIM), jnp.float32) * s, 'bq': jnp.zeros((N_HEADS * HEAD_DIM,), jnp.float32), 'wk': jax.random.normal(ks[3], (D, N_KV_HEADS * HEAD_DIM), jnp.float32) * s, 'bk': jnp.zeros((N_KV_HEADS * HEAD_DIM,), jnp.float32), 'wv': jax.random.normal(ks[4], (D, N_KV_HEADS * HEAD_DIM), jnp.float32) * s, 'bv': jnp.zeros((N_KV_HEADS * HEAD_DIM,), jnp.float32), 'wo': jax.random.normal(ks[5], (N_HEADS * HEAD_DIM, D), jnp.float32) * s, 'w_gate': jax.random.normal(ks[6], (D, I), jnp.float32) * s, 'w_up': jax.random.normal(ks[7], (D, I), jnp.float32) * s, 'w_down': jax.random.normal(ks[8], (I, D), jnp.float32) * s, 'ln1_w': jnp.ones((D,), jnp.float32), 'ln2_w': jnp.ones((D,), jnp.float32)}
    _L1_ffn_in = _L1_ffn_setup()
    _d = {'L0_attn_hidden_states': _L0_attn_in['hidden_states'], 'L0_attn_Wq': _L0_attn_in['Wq'], 'L0_attn_Wk': _L0_attn_in['Wk'], 'L0_attn_Wog': _L0_attn_in['Wog'], 'L0_attn_Wig': _L0_attn_in['Wig'], 'L0_attn_g_weight': _L0_attn_in['g_weight'], 'L0_ffn_input_ids': _L0_ffn_in['input_ids'], 'L0_ffn_gate_w': _L0_ffn_in['gate_w'], 'L0_ffn_gate_b': _L0_ffn_in['gate_b'], 'L0_ffn_W1': _L0_ffn_in['W1'], 'L0_ffn_W3': _L0_ffn_in['W3'], 'L0_ffn_W2': _L0_ffn_in['W2'], 'L0_ffn_Ws1': _L0_ffn_in['Ws1'], 'L0_ffn_Ws3': _L0_ffn_in['Ws3'], 'L0_ffn_Ws2': _L0_ffn_in['Ws2'], 'L1_attn_Wq': _L1_attn_in['Wq'], 'L1_attn_bq': _L1_attn_in['bq'], 'L1_attn_Wk': _L1_attn_in['Wk'], 'L1_attn_bk': _L1_attn_in['bk'], 'L1_attn_Wv': _L1_attn_in['Wv'], 'L1_attn_bv': _L1_attn_in['bv'], 'L1_attn_Wo': _L1_attn_in['Wo'], 'L1_attn_bo': _L1_attn_in['bo'], 'L1_ffn_w_router': _L1_ffn_in['w_router'], 'L1_ffn_wq': _L1_ffn_in['wq'], 'L1_ffn_bq': _L1_ffn_in['bq'], 'L1_ffn_wk': _L1_ffn_in['wk'], 'L1_ffn_bk': _L1_ffn_in['bk'], 'L1_ffn_wv': _L1_ffn_in['wv'], 'L1_ffn_bv': _L1_ffn_in['bv'], 'L1_ffn_wo': _L1_ffn_in['wo'], 'L1_ffn_w_gate': _L1_ffn_in['w_gate'], 'L1_ffn_w_up': _L1_ffn_in['w_up'], 'L1_ffn_w_down': _L1_ffn_in['w_down'], 'L1_ffn_ln1_w': _L1_ffn_in['ln1_w'], 'L1_ffn_ln2_w': _L1_ffn_in['ln2_w']}
    _x0 = _d['L0_attn_hidden_states']
    _d['L0_attn_hidden_states'] = jax.random.normal(jax.random.fold_in(jax.random.key(seed), 1), (1, 2048, 512), dtype=_x0.dtype)
    del _x0
    return _d

def reference(L0_attn_hidden_states, L0_attn_Wq, L0_attn_Wk, L0_attn_Wog, L0_attn_Wig, L0_attn_g_weight, L0_ffn_input_ids, L0_ffn_gate_w, L0_ffn_gate_b, L0_ffn_W1, L0_ffn_W3, L0_ffn_W2, L0_ffn_Ws1, L0_ffn_Ws3, L0_ffn_Ws2, L1_attn_Wq, L1_attn_bq, L1_attn_Wk, L1_attn_bk, L1_attn_Wv, L1_attn_bv, L1_attn_Wo, L1_attn_bo, L1_ffn_w_router, L1_ffn_wq, L1_ffn_bq, L1_ffn_wk, L1_ffn_bk, L1_ffn_wv, L1_ffn_bv, L1_ffn_wo, L1_ffn_w_gate, L1_ffn_w_up, L1_ffn_w_down, L1_ffn_ln1_w, L1_ffn_ln2_w):

    def _L0_attn_ref(hidden_states, Wq, Wk, Wog, Wig, g_weight):
        import jax, jax.numpy as jnp
        import numpy as np
        B, L, H, NH = (2, 512, 512, 16)
        K = H // NH
        EPS = 1e-05
        SCALE = K ** (-0.5)

        def _gla(q, k, v, g):

            def step(S, xs):
                q_t, k_t, v_t, g_t = xs
                S = jnp.exp(g_t)[:, :, None] * S + k_t[:, :, None] * v_t[:, None, :]
                o_t = jnp.einsum('bk,bkv->bv', q_t, S)
                return (S, o_t)
            S0 = jnp.zeros((q.shape[0], q.shape[2], v.shape[2]), dtype=q.dtype)
            xs = (jnp.swapaxes(q, 0, 1), jnp.swapaxes(k, 0, 1), jnp.swapaxes(v, 0, 1), jnp.swapaxes(g, 0, 1))
            _, o = jax.lax.scan(step, S0, xs)
            return jnp.swapaxes(o, 0, 1)
        x = hidden_states
        q = x @ Wq.T
        k_sig = jax.nn.sigmoid(x @ Wk.T)
        q = jax.nn.silu(q) * SCALE
        gf = jax.nn.log_sigmoid(-k_sig)
        o = _gla(q, k_sig, x, gf)
        go = o @ Wog.T + x @ Wig.T
        rms = o * jax.lax.rsqrt(jnp.mean(o * o, axis=-1, keepdims=True) + EPS) * g_weight
        return rms * go * jax.nn.sigmoid(go)

    def _L0_ffn_ref(x, input_ids, gate_w, gate_b, W1, W3, W2, Ws1, Ws3, Ws2):
        import jax, jax.numpy as jnp
        import numpy as np
        E = 16
        K = 2
        D = 512
        I = 352
        CAP = 256
        VOCAB = 32320
        shape = x.shape
        xt = x.reshape(-1, D)
        T = xt.shape[0]
        logits = xt.astype(jnp.float32) @ gate_w.astype(jnp.float32).T
        scores = jnp.sqrt(jax.nn.softplus(logits))
        _, idx = jax.lax.top_k(scores + gate_b, K)
        w = jnp.take_along_axis(scores, idx, axis=1)
        w = w / jnp.sum(w, axis=1, keepdims=True)
        e = idx.reshape(-1)
        onehot = jax.nn.one_hot(e, E, dtype=jnp.int32)
        pos = jnp.sum(onehot * (jnp.cumsum(onehot, axis=0) - 1), axis=1)
        valid = pos < CAP
        posc = jnp.where(valid, pos, 0)
        x_pairs = jnp.repeat(xt, K, axis=0)
        x_pairs = jnp.where(valid[:, None], x_pairs, 0.0)
        buf = jnp.zeros((E, CAP, D), xt.dtype).at[e, posc].add(x_pairs)
        g = jnp.einsum('ecd,eid->eci', buf, W1).astype(jnp.float32)
        u = jnp.einsum('ecd,eid->eci', buf, W3).astype(jnp.float32)
        h = (jax.nn.silu(g) * u).astype(xt.dtype)
        out = jnp.einsum('eci,edi->ecd', h, W2)
        y_pairs = out[e, posc] * (w.reshape(-1) * valid)[:, None]
        y = y_pairs.reshape(T, K, D).sum(axis=1)
        gs = jax.nn.silu((xt @ Ws1.T).astype(jnp.float32))
        us = (xt @ Ws3.T).astype(jnp.float32)
        shared = (gs * us).astype(xt.dtype) @ Ws2.T
        return (y + shared).astype(x.dtype).reshape(shape)

    def _L1_attn_ref(x, Wq, bq, Wk, bk, Wv, bv, Wo, bo):
        import jax, jax.numpy as jnp
        import numpy as np
        D_MODEL = 512
        N_HEADS = 16
        D_K = D_MODEL // N_HEADS
        EPS = 1e-06
        b, n, _ = x.shape
        h, d = (N_HEADS, D_K)

        def proj(W, bias):
            y = jnp.einsum('bnm,dm->bnd', x, W) + bias
            return y.reshape(b, n, h, d).transpose(0, 2, 1, 3)
        Q = jax.nn.relu(proj(Wq, bq))
        K = jax.nn.relu(proj(Wk, bk))
        V = proj(Wv, bv)
        pos = jnp.arange(n, dtype=x.dtype)
        decay = jnp.exp(-pos / n)[None, None, :, None]
        Q = Q * decay
        K = K * decay
        KV = jnp.einsum('bhnd,bhne->bhde', K, V)
        Ksum = K.sum(axis=2)
        Z = 1.0 / (jnp.einsum('bhnd,bhd->bhn', Q, Ksum)[..., None] + EPS)
        out = jnp.einsum('bhnd,bhde->bhne', Q, KV) * Z
        out = out.transpose(0, 2, 1, 3).reshape(b, n, h * d)
        return jnp.einsum('bnm,dm->bnd', out, Wo) + bo

    def _L1_ffn_ref(hidden_states, w_router, wq, bq, wk, bk, wv, bv, wo, w_gate, w_up, w_down, ln1_w, ln2_w):
        import jax, jax.numpy as jnp
        import numpy as np
        CAPACITY = 0.125
        HEAD_DIM = 128
        N_HEADS = 16
        N_KV_HEADS = 8
        ROPE_THETA = 10000.0
        EPS = 1e-06

        def _rms_norm(x, w):
            return x * jax.lax.rsqrt(jnp.mean(x * x, axis=-1, keepdims=True) + EPS) * w

        def _rotate_half(t):
            h = t.shape[-1] // 2
            return jnp.concatenate([-t[..., h:], t[..., :h]], axis=-1)
        B, T, D = hidden_states.shape
        k = max(1, int(T * CAPACITY))
        scores = jnp.einsum('btd,d->bt', hidden_states, w_router)
        _, idx = jax.lax.top_k(scores, k)
        idx = jnp.sort(idx, axis=-1)
        b = jnp.arange(B)[:, None]
        sel = hidden_states[b, idx]
        sel_scores = scores[b, idx]
        S = B * k
        x = sel.reshape(S, D)
        pos = idx.reshape(S)
        inv_freq = 1.0 / ROPE_THETA ** (jnp.arange(0, HEAD_DIM, 2, dtype=jnp.float32) / HEAD_DIM)
        ang = pos.astype(jnp.float32)[:, None] * inv_freq
        cos = jnp.concatenate([jnp.cos(ang), jnp.cos(ang)], axis=-1)[:, None, :]
        sin = jnp.concatenate([jnp.sin(ang), jnp.sin(ang)], axis=-1)[:, None, :]
        h = _rms_norm(x, ln1_w)
        q = (h @ wq + bq).reshape(S, N_HEADS, HEAD_DIM)
        kk = (h @ wk + bk).reshape(S, N_KV_HEADS, HEAD_DIM)
        v = (h @ wv + bv).reshape(S, N_KV_HEADS, HEAD_DIM)
        q = q * cos + _rotate_half(q) * sin
        kk = kk * cos + _rotate_half(kk) * sin
        rep = N_HEADS // N_KV_HEADS
        kk = jnp.repeat(kk, rep, axis=1)
        v = jnp.repeat(v, rep, axis=1)
        att = jnp.einsum('shd,thd->hst', q, kk) / np.sqrt(HEAD_DIM)
        causal = jnp.tril(jnp.ones((S, S), bool))
        att = jnp.where(causal[None], att, jnp.finfo(att.dtype).min)
        att = jax.nn.softmax(att, axis=-1)
        attn_out = jnp.einsum('hst,thd->shd', att, v).reshape(S, N_HEADS * HEAD_DIM) @ wo
        x1 = x + attn_out
        h2 = _rms_norm(x1, ln2_w)
        mlp = jax.nn.silu(h2 @ w_gate) * (h2 @ w_up) @ w_down
        processed = x1 + mlp
        gate = jax.nn.sigmoid(sel_scores).reshape(S, 1)
        gated = gate * processed + (1.0 - gate) * x
        output = hidden_states.at[b, idx].set(gated.reshape(B, k, D))
        return output
    x = L0_attn_hidden_states
    x = x + _L0_attn_ref(_layernorm(x, axis=-1), L0_attn_Wq, L0_attn_Wk, L0_attn_Wog, L0_attn_Wig, L0_attn_g_weight)
    x = x + _L0_ffn_ref(_layernorm(x, axis=-1), L0_ffn_input_ids, L0_ffn_gate_w, L0_ffn_gate_b, L0_ffn_W1, L0_ffn_W3, L0_ffn_W2, L0_ffn_Ws1, L0_ffn_Ws3, L0_ffn_Ws2)
    x = x + _L1_attn_ref(_layernorm(x, axis=-1), L1_attn_Wq, L1_attn_bq, L1_attn_Wk, L1_attn_bk, L1_attn_Wv, L1_attn_bv, L1_attn_Wo, L1_attn_bo)
    x = x + _L1_ffn_ref(_layernorm(x, axis=-1), L1_ffn_w_router, L1_ffn_wq, L1_ffn_bq, L1_ffn_wk, L1_ffn_bk, L1_ffn_wv, L1_ffn_bv, L1_ffn_wo, L1_ffn_w_gate, L1_ffn_w_up, L1_ffn_w_down, L1_ffn_ln1_w, L1_ffn_ln2_w)
    return x

_drawn_inputs = setup_inputs


def setup_inputs(seed=0):
    import zlib

    import numpy as np

    out = dict(_drawn_inputs(seed))
    spreads = {'L0_attn_g_weight': (1.0, 0.2),
     'L1_attn_bq': (0.0, 0.8),
     'L1_attn_bk': (0.0, 0.8),
     'L1_attn_bv': (0.0, 0.1),
     'L1_attn_bo': (0.0, 0.1),
     'L1_ffn_bq': (0.0, 0.8),
     'L1_ffn_bk': (0.0, 0.8),
     'L1_ffn_bv': (0.0, 0.8),
     'L1_ffn_ln1_w': (1.0, 0.6),
     'L1_ffn_ln2_w': (1.0, 0.6)}
    factors = {'L1_attn_Wq': 4.153,
     'L1_attn_Wk': 3.435,
     'L1_ffn_w_router': 3.397,
     'L1_ffn_wq': 8.0,
     'L1_ffn_wk': 8.0,
     'L1_ffn_wv': 5.857,
     'L1_ffn_wo': 4.148,
     'L1_ffn_w_gate': 4.996,
     'L1_ffn_w_up': 4.904,
     'L1_ffn_w_down': 4.891}
    for name, (base, spread) in spreads.items():
        noise = np.random.default_rng([zlib.crc32(name.encode()), seed]).standard_normal(out[name].shape)
        drawn = base * np.exp(spread * noise) if base else spread * noise
        out[name] = jnp.asarray(drawn.astype(out[name].dtype))
    for name, factor in factors.items():
        out[name] = (out[name] * factor).astype(out[name].dtype)
    return out
```

```python
from contextlib import ExitStack

import numpy as np

import concourse.bass as bass
from concourse import mybir

ALU = mybir.AluOpType
ACT = mybir.ActivationFunctionType
AX = mybir.AxisListType
F32 = mybir.dt.float32
U32 = mybir.dt.uint32

P = 128
T = 2048
D = 512
NT = T // P
KT = D // P
NB = 4
BT = NT // NB
BW = T // NB
DK = 32
SUB = 32
NE = 16
CAP = 256
FI = 352
FM = 3
SEL = 256
ST = SEL // P
HD = 128
NHQ, NHK = 16, 8
FF = 2048
FFT = FF // P
ROW = 2 * D + 2

_AT = {}
_n = 0
for _name, _w in (("ident", P), ("causal", P), ("before", P), ("ones", P), ("own", 16), ("cq", 16), ("ck", 16),
                  ("expert", NT * NE), ("rank", NT * NE), ("restart", NT * NE), ("token", NT), ("decay", NT),
                  ("neghalf", NT), ("half", NT * NE), ("addmask", 3 * P)):
    _AT[_name] = (_n, _n + _w)
    _n += _w
NCONST = _n


def constants():
    c = np.zeros((P, NCONST), np.float32)

    def put(name, a):
        lo, hi = _AT[name]
        c[:, lo:hi] = np.asarray(a, np.float32).reshape(P, hi - lo)

    r = np.arange(P)
    put("ident", np.eye(P))
    put("causal", r[:, None] <= r[None, :])
    put("before", r[:, None] < r[None, :])
    lower = np.where(r[None, :] <= r[:, None], 0.0, -3.0e38)
    put("addmask", np.concatenate([lower, np.zeros((P, P)), lower], axis=1))
    put("ones", np.ones((P, P)))
    g = r // SUB
    own = np.zeros((P, BT, 4))
    cq = np.zeros((P, BT, 4))
    ck = np.zeros((P, BT, 4))
    for b in range(4):
        own[g == b, :, b] = 1
    cq[g == 0, :, 2] = 1
    cq[g == 1, :, 1] = 1
    cq[g == 2, :, 3] = 1
    cq[g == 3, :, 0] = 1
    put("own", own)
    put("cq", cq)
    put("ck", ck)
    put("expert", np.broadcast_to(np.arange(NE), (P, NT, NE)))
    put("rank", np.broadcast_to(NE - np.arange(NE), (P, NT, NE)))
    put("restart", np.broadcast_to(np.arange(NT) > 0, (P, NE, NT)))
    token = np.arange(NT)[None, :] * P + r[:, None]
    put("token", token)
    put("decay", np.exp(-token.astype(np.float32) / np.float32(T)))
    put("neghalf", np.full((P, NT), -0.5))
    put("half", np.full((P, NT * NE), 0.5))
    return c


def turns():
    freq = (1.0 / np.float32(10000.0) ** (np.arange(0, HD, 2, dtype=np.float32) / np.float32(HD))).astype(np.float32)
    ang = np.arange(T, dtype=np.float32)[:, None] * freq
    co, si = np.cos(ang).astype(np.float32), np.sin(ang).astype(np.float32)
    return np.concatenate([co, co, si, -si], axis=1)


class Ring:

    def __init__(self, sem, name, banks, tasks):
        self.banks = banks
        self.at = {t: i for i, t in enumerate(tasks)}
        assert len(self.at) == len(tasks)
        self.filled = sem(f"{name}_filled")
        self.drained = [sem(f"{name}_drained{b}") for b in banks]

    def bank(self, task):
        return self.banks[self.at[task] % len(self.banks)]

    def free(self, pe, task):
        k, n = divmod(self.at[task], len(self.banks))
        if k:
            pe.wait_ge(self.drained[n], k)

    def full(self, eng, task):
        eng.wait_ge(self.filled, self.at[task] + 1)

    def empty(self, task):
        return self.drained[self.at[task] % len(self.banks)]

    def all_drained(self, pe):
        total = len(self.at)
        for n in range(len(self.banks)):
            uses = (total - n + len(self.banks) - 1) // len(self.banks)
            if uses:
                pe.wait_ge(self.drained[n], uses)


class Chain:

    def __init__(self, sem):
        self.sem, self.n = sem, 0

    def __call__(self, eng, ins):
        ins.then_inc(self.sem, 1)
        self.n += 1
        eng.wait_ge(self.sem, self.n)


class Build:
    pass


def setup(nc, ctx, io):
    k = Build()
    k.nc, k.ctx, k.io = nc, ctx, io
    k.phase_sems = []

    def sem(name):
        k.phase_sems.append(nc.alloc_semaphore(name))
        return k.phase_sems[-1]

    k.sem = sem
    k.rows = ctx.enter_context(nc.sbuf_tensor("rows", [P, NT, ROW], F32))
    k.xnt = ctx.enter_context(nc.sbuf_tensor("xnt", [P, KT * T], F32))
    k.con = ctx.enter_context(nc.sbuf_tensor("con", [P, NCONST], F32))
    k.small = ctx.enter_context(nc.sbuf_tensor("small", [P, 192], F32))
    k.arena_size = 26368
    k.arena = ctx.enter_context(nc.sbuf_tensor("arena", [P, k.arena_size], F32))
    k.ps = ctx.enter_context(nc.psum_tensor("ps", [P, 8, 512], F32))
    k.chain = {e: Chain(k.sem(f"{e}_done")) for e in ("dve", "act", "pool")}
    k.s_con = k.sem("constants_in")
    return k


def c(k, name, rows=slice(0, P)):
    lo, hi = _AT[name]
    return k.con[rows, lo:hi]


def recycle(k):
    k.nc.all_engine_barrier()
    k.nc.clear_and_free_semaphores(k.phase_sems)
    k.phase_sems.clear()
    k.nc.all_engine_barrier()


class Place:

    def __init__(self, tensor, at, end):
        self.tensor, self.at, self.end = tensor, at, end

    def __call__(self, *dims):
        n = int(np.prod(dims))
        a = self.tensor[:, self.at:self.at + n]
        self.at += n
        assert self.at <= self.end, (self.at, self.end)
        if len(dims) == 2:
            a = a.rearrange("p (a b) -> p a b", b=dims[1])
        if len(dims) == 3:
            a = a.rearrange("p (a b c) -> p a b c", b=dims[1], c=dims[2])
        return a


def wide(ap, n):
    return ap.unsqueeze(2).to_broadcast((ap.shape[0], ap.shape[1], n))


def sems(k, prefix, names):
    return {n: k.sem(f"{prefix}_{n}") for n in names.split()}


def gated_linear_attention(k):
    nc, io, ps, rows = k.nc, k.io, k.ps, k.rows
    put = Place(k.arena, 4352, k.arena_size)
    w_qk, w_og, w_ig, gw = put(KT, 2 * P), put(KT, D), put(KT, D), put(D)
    xn = [put(BT, D) for _ in range(2)]
    put_x = Place(k.xnt, 0, KT * T)
    xnt = [put_x(KT, BW) for _ in range(2)]
    ksig, decay, qsig, starts, prod, inv, qs = (put(BW) for _ in range(7))
    qd, kd, qx, kx = (put(BW) for _ in range(4))
    att, kst, state = put(BT, P), put(BT, DK), put(2, D)
    o, ot, sg = put(2, D), put(2, KT, P), put(2, D)
    og, gated, junk = put(D), put(D), put(D)
    tiny = Place(k.small, 0, 192)
    stats, mv, rstd, ve = tiny(BT, 6), tiny(BT, 2), tiny(BT), tiny(BT)
    ss, rr, ms = tiny(BT), tiny(BT), tiny(BT)
    stats2, mv2, rstd2, ve2 = tiny(BT, 6), tiny(BT, 2), tiny(BT), tiny(BT)
    cq, ck, own = c(k, "cq"), c(k, "ck"), c(k, "own")

    tasks = []
    for n in range(NB):
        tasks += [("xT", n, i) for i in range(KT)] + [("q", n), ("k", n), ("AT", n), ("KST", n)]
        tasks += [("U", n, 0), ("o", n, 0), ("U", n, 1), ("o", n, 1), ("oT", n, 0), ("U", n, 2), ("o", n, 2),
                  ("oT", n, 1), ("U", n, 3), ("o", n, 3), ("oT", n, 2), ("oT", n, 3)]
    ring = Ring(k.sem, "gla", [4, 5, 6, 7], tasks)
    x_in = [k.sem(f"x_in{n}") for n in range(NB)]
    s = sems(k, "gla", """w_qk_in w_og_in w_ig_in gw_in ln_stats ln_rstd ln_out xnt_out decay_out qsig_out
             features att_out kst_out state_out o_out square_out rr_out ot_out go_full go_empty sg_out sg_used
             og_out ln2_stats ln2_rstd zero_out zeros_in""")
    dve_done, act_done, pool_done = k.chain["dve"], k.chain["act"], k.chain["pool"]

    def bank(task):
        return ps[:, ring.bank(task), :]

    with nc.Block() as block:

        @block.sync
        def _(sp):
            sp.dma_start(k.con[:, :], io["consts"]).then_inc(k.s_con, 16)
            for n in range(NB):
                x = io["x"].rearrange("(t p) d -> p t d", p=P)[:, n * BT:(n + 1) * BT, :]
                sp.dma_start(rows[:, n * BT:(n + 1) * BT, 0:D], x).then_inc(x_in[n], 16)
                if n == 0:
                    sp.dma_start(w_qk, io["w_qk"]).then_inc(s["w_qk_in"], 16)
                    sp.dma_start(w_ig, io["w_ig"]).then_inc(s["w_ig_in"], 16)
                    sp.dma_start(w_og, io["w_og"]).then_inc(s["w_og_in"], 16)
                    sp.dma_start(gw, io["g_weight"].partition_broadcast(P)).then_inc(s["gw_in"], 16)
            sp.dma_start(k.w_shared, io["w_shared"]).then_inc(k.s_shared, 16)
            sp.wait_ge(s["zero_out"], 1)
            zeros = og.unsqueeze(1).to_broadcast((P, NE * CAP // P, D))
            sp.dma_start(k.expert_in.rearrange("(p r) d -> p r d", p=P), zeros).then_inc(s["zeros_in"], 16)

        @block.gpsimd
        def _(pool):
            pool.wait_ge(k.s_con, 16)

            def rsqrt(out, tmp, src, scale, done, eps=1e-5):
                pool_done(pool, pool.tensor_scalar(tmp, src, scale, eps, ALU.mult, ALU.add))
                n = out.shape[1]
                pool.tensor_tensor(out, tmp, c(k, "neghalf")[:, 0:n], ALU.pow).then_inc(done, 1)

            pool.wait_ge(s["ln_stats"], 1)
            rsqrt(rstd, ve, mv[:, :, 1], 1.0, s["ln_rstd"])
            for n in range(NB):
                if n + 1 < NB:
                    pool.wait_ge(s["ln_stats"], n + 2)
                    rsqrt(rstd, ve, mv[:, :, 1], 1.0, s["ln_rstd"])
                for i in range(BT):
                    pool.wait_ge(s["square_out"], n * BT + i + 1)
                    rsqrt(rr[:, i:i + 1], ms[:, i:i + 1], ss[:, i:i + 1], 1.0 / D, s["rr_out"])
                pool.wait_ge(s["ln2_stats"], n + 1)
                rsqrt(rstd2, ve2, mv2[:, :, 1], 1.0, s["ln2_rstd"])

        @block.scalar
        def _(act):
            def o_out(n, i):
                t = n * BT + i
                if t >= 2:
                    act.wait_ge(s["og_out"], t - 1)
                ring.full(act, ("o", n, i))
                act.activation(o[:, i % 2, :], bank(("o", n, i)), ACT.Copy).then_inc(s["o_out"], 1)
                act.activation(junk, bank(("o", n, i)), ACT.Square,
                               accum_out=ss[:, i:i + 1]).then_inc(s["square_out"], 1)
                act.wait_ge(s["square_out"], t + 1)
                act.sem_inc(ring.empty(("o", n, i)), 1)

            def ot_out(n, i):
                ring.full(act, ("oT", n, i))
                act.activation(ot[:, i % 2, :, :], bank(("oT", n, i)).rearrange("p (a b) -> p a b", b=P),
                               ACT.Copy).then_inc(ring.empty(("oT", n, i)), 1)

            def sg_out(n, i):
                t = n * BT + i
                act.wait_ge(s["go_full"], t + 1)
                if t >= 2:
                    act.wait_ge(s["sg_used"], t - 1)
                act.activation(sg[:, i % 2, :], ps[:, i, :], ACT.Sigmoid).then_inc(s["sg_out"], 1)

            for n in range(NB):
                for i in range(KT):
                    ring.full(act, ("xT", n, i))
                    act.activation(xnt[n % 2][:, i, :], bank(("xT", n, i)),
                                   ACT.Copy).then_inc(ring.empty(("xT", n, i)), 1)
                ring.full(act, ("k", n))
                if n:
                    act.wait_ge(s["features"], n)
                act_done(act, act.activation(ksig, bank(("k", n)), ACT.Sigmoid))
                act.activation(decay, ksig, ACT.Sigmoid, scale=-1.0).then_inc(s["decay_out"], 1)
                act.activation(qsig, bank(("q", n)), ACT.Sigmoid).then_inc(s["qsig_out"], 1)
                o_out(n, 0)
                o_out(n, 1)
                ot_out(n, 0)
                o_out(n, 2)
                ot_out(n, 1)
                sg_out(n, 0)
                o_out(n, 3)
                ot_out(n, 2)
                sg_out(n, 1)
                ot_out(n, 3)
                sg_out(n, 2)
                sg_out(n, 3)

        @block.tensor
        def _(pe):
            pe.wait_ge(k.s_con, 16)
            ident = c(k, "ident")

            def project_out(n, i):
                t = n * BT + i
                pe.wait_ge(ring.empty(("oT", n, i)), ring.at[("oT", n, i)] // 4 + 1)
                for j in range(KT):
                    mm = pe.matmul(ps[:, i, :], ot[:, i % 2, j, :], w_og[:, j, :], start=False, stop=(j == KT - 1))
                mm.then_inc(s["go_full"], 1)

            def project_in(n, i):
                t = n * BT + i
                if n:
                    pe.wait_ge(s["go_empty"], t - BT + 1)
                for j in range(KT):
                    pe.matmul(ps[:, i, :], xnt[n % 2][:, j, i * P:(i + 1) * P], w_ig[:, j, :],
                              start=(j == 0), stop=False)

            def update(n, i):
                ring.free(pe, ("U", n, i))
                pe.matmul(bank(("U", n, i))[96:128, :], kst[:, i, :], xn[n % 2][:, i, :],
                          start=True, stop=True).then_inc(ring.filled, 1)

            def output(n, i):
                t = n * BT + i
                ring.free(pe, ("o", n, i))
                pe.matmul(bank(("o", n, i)), att[:, i, :], xn[n % 2][:, i, :], start=True, stop=False)
                pe.wait_ge(s["state_out"], t + 1)
                pe.matmul(bank(("o", n, i)), qx[96:128, i * P:(i + 1) * P], state[96:128, t % 2, :],
                          start=False, stop=True).then_inc(ring.filled, 1)

            def turn(n, i):
                t = n * BT + i
                pe.wait_ge(s["o_out"], t + 1)
                ring.free(pe, ("oT", n, i))
                for j in range(KT):
                    mm = pe.transpose(bank(("oT", n, i))[:, j * P:(j + 1) * P], o[:, i % 2, j * P:(j + 1) * P], ident)
                mm.then_inc(ring.filled, 1)

            for n in range(NB):
                pe.wait_ge(s["ln_out"], n + 1)
                for j in range(KT):
                    ring.free(pe, ("xT", n, j))
                    for i in range(BT):
                        mm = pe.transpose(bank(("xT", n, j))[:, i * P:(i + 1) * P],
                                          xn[n % 2][:, i, j * P:(j + 1) * P], ident)
                    mm.then_inc(ring.filled, 1)
                if n == 0:
                    pe.wait_ge(s["w_qk_in"], 16)
                for h, what in enumerate("qk"):
                    ring.free(pe, (what, n))
                    for j in range(KT):
                        if h == 0:
                            pe.wait_ge(ring.empty(("xT", n, j)), ring.at[("xT", n, j)] // 4 + 1)
                        mm = pe.matmul(bank((what, n)), w_qk[:, j, h * P:(h + 1) * P], xnt[n % 2][:, j, :],
                                       start=(j == 0), stop=(j == KT - 1))
                    mm.then_inc(ring.filled, 1)
                if n == 0:
                    pe.wait_ge(s["w_ig_in"], 16)
                for i in range(3):
                    project_in(n, i)
                pe.wait_ge(s["features"], n + 1)
                ring.free(pe, ("AT", n))
                for i in range(BT):
                    r = slice(i * P, (i + 1) * P)
                    pe.matmul(bank(("AT", n))[:, r], kd[:, r], qd[:, r], start=True, stop=False)
                    mm = pe.matmul(bank(("AT", n))[:, r], kx[0:96, r], qx[0:96, r], start=False, stop=True)
                mm.then_inc(ring.filled, 1)
                ring.free(pe, ("KST", n))
                for i in range(BT):
                    mm = pe.transpose(bank(("KST", n))[:, i * DK:(i + 1) * DK], kx[96:128, i * P:(i + 1) * P],
                                      ident[96:128, 96:128])
                mm.then_inc(ring.filled, 1)
                project_in(n, 3)
                pe.wait_ge(s["kst_out"], n + 1)
                pe.wait_ge(s["att_out"], n + 1)
                if n == 0:
                    pe.wait_ge(s["w_og_in"], 16)
                update(n, 0)
                output(n, 0)
                update(n, 1)
                output(n, 1)
                turn(n, 0)
                update(n, 2)
                output(n, 2)
                turn(n, 1)
                project_out(n, 0)
                update(n, 3)
                output(n, 3)
                turn(n, 2)
                project_out(n, 1)
                turn(n, 3)
                project_out(n, 2)
                project_out(n, 3)

        @block.vector
        def _(dve):
            def done(ins):
                dve_done(dve, ins)

            def ln_in(n):
                dve.wait_ge(x_in[n], 16)
                for i in range(BT):
                    done(dve.bn_stats(stats[:, i, :], rows[:, n * BT + i, 0:D]))
                for i in range(BT):
                    ins = dve.bn_aggr(mv[:, i, :], stats[:, i, :])
                ins.then_inc(s["ln_stats"], 1)
                dve.wait_ge(s["ln_rstd"], n + 1)
                for i in range(BT):
                    ins = dve.tensor_scalar(xn[n % 2][:, i, :], rows[:, n * BT + i, 0:D], mv[:, i, 0:1],
                                            rstd[:, i:i + 1], ALU.subtract, ALU.mult)
                ins.then_inc(s["ln_out"], 1)

            def features(n):
                dve.wait_ge(s["decay_out"], n + 1)
                first = decay.rearrange("p (c t) -> p c t", t=SUB)[:, :, 0:1]
                done(dve.tensor_copy(starts.rearrange("p (c t) -> p c t", t=SUB)[:, :, 0:1], first))
                done(dve.memset(first, 0.0))
                done(dve.tensor_tensor_scan(prod, decay, starts, 0.0, ALU.mult, ALU.add))
                dve.reciprocal(inv, prod)
                ring.full(dve, ("q", n))
                dve.wait_ge(s["qsig_out"], n + 1)
                ins = dve.scalar_tensor_tensor(qs, bank(("q", n)), float(DK) ** -0.5, qsig, ALU.mult, ALU.mult)
                ins.then_inc(ring.empty(("q", n)), 1)
                dve.sem_inc(ring.empty(("k", n)), 1)
                end = prod.rearrange("p (c b t) -> p c b t", b=4, t=SUB)[:, :, :, SUB - 1]
                q3, k3 = (a.rearrange("p (c b) -> p c b", b=4) for a in (cq, ck))

                def whole(g, b):
                    return end[g * SUB:(g + 1) * SUB, :, b]

                def q_(g, b):
                    return q3[g * SUB:(g + 1) * SUB, :, b]

                def k_(g, b):
                    return k3[g * SUB:(g + 1) * SUB, :, b]

                dve.tensor_copy(q_(0, 3), whole(0, 2))
                dve.tensor_copy(q_(3, 1), whole(3, 0))
                dve.tensor_copy(k_(0, 1), whole(0, 1))
                dve.tensor_tensor(k_(0, 0), whole(0, 0), whole(0, 1), ALU.mult)
                dve.tensor_copy(k_(1, 0), whole(1, 0))
                dve.tensor_copy(k_(2, 2), whole(2, 2))
                done(dve.tensor_copy(k_(3, 3), whole(3, 3)))
                dve.tensor_tensor(q_(3, 2), q_(3, 1), whole(3, 1), ALU.mult)
                done(dve.tensor_tensor(k_(3, 2), k_(3, 3), whole(3, 2), ALU.mult))
                dve.tensor_tensor(q_(3, 3), q_(3, 2), whole(3, 2), ALU.mult)
                done(dve.tensor_tensor(k_(3, 1), k_(3, 2), whole(3, 1), ALU.mult))
                done(dve.tensor_tensor(k_(3, 0), k_(3, 1), whole(3, 0), ALU.mult))
                dve.tensor_tensor(qs, qs, prod, ALU.mult)
                done(dve.tensor_tensor(ksig, ksig, inv, ALU.mult))

                def scaled(out, a, by):
                    return dve.tensor_tensor(out.rearrange("p (c t) -> p c t", t=SUB),
                                             a.rearrange("p (c t) -> p c t", t=SUB), wide(by, SUB), ALU.mult)

                scaled(qd, qs, own)
                scaled(kd, ksig, own)
                scaled(qx, qs, cq)
                scaled(kx, ksig, ck).then_inc(s["features"], 1)

            def post(n, i):
                t = n * BT + i
                dve.wait_ge(s["rr_out"], t + 1)
                dve.wait_ge(s["o_out"], t + 1)
                if t == 0:
                    dve.wait_ge(s["zeros_in"], 16)
                dve.scalar_tensor_tensor(og, o[:, i % 2, :], rr[:, i:i + 1], gw, ALU.mult,
                                         ALU.mult).then_inc(s["og_out"], 1)
                dve.wait_ge(s["sg_out"], t + 1)
                dve.tensor_tensor(gated, ps[:, i, :], sg[:, i % 2, :], ALU.mult).then_inc(s["go_empty"], 1)
                dve.wait_ge(s["go_empty"], t + 1)
                dve.sem_inc(s["sg_used"], 1)
                done(dve.tensor_tensor(og, og, gated, ALU.mult))
                x = rows[:, t, 0:D]
                done(dve.tensor_tensor(x, x, og, ALU.add))
                done(dve.bn_stats(stats2[:, i, :], x))
                ins = dve.bn_aggr(mv2[:, i, :], stats2[:, i, :])
                if i == BT - 1:
                    ins.then_inc(s["ln2_stats"], 1)

            dve.wait_ge(k.s_con, 16)
            dve.memset(og, 0.0).then_inc(s["zero_out"], 1)
            dve.memset(starts, 0.0)
            dve.memset(state[96:128, 0, :], 0.0).then_inc(s["state_out"], 1)
            ln_in(0)
            for n in range(NB):
                features(n)
                if n + 1 < NB:
                    ln_in(n + 1)
                ring.full(dve, ("AT", n))
                dve.tensor_tensor(att, bank(("AT", n)).rearrange("p (a b) -> p a b", b=P),
                                  c(k, "causal").unsqueeze(1).to_broadcast((P, BT, P)),
                                  ALU.mult).then_inc(s["att_out"], 1)
                dve.wait_ge(s["att_out"], n + 1)
                dve.sem_inc(ring.empty(("AT", n)), 1)
                ring.full(dve, ("KST", n))
                dve.tensor_copy(kst, bank(("KST", n))[:, 0:BT * DK].rearrange("p (a b) -> p a b", b=DK)
                                ).then_inc(s["kst_out"], 1)
                dve.wait_ge(s["kst_out"], n + 1)
                dve.sem_inc(ring.empty(("KST", n)), 1)
                if n == 0:
                    dve.wait_ge(s["gw_in"], 16)

                def step(i):
                    t = n * BT + i
                    ring.full(dve, ("U", n, i))
                    dve.scalar_tensor_tensor(state[96:128, (t + 1) % 2, :], state[96:128, t % 2, :],
                                             ck[96:128, 4 * i:4 * i + 1], bank(("U", n, i))[96:128, :],
                                             ALU.mult, ALU.add).then_inc(s["state_out"], 1)
                    dve.wait_ge(s["state_out"], t + 2)
                    dve.sem_inc(ring.empty(("U", n, i)), 1)

                step(0)
                step(1)
                step(2)
                post(n, 0)
                step(3)
                post(n, 1)
                post(n, 2)
                post(n, 3)
                dve.wait_ge(s["ln2_rstd"], n + 1)
                for i in range(BT):
                    t = n * BT + i
                    dve.tensor_scalar(rows[:, t, D:2 * D], rows[:, t, 0:D], mv2[:, i, 0:1], rstd2[:, i:i + 1],
                                      ALU.subtract, ALU.mult)


W_UP = KT * 2 * FI
W_ALL = W_UP + FM * D
FROWS = [P, P, FI - 2 * P]


def weights(a):
    return (a[:, 0:W_UP].rearrange("p (a b) -> p a b", b=2 * FI),
            a[:, W_UP:W_ALL].rearrange("p (a b) -> p a b", b=D))


def expert_memory(k):
    put = Place(k.arena, W_ALL, k.arena_size)
    k.w_expert = [put(W_ALL) for _ in range(2)]
    k.h_shared = [put(FM, BW) for _ in range(2)]
    k.silu_shared = [put(BW) for _ in range(2)]
    k.routing_at = put.at
    k.xe = [put(ST, D) for _ in range(2)]
    k.xet, k.he, k.silu_e = put(KT, CAP), put(FM, CAP), put(FM, CAP)
    k.ye = [put(ST, D) for _ in range(2)]
    tiny = Place(k.small, 0, 192)
    k.weight = [tiny(NT) for _ in range(2)]
    k.take, k.give = ([tiny(NT).bitcast(U32) for _ in range(2)] for _ in range(2))
    k.tiny_at = tiny.at


def route_and_shared(k):
    nc, io, ps, rows = k.nc, k.io, k.ps, k.rows
    xnt = k.xnt.rearrange("p (a b) -> p a b", b=T) if False else k.xnt[:, :].rearrange("p (a b) -> p a b", b=T)
    up, down = weights(k.w_shared)
    put = Place(k.arena, k.routing_at, k.arena_size)
    logit_rows, gate_w, gate_b = put(T), put(KT, NE), put(NE)
    E_ = NT * NE
    x, ab, ex, u, d, z, ln, score, biased, eq, first, second, m, pos, tmp, tmp2 = (put(E_) for _ in range(16))
    tiny = Place(k.small, k.tiny_at, 192)
    best, which, total = tiny(NT), tiny(NT), tiny(NT)
    at, es, ok = tiny(NT), tiny(NT), tiny(NT)

    def te(a):
        return a.rearrange("p (t e) -> p t e", e=NE)

    turn_tasks = []
    for n in range(NB):
        turn_tasks += [("x2T", n, j) for j in range(KT)] + [("logits", n)]
    turn_tasks += [("logitsT",)]
    for n in range(NB):
        for m_ in range(FM):
            turn_tasks += [("g", n, m_), ("u", n, m_)]
    inner = Ring(k.sem, "inner", [4, 5, 6, 7], turn_tasks)
    outer_tasks = []
    for n in range(NB):
        outer_tasks += [("down", n, i) for i in range(BT)] + ([("before",)] if n == 0 else [])
    outer = Ring(k.sem, "outer", [0, 1, 2, 3], outer_tasks)
    s = sems(k, "route", """gate_in rows_out silu_out h_out abs_in exp_out ln_in ln_out power_in
             power_out chosen down_used logits_out""")
    dve_done, act_done = k.chain["dve"], k.chain["act"]

    with nc.Block() as block:

        @block.sync
        def _(sp):
            sp.dma_start(gate_w, io["gate_w"]).then_inc(s["gate_in"], 16)
            sp.dma_start(gate_b, io["gate_b"].partition_broadcast(P)).then_inc(s["gate_in"], 16)
            for e in range(2):
                sp.dma_start(k.w_expert[e], io["w_expert"][e]).then_inc(k.w_in[e], 16)
            sp.wait_ge(k.given, 16 * 2 * NT)
            for e in range(2):
                sp.dma_start(k.xe[e], k.expert_in[e * CAP:(e + 1) * CAP, :].rearrange("(a p) d -> p a d", p=P)
                             ).then_inc(k.xe_in[e], 16)

        @block.tensor
        def _(pe):
            ident = c(k, "ident")
            pe.wait_ge(s["gate_in"], 32)

            def turn(n):
                for j in range(KT):
                    inner.free(pe, ("x2T", n, j))
                    b = ps[:, inner.bank(("x2T", n, j)), :]
                    for i in range(BT):
                        mm = pe.transpose(b[:, i * P:(i + 1) * P], rows[:, n * BT + i, D + j * P:D + (j + 1) * P],
                                          ident)
                    mm.then_inc(inner.filled, 1)

            def logits(n):
                inner.free(pe, ("logits", n))
                for j in range(KT):
                    pe.wait_ge(inner.empty(("x2T", n, j)), inner.at[("x2T", n, j)] // 4 + 1)
                    mm = pe.matmul(ps[0:NE, inner.bank(("logits", n)), :], gate_w[:, j, :],
                                   xnt[:, j, n * BW:(n + 1) * BW], start=(j == 0), stop=(j == KT - 1))
                mm.then_inc(inner.filled, 1)

            for n in range(NB):
                turn(n)
                logits(n)
            pe.wait_ge(s["logits_out"], NB)
            inner.free(pe, ("logitsT",))
            for t in range(NT):
                mm = pe.transpose(ps[:, inner.bank(("logitsT",)), t * NE:(t + 1) * NE],
                                  logit_rows[0:NE, t * P:(t + 1) * P], ident[0:NE, 0:NE])
            mm.then_inc(inner.filled, 1)
            pe.wait_ge(k.s_shared, 16)
            for n in range(NB):
                for m_ in range(FM):
                    for h, what in enumerate("gu"):
                        inner.free(pe, (what, n, m_))
                        for j in range(KT):
                            lo = h * FI + m_ * P
                            mm = pe.matmul(ps[0:FROWS[m_], inner.bank((what, n, m_)), :],
                                           up[:, j, lo:lo + FROWS[m_]], xnt[:, j, n * BW:(n + 1) * BW],
                                           start=(j == 0), stop=(j == KT - 1))
                        mm.then_inc(inner.filled, 1)
                for i in range(BT):
                    outer.free(pe, ("down", n, i))
                    for m_ in range(FM):
                        pe.wait_ge(s["h_out"], n * FM + m_ + 1)
                        mm = pe.matmul(ps[:, outer.bank(("down", n, i)), :],
                                       k.h_shared[n % 2][0:FROWS[m_], m_, i * P:(i + 1) * P],
                                       down[0:FROWS[m_], m_, :], start=(m_ == 0), stop=(m_ == FM - 1))
                    mm.then_inc(outer.filled, 1)
                if n == 0:
                    pe.wait_ge(s["chosen"], 1)
                    outer.free(pe, ("before",))
                    b = ps[:, outer.bank(("before",)), :]
                    pe.matmul(b[:, 0:E_], c(k, "before"), m, start=True, stop=True)
                    pe.matmul(b[:, E_:2 * E_], c(k, "ones"), m, start=True, stop=True).then_inc(outer.filled, 1)

        @block.scalar
        def _(act):
            for n in range(NB):
                for j in range(KT):
                    inner.full(act, ("x2T", n, j))
                    act.activation(xnt[:, j, n * BW:(n + 1) * BW], ps[:, inner.bank(("x2T", n, j)), :],
                                   ACT.Copy).then_inc(inner.empty(("x2T", n, j)), 1)
                inner.full(act, ("logits", n))
                act.activation(logit_rows[0:NE, n * BW:(n + 1) * BW], ps[0:NE, inner.bank(("logits", n)), :],
                               ACT.Copy).then_inc(s["logits_out"], 1)
                act.wait_ge(s["logits_out"], n + 1)
                act.sem_inc(inner.empty(("logits", n)), 1)
            act.wait_ge(s["abs_in"], 1)
            act_done(act, act.activation(ab, x, ACT.Abs))
            act.activation(ex, ab, ACT.Exp, scale=-1.0).then_inc(s["exp_out"], 1)
            act.wait_ge(s["ln_in"], 1)
            act.activation(ln, u, ACT.Ln).then_inc(s["ln_out"], 1)
            for n in range(NB):
                for m_ in range(FM):
                    q = n * FM + m_
                    if q >= 2:
                        act.wait_ge(s["h_out"], q - 1)
                    inner.full(act, ("g", n, m_))
                    r = FROWS[m_]
                    act.activation(k.silu_shared[q % 2][0:r, :], ps[0:r, inner.bank(("g", n, m_)), :],
                                   ACT.Silu).then_inc(s["silu_out"], 1)
                    act.wait_ge(s["silu_out"], q + 1)
                    act.sem_inc(inner.empty(("g", n, m_)), 1)

        @block.gpsimd
        def _(pool):
            pool.wait_ge(s["power_in"], 1)
            pool.tensor_tensor(score, tmp, c(k, "half"), ALU.pow).then_inc(s["power_out"], 1)
            pool.wait_ge(s["rows_out"], 1)
            for t in range(NT):
                for slot in range(2):
                    pool.indirect_dma_start(
                        out=k.expert_in[:, :],
                        out_offset=bass.IndirectOffsetOnAxis(ap=k.give[slot][:, t:t + 1], axis=0),
                        in_=rows[:, t, D:2 * D], in_offset=None, bounds_check=NE * CAP - 1,
                        oob_is_err=False).then_inc(k.given, 16)

        @block.vector
        def _(dve):
            def done(ins):
                dve_done(dve, ins)

            def per_token(a):
                return wide(a, NE)

            def shared(n):
                for m_ in range(FM):
                    q = n * FM + m_
                    r = FROWS[m_]
                    inner.full(dve, ("u", n, m_))
                    dve.wait_ge(s["silu_out"], q + 1)
                    dve.tensor_tensor(k.h_shared[n % 2][0:r, m_, :], ps[0:r, inner.bank(("u", n, m_)), :],
                                      k.silu_shared[q % 2][0:r, :], ALU.mult).then_inc(s["h_out"], 1)
                    dve.wait_ge(s["h_out"], q + 1)
                    dve.sem_inc(inner.empty(("u", n, m_)), 1)
                for i in range(BT):
                    xr = rows[:, n * BT + i, 0:D]
                    outer.full(dve, ("down", n, i))
                    dve.tensor_tensor(xr, ps[:, outer.bank(("down", n, i)), :], xr,
                                      ALU.add).then_inc(outer.empty(("down", n, i)), 1)

            inner.full(dve, ("logitsT",))
            dve.tensor_copy(x, ps[:, inner.bank(("logitsT",)), 0:E_]).then_inc(s["abs_in"], 1)
            dve.wait_ge(s["abs_in"], 1)
            dve.sem_inc(inner.empty(("logitsT",)), 1)
            dve.wait_ge(s["exp_out"], 1)
            dve.tensor_scalar(u, ex, 1.0, None, ALU.add).then_inc(s["ln_in"], 1)
            dve.wait_ge(s["ln_in"], 1)
            done(dve.tensor_scalar(d, u, -1.0, None, ALU.add))
            done(dve.tensor_scalar(z, d, 0.0, None, ALU.is_equal))
            done(dve.tensor_tensor(d, d, z, ALU.add))
            done(dve.reciprocal(tmp2, d))
            done(dve.tensor_tensor(tmp2, tmp2, ex, ALU.mult))
            done(dve.tensor_tensor(z, z, ex, ALU.mult))
            dve.wait_ge(s["ln_out"], 1)
            done(dve.tensor_tensor(tmp2, tmp2, ln, ALU.mult))
            done(dve.tensor_tensor(tmp2, tmp2, z, ALU.add))
            dve.scalar_tensor_tensor(tmp, x, 0.0, tmp2, ALU.max, ALU.add).then_inc(s["power_in"], 1)
            dve.wait_ge(s["gate_in"], 32)
            dve.wait_ge(s["power_out"], 1)
            done(dve.tensor_tensor(te(biased), te(score), gate_b.unsqueeze(1).to_broadcast((P, NT, NE)), ALU.add))
            for slot, onehot in enumerate((first, second)):
                done(dve.tensor_reduce(best, te(biased), AX.X, ALU.max))
                done(dve.tensor_tensor(te(eq), te(biased), per_token(best), ALU.is_equal))
                done(dve.tensor_tensor(eq, eq, c(k, "rank"), ALU.mult))
                done(dve.tensor_reduce(which, te(eq), AX.X, ALU.max))
                done(dve.tensor_tensor(te(onehot), te(eq), per_token(which), ALU.is_equal))
                if slot == 0:
                    done(dve.scalar_tensor_tensor(biased, onehot, -3.0e38, biased, ALU.mult, ALU.add))
                done(dve.tensor_tensor(tmp, score, onehot, ALU.mult))
                done(dve.tensor_reduce(k.weight[slot], te(tmp), AX.X, ALU.add))
            dve.tensor_tensor(m, first, second, ALU.add).then_inc(s["chosen"], 1)
            done(dve.tensor_tensor(total, k.weight[0], k.weight[1], ALU.add))
            done(dve.reciprocal(total, total))
            for slot in range(2):
                done(dve.tensor_tensor(k.weight[slot], k.weight[slot], total, ALU.mult))
            shared(0)
            outer.full(dve, ("before",))
            b = ps[:, outer.bank(("before",)), :]
            within, whole = b[:, 0:E_], b[:, E_:2 * E_]
            done(dve.tensor_copy(tmp.rearrange("p (e t) -> p t e", t=NT), te(whole)))
            done(dve.tensor_tensor_scan(tmp2, c(k, "restart"), tmp, 0.0, ALU.mult, ALU.add))
            done(dve.tensor_tensor(tmp2, tmp2, tmp, ALU.subtract))
            dve.tensor_tensor(te(pos), te(within), tmp2.rearrange("p (e t) -> p t e", t=NT),
                              ALU.add).then_inc(outer.empty(("before",)), 1)
            dve.wait_ge(outer.empty(("before",)), outer.at[("before",)] // 4 + 1)
            for slot, onehot in enumerate((first, second)):
                done(dve.tensor_tensor(tmp, pos, onehot, ALU.mult))
                done(dve.tensor_reduce(at, te(tmp), AX.X, ALU.add))
                done(dve.tensor_tensor(tmp, c(k, "expert"), onehot, ALU.mult))
                done(dve.tensor_reduce(es, te(tmp), AX.X, ALU.add))
                done(dve.tensor_scalar(ok, at, float(CAP), None, ALU.is_lt))
                done(dve.tensor_tensor(at, at, ok, ALU.mult))
                done(dve.tensor_tensor(k.weight[slot], k.weight[slot], ok, ALU.mult))
                done(dve.scalar_tensor_tensor(at, es, float(CAP), at, ALU.mult, ALU.add))
                done(dve.tensor_copy(k.take[slot], at))
                done(dve.tensor_scalar(ok, ok, -2.0 * NE * CAP, 2.0 * NE * CAP, ALU.mult, ALU.add))
                done(dve.tensor_tensor(at, at, ok, ALU.add))
                done(dve.tensor_copy(k.give[slot], at))
            dve.sem_inc(s["rows_out"], 1)
            for n in range(1, NB):
                shared(n)


def experts(k):
    nc, io, ps = k.nc, k.io, k.ps
    s = sems(k, "expert", "turned xt_out gu_full silu_out h_out down_full y_used")
    y_stored = k.y_stored
    turn_bank, up_bank, down_bank = (4, 5), (6, 7, 0), (1, 2)
    pairs = NE // 2

    def each_pair(eng, body):
        with eng.Fori(0, pairs - 1) as it:
            body(it, 0, False)
            body(it, 1, False)
        body(pairs - 1, 0, False)
        body(pairs - 1, 1, True)

    with nc.Block() as block:

        @block.sync
        def _(sp):
            sp.dma_start(k.xnt[:, :], io["w_attention"]).then_inc(k.attention_in, 16)
            with sp.Fori(0, pairs - 1) as it:
                for p in range(2):
                    e = it * 2 + (p + 2)
                    sp.wait_ge(s["turned"], it * 4 + 2 * (p + 1))
                    sp.dma_start(k.xe[p], k.expert_in.rearrange("(e a p) d -> e p a d", p=P, a=ST)[e]
                                 ).then_inc(k.xe_in[p], 16)
                    sp.wait_ge(s["down_full"], it * 4 + 2 * (p + 1))
                    sp.dma_start(k.w_expert[p], io["w_expert"][e]).then_inc(k.w_in[p], 16)

        @block.tensor
        def _(pe):
            ident = c(k, "ident")

            def turn(p):
                for a in range(ST):
                    for j in range(KT):
                        mm = pe.transpose(ps[:, turn_bank[a], j * P:(j + 1) * P],
                                          k.xe[p][:, a, j * P:(j + 1) * P], ident)
                    mm.then_inc(s["turned"], 1)

            def body(it, p, last):
                up, down = weights(k.w_expert[p])
                pe.wait_ge(k.w_in[p], it * 16 + 16)
                pe.wait_ge(s["xt_out"], it * 4 + 2 * (p + 1))
                for m in range(FM):
                    for h in range(2):
                        for j in range(KT):
                            lo = h * FI + m * P
                            mm = pe.matmul(ps[0:FROWS[m], up_bank[m], h * CAP:(h + 1) * CAP],
                                           up[:, j, lo:lo + FROWS[m]], k.xet[:, j, :],
                                           start=(j == 0), stop=(j == KT - 1))
                    mm.then_inc(s["gu_full"], 1)
                if not last:
                    pe.wait_ge(k.xe_in[1 - p], it * 16 + (16 if p == 0 else 32))
                    turn(1 - p)
                for a in range(ST):
                    pe.wait_ge(s["y_used"], it * 4 + 2 * p + a + 1)
                    for m in range(FM):
                        if a == 0:
                            pe.wait_ge(s["h_out"], it * 6 + 3 * p + m + 1)
                        mm = pe.matmul(ps[:, down_bank[a], :], k.he[0:FROWS[m], m, a * P:(a + 1) * P],
                                       down[0:FROWS[m], m, :], start=(m == 0), stop=(m == FM - 1))
                    mm.then_inc(s["down_full"], 1)

            pe.wait_ge(k.xe_in[0], 16)
            turn(0)
            each_pair(pe, body)

        @block.scalar
        def _(act):
            act.sem_inc(s["y_used"], ST)
            for p in range(2):
                act.sem_inc(y_stored[p], 16)

            def xt(count, a):
                act.wait_ge(s["turned"], count)
                act.activation(k.xet[:, :, a * P:(a + 1) * P],
                               ps[:, turn_bank[a], :].rearrange("p (a b) -> p a b", b=P),
                               ACT.Copy).then_inc(s["xt_out"], 1)

            def body(it, p, last):
                for m in range(FM):
                    act.wait_ge(s["gu_full"], it * 6 + 3 * p + m + 1)
                    r = FROWS[m]
                    act.activation(k.silu_e[0:r, m, :], ps[0:r, up_bank[m], 0:CAP],
                                   ACT.Silu).then_inc(s["silu_out"], 1)
                if not last:
                    for a in range(ST):
                        xt(it * 4 + 2 * (p + 1) + a + 1, a)
                act.wait_ge(y_stored[p], it * 16 + 16)
                for a in range(ST):
                    act.wait_ge(s["down_full"], it * 4 + 2 * p + a + 1)
                    act.activation(k.ye[p][:, a, :], ps[:, down_bank[a], :], ACT.Copy).then_inc(s["y_used"], 1)
                act.wait_ge(s["y_used"], it * 4 + 2 * p + 2 * ST)
                e = it * 2 + p
                act.dma_start(k.expert_out.rearrange("(e a p) d -> e p a d", p=P, a=ST)[e], k.ye[p]
                              ).then_inc(y_stored[p], 16)

            for a in range(ST):
                xt(a + 1, a)
            each_pair(act, body)

        @block.vector
        def _(dve):
            def body(it, p, last):
                for m in range(FM):
                    r = FROWS[m]
                    dve.wait_ge(s["silu_out"], it * 6 + 3 * p + m + 1)
                    dve.tensor_tensor(k.he[0:r, m, :], ps[0:r, up_bank[m], CAP:2 * CAP], k.silu_e[0:r, m, :],
                                      ALU.mult).then_inc(s["h_out"], 1)

            each_pair(dve, body)


def attention_memory(k):
    k.w_attn = [k.xnt[:, i * KT * D:(i + 1) * KT * D].rearrange("p (a b) -> p a b", b=D) for i in range(4)]
    put = Place(k.arena, 0, k.arena_size)
    k.qt, k.kv, k.ksum = put(KT, T), put(KT, P), put(KT, P)
    k.attention_at = put.at


def linear_attention_sums(k):
    nc, io, ps, rows = k.nc, k.io, k.ps, k.rows
    attention_memory(k)
    w_q, w_k, w_v, _ = k.w_attn
    put = Place(k.arena, k.attention_at, k.arena_size)
    taken = [put(D) for _ in range(8)]
    xnt = [put(KT, BW) for _ in range(2)]
    k_biased, kt, vt = put(D), put(2, D), put(2, D)
    b_k, b_v, b_o, decay_row = put(D), put(D), put(D), put(T)
    tiny = Place(k.small, k.tiny_at, 192)
    stats, mv, rstd, ve, b_q = tiny(BT, 6), tiny(BT, 2), tiny(BT), tiny(BT), tiny(KT)

    tasks = []
    for n in range(NB):
        tasks += [("xT", n, j) for j in range(KT)] + [("Q", n, m) for m in range(KT)]
        for i in range(BT):
            tasks += [("K", n, i), ("V", n, i)]
    ring = Ring(k.sem, "sums", [2, 3, 4, 5, 6, 7], tasks)
    s = sems(k, "sums", """biases_in taken_used ln_stats ln_rstd ln_out kb_out k_out v_out kv_used q_out
             kv_full zeroed""")
    taken_in = [k.sem(f"taken_in{i}") for i in range(8)]
    dve_done, pool_done = k.chain["dve"], k.chain["pool"]

    def bank(task):
        return ps[:, ring.bank(task), :]

    with nc.Block() as block:

        @block.sync
        def _(sp):
            for p in range(2):
                sp.wait_ge(k.y_stored[p], 16 * (NE // 2 + 1))
            for to, what in ((b_k, "b_k"), (b_v, "b_v"), (b_o, "b_o"), (decay_row, "decay_row")):
                sp.dma_start(to, io[what].partition_broadcast(P)).then_inc(s["biases_in"], 16)
            sp.dma_start(b_q, io["b_q"]).then_inc(s["biases_in"], 16)

        @block.gpsimd
        def _(pool):
            pool.memset(k.kv, 0.0).then_inc(s["zeroed"], 1)
            pool.memset(k.ksum, 0.0).then_inc(s["zeroed"], 1)
            for p in range(2):
                pool.wait_ge(k.y_stored[p], 16 * (NE // 2 + 1))

            def take(n):
                for i in range(BT):
                    for slot in range(2):
                        q = (n * BT + i) * 2 + slot
                        if q >= 8:
                            pool.wait_ge(s["taken_used"], q - 7)
                        pool.indirect_dma_start(
                            out=taken[q % 8], out_offset=None, in_=k.expert_out[:, :],
                            in_offset=bass.IndirectOffsetOnAxis(
                                ap=k.take[slot][:, n * BT + i:n * BT + i + 1], axis=0),
                            bounds_check=NE * CAP - 1, oob_is_err=False).then_inc(taken_in[q % 8], 16)

            take(0)
            for n in range(NB):
                pool.wait_ge(s["ln_stats"], n + 1)
                pool_done(pool, pool.tensor_scalar(ve, mv[:, :, 1], 1.0, 1e-5, ALU.mult, ALU.add))
                pool.tensor_tensor(rstd, ve, c(k, "neghalf")[:, 0:BT], ALU.pow).then_inc(s["ln_rstd"], 1)
                if n == 0:
                    pool.wait_ge(s["biases_in"], 16 * 5)
                if n + 1 < NB:
                    take(n + 1)
                pool.wait_ge(s["ln_out"], n + 1)
                for i in range(BT):
                    x = rows[:, n * BT + i, 0:D]
                    pool.tensor_tensor(x, x, b_o, ALU.add)
                for m in range(KT):
                    pool.wait_ge(s["q_out"], n * KT + m + 1)
                    q = k.qt[:, m, n * BW:(n + 1) * BW]
                    pool.tensor_tensor(q, q, decay_row[:, n * BW:(n + 1) * BW], ALU.mult)

        @block.scalar
        def _(act):
            act.wait_ge(s["biases_in"], 16 * 5)
            for n in range(NB):
                for j in range(KT):
                    ring.full(act, ("xT", n, j))
                    act.activation(xnt[n % 2][:, j, :], bank(("xT", n, j)),
                                   ACT.Copy).then_inc(ring.empty(("xT", n, j)), 1)
                for m in range(KT):
                    ring.full(act, ("Q", n, m))
                    act.activation(k.qt[:, m, n * BW:(n + 1) * BW], bank(("Q", n, m)), ACT.Relu,
                                   bias=b_q[:, m:m + 1]).then_inc(s["q_out"], 1)
                    act.wait_ge(s["q_out"], n * KT + m + 1)
                    act.sem_inc(ring.empty(("Q", n, m)), 1)
                for i in range(BT):
                    t = n * BT + i
                    act.wait_ge(s["kb_out"], t + 1)
                    if t >= 2:
                        act.wait_ge(s["kv_used"], t - 1)
                    act.activation(kt[:, t % 2, :], k_biased, ACT.Relu,
                                   scale=c(k, "decay")[:, t:t + 1]).then_inc(s["k_out"], 1)

        @block.tensor
        def _(pe):
            ident = c(k, "ident")

            def add_tile(t):
                pe.wait_ge(s["k_out"], t + 1)
                pe.wait_ge(s["v_out"], t + 1)
                for m in range(KT):
                    r = slice(m * P, (m + 1) * P)
                    pe.matmul(ps[:, 0, r], kt[:, t % 2, r], vt[:, t % 2, r], start=(t == 0 and m == 0),
                              stop=(t == NT - 1), skip_group_check=True)
                for m in range(KT):
                    mm = pe.matmul(ps[:, 1, m * DK:(m + 1) * DK], kt[:, t % 2, m * P:(m + 1) * P],
                                   c(k, "ones")[:, 0:DK], start=(t == 0 and m == 0), stop=(t == NT - 1),
                                   skip_group_check=True)
                mm.then_inc(s["kv_used"], 1)

            pe.wait_ge(k.attention_in, 16)
            for n in range(NB):
                pe.wait_ge(s["ln_out"], n + 1)
                for j in range(KT):
                    ring.free(pe, ("xT", n, j))
                    for i in range(BT):
                        mm = pe.transpose(bank(("xT", n, j))[:, i * P:(i + 1) * P],
                                          rows[:, n * BT + i, D + j * P:D + (j + 1) * P], ident)
                    mm.then_inc(ring.filled, 1)
                if n:
                    add_tile(n * BT - 1)
                for m in range(KT):
                    ring.free(pe, ("Q", n, m))
                    for j in range(KT):
                        if m == 0:
                            pe.wait_ge(ring.empty(("xT", n, j)), ring.at[("xT", n, j)] // 6 + 1)
                        mm = pe.matmul(bank(("Q", n, m)), w_q[:, j, m * P:(m + 1) * P], xnt[n % 2][:, j, :],
                                       start=(j == 0), stop=(j == KT - 1))
                    mm.then_inc(ring.filled, 1)
                for i in range(BT):
                    for what, w in (("K", w_k), ("V", w_v)):
                        ring.free(pe, (what, n, i))
                        for j in range(KT):
                            mm = pe.matmul(bank((what, n, i)), xnt[n % 2][:, j, i * P:(i + 1) * P], w[:, j, :],
                                           start=(j == 0), stop=(j == KT - 1))
                        mm.then_inc(ring.filled, 1)
                    if i:
                        add_tile(n * BT + i - 1)
            add_tile(NT - 1)

        @block.vector
        def _(dve):
            def done(ins):
                dve_done(dve, ins)

            def combine_and_norm(n):
                for i in range(BT):
                    t = n * BT + i
                    x = rows[:, t, 0:D]
                    for slot in range(2):
                        q = 2 * t + slot
                        dve.wait_ge(taken_in[q % 8], 16 * (q // 8 + 1))
                        dve.scalar_tensor_tensor(x, taken[q % 8], k.weight[slot][:, t:t + 1], x, ALU.mult,
                                                 ALU.add).then_inc(s["taken_used"], 1)
                        dve.wait_ge(s["taken_used"], q + 1)
                    done(dve.bn_stats(stats[:, i, :], x))
                    ins = dve.bn_aggr(mv[:, i, :], stats[:, i, :])
                ins.then_inc(s["ln_stats"], 1)
                dve.wait_ge(s["ln_rstd"], n + 1)
                for i in range(BT):
                    t = n * BT + i
                    ins = dve.tensor_scalar(rows[:, t, D:2 * D], rows[:, t, 0:D], mv[:, i, 0:1],
                                            rstd[:, i:i + 1], ALU.subtract, ALU.mult)
                ins.then_inc(s["ln_out"], 1)

            combine_and_norm(0)
            dve.wait_ge(s["biases_in"], 16 * 5)
            for n in range(NB):
                if n + 1 < NB:
                    combine_and_norm(n + 1)
                for i in range(BT):
                    t = n * BT + i
                    ring.full(dve, ("K", n, i))
                    if t:
                        dve.wait_ge(s["k_out"], t)
                    dve.tensor_tensor(k_biased, bank(("K", n, i)), b_k, ALU.add).then_inc(s["kb_out"], 1)
                    dve.wait_ge(s["kb_out"], t + 1)
                    dve.sem_inc(ring.empty(("K", n, i)), 1)
                    ring.full(dve, ("V", n, i))
                    if t >= 2:
                        dve.wait_ge(s["kv_used"], t - 1)
                    dve.tensor_tensor(vt[:, t % 2, :], bank(("V", n, i)), b_v, ALU.add).then_inc(s["v_out"], 1)
                    dve.wait_ge(s["v_out"], t + 1)
                    dve.sem_inc(ring.empty(("V", n, i)), 1)
            dve.wait_ge(s["kv_used"], NT)
            dve.wait_ge(s["zeroed"], 2)
            kv = ps[:, 0, :].rearrange("p (a b) -> p a b", b=P)
            ksum = ps[:, 1, 0:KT * DK].rearrange("p (a b) -> p a b", b=DK)
            for g in range(4):
                r = slice(g * DK, (g + 1) * DK)
                dve.tensor_copy(k.kv[r, :, r], kv[r, :, r])
                dve.tensor_copy(k.ksum[r, :, r], ksum[r, :, :])


def linear_attention(k):
    nc, io, ps, rows = k.nc, k.io, k.ps, k.rows
    w_o = k.w_attn[3]
    put = Place(k.arena, k.attention_at, k.arena_size)
    out_t = [put(KT, BW) for _ in range(2)]
    den, inv, router, junk = put(2, BW), put(BW), put(D), put(D)
    k.linear_at = put.at
    tiny = Place(k.small, 0, 192)
    stats, mv, rstd, ve = tiny(BT, 6), tiny(BT, 2), tiny(BT), tiny(BT)
    tasks = []
    for n in range(NB + 1):
        if n < NB:
            for m in range(KT):
                tasks += [("num", n, m), ("den", n, m)]
        if n:
            tasks += [("out", n - 1, i) for i in range(BT)]
    ring = Ring(k.sem, "attention", list(range(8)), tasks)
    s = sems(k, "attention", "router_in den_out out_t ln_stats ln_rstd")
    k.router_in = s["router_in"]
    dve_done, pool_done = k.chain["dve"], k.chain["pool"]

    def bank(task):
        return ps[:, ring.bank(task), :]

    with nc.Block() as block:

        @block.sync
        def _(sp):
            sp.dma_start(router, io["w_router"].partition_broadcast(P)).then_inc(s["router_in"], 16)

        @block.gpsimd
        def _(pool):
            pool.tensor_copy(rows[:, :, 2 * D + 1], c(k, "token"))
            for n in range(NB):
                pool.wait_ge(s["ln_stats"], n + 1)
                pool_done(pool, pool.tensor_scalar(ve, mv[:, :, 1], 1.0, 1e-5, ALU.mult, ALU.add))
                pool.tensor_tensor(rstd, ve, c(k, "neghalf")[:, 0:BT], ALU.pow).then_inc(s["ln_rstd"], 1)

        @block.scalar
        def _(act):
            for n in range(NB):
                for m in range(KT):
                    q = n * KT + m
                    if q >= 2:
                        act.wait_ge(s["out_t"], q - 1)
                    ring.full(act, ("den", n, m))
                    act.activation(den[:, q % 2, :], bank(("den", n, m)), ACT.Copy,
                                   bias=1e-6).then_inc(s["den_out"], 1)
                    act.wait_ge(s["den_out"], q + 1)
                    act.sem_inc(ring.empty(("den", n, m)), 1)

        @block.tensor
        def _(pe):
            for n in range(NB + 1):
                if n < NB:
                    for m in range(KT):
                        for what, w in (("num", k.kv), ("den", k.ksum)):
                            ring.free(pe, (what, n, m))
                            pe.matmul(bank((what, n, m)), w[:, m, :], k.qt[:, m, n * BW:(n + 1) * BW],
                                      start=True, stop=True).then_inc(ring.filled, 1)
                if n:
                    for i in range(BT):
                        ring.free(pe, ("out", n - 1, i))
                        for m in range(KT):
                            pe.wait_ge(s["out_t"], (n - 1) * KT + m + 1)
                            mm = pe.matmul(bank(("out", n - 1, i)), out_t[(n - 1) % 2][:, m, i * P:(i + 1) * P],
                                           w_o[:, m, :], start=(m == 0), stop=(m == KT - 1))
                        mm.then_inc(ring.filled, 1)

        @block.vector
        def _(dve):
            def done(ins):
                dve_done(dve, ins)

            for n in range(NB + 1):
                if n < NB:
                    for m in range(KT):
                        q = n * KT + m
                        dve.wait_ge(s["den_out"], q + 1)
                        done(dve.reciprocal(inv, den[:, q % 2, :]))
                        ring.full(dve, ("num", n, m))
                        dve.tensor_tensor(out_t[n % 2][:, m, :], bank(("num", n, m)), inv,
                                          ALU.mult).then_inc(s["out_t"], 1)
                        dve.wait_ge(s["out_t"], q + 1)
                        dve.sem_inc(ring.empty(("num", n, m)), 1)
                if n:
                    for i in range(BT):
                        t = (n - 1) * BT + i
                        x = rows[:, t, 0:D]
                        ring.full(dve, ("out", n - 1, i))
                        dve.tensor_tensor(x, bank(("out", n - 1, i)), x,
                                          ALU.add).then_inc(ring.empty(("out", n - 1, i)), 1)
                        dve.wait_ge(ring.empty(("out", n - 1, i)), ring.at[("out", n - 1, i)] // 8 + 1)
                        done(dve.bn_stats(stats[:, i, :], x))
                        ins = dve.bn_aggr(mv[:, i, :], stats[:, i, :])
                    ins.then_inc(s["ln_stats"], 1)
                    dve.wait_ge(s["ln_rstd"], n)
                    if n == 1:
                        dve.wait_ge(s["router_in"], 16)
                    for i in range(BT):
                        t = (n - 1) * BT + i
                        done(dve.tensor_scalar(rows[:, t, D:2 * D], rows[:, t, 0:D], mv[:, i, 0:1],
                                               rstd[:, i:i + 1], ALU.subtract, ALU.mult))
                        dve.tensor_tensor_reduce(junk, rows[:, t, D:2 * D], router, 1.0, 0.0, ALU.mult, ALU.add,
                                                 rows[:, t, 2 * D:2 * D + 1])


def select_tokens(k):
    nc, io, ps, rows = k.nc, k.io, k.ps, k.rows
    put = Place(k.arena, 0, k.arena_size)
    score_rows, score_all = put(P), put(T)
    higher = [put(T // 2).bitcast(mybir.dt.bfloat16) for _ in range(3)]
    one = put(1).bitcast(mybir.dt.bfloat16)[:, 0:1]
    same, base = put(2, P), put(4, D)
    tiny = Place(k.small, 0, 192)
    chosen, total, place, past = tiny(NT), tiny(NT), tiny(NT), tiny(NT)
    to = tiny(NT).bitcast(U32)
    s = sems(k, "select", """score_t score_out stored broadcast higher_out counted chosen placed place_out
             one_out base_out""")
    base_in = k.base_in
    dve_done = k.chain["dve"]

    with nc.Block() as block:

        @block.sync
        def _(sp):
            sp.wait_ge(s["score_out"], 1)
            sp.dma_start(k.scores.rearrange("(a b) -> a b", b=P), score_rows[0:NT, :]).then_inc(s["stored"], 16)
            sp.wait_ge(s["stored"], 16)
            sp.dma_start(score_all, k.scores.partition_broadcast(P)).then_inc(s["broadcast"], 16)
            for t in range(NT):
                sp.wait_ge(s["base_out"], t + 1)
                sp.dma_start(io["out"][t * P:(t + 1) * P, :], base[:, t % 4, :]).then_inc(base_in[t % 4], 16)

        @block.gpsimd
        def _(pool):
            for t in range(NT):
                if t >= 4:
                    pool.wait_ge(base_in[t % 4], 16 * (t // 4))
                pool.tensor_tensor(base[:, t % 4, :], rows[:, t, 0:D], rows[:, t, D:2 * D],
                                   ALU.add).then_inc(s["base_out"], 1)
            pool.wait_ge(s["place_out"], 1)
            for t in range(NT):
                pool.indirect_dma_start(
                    out=k.selected[:, :], out_offset=bass.IndirectOffsetOnAxis(ap=to[:, t:t + 1], axis=0),
                    in_=rows[:, t, :], in_offset=None, bounds_check=SEL - 1,
                    oob_is_err=False).then_inc(k.rows_selected, 16)

        @block.scalar
        def _(act):
            act.wait_ge(s["score_t"], 1)
            act.activation(score_rows[0:NT, :], ps[0:NT, 0, 0:P], ACT.Copy).then_inc(s["score_out"], 1)

        @block.tensor
        def _(pe):
            pe.transpose(ps[0:NT, 0, 0:P], rows[:, :, 2 * D], c(k, "ident")).then_inc(s["score_t"], 1)
            pe.wait_ge(s["one_out"], 1)
            for u in range(NT):
                pe.wait_ge(s["higher_out"], u + 1)
                for t in range(NT):
                    mm = pe.matmul(ps[:, 1, t:t + 1], higher[u % 3][:, t * P:(t + 1) * P], one,
                                   start=(u == 0 and t == 0), stop=(u == NT - 1), skip_group_check=True)
                mm.then_inc(s["counted"], 1)
            pe.wait_ge(s["chosen"], 1)
            pe.matmul(ps[:, 2, 0:NT], c(k, "before"), chosen, start=True, stop=True)
            pe.matmul(ps[:, 2, NT:2 * NT], c(k, "ones"), chosen, start=True, stop=True).then_inc(s["placed"], 1)

        @block.vector
        def _(dve):
            def done(ins):
                dve_done(dve, ins)

            dve.memset(one, 1.0).then_inc(s["one_out"], 1)
            dve.wait_ge(s["broadcast"], 16)
            for u in range(NT):
                if u >= 3:
                    dve.wait_ge(s["counted"], u - 2)
                own = rows[:, u, 2 * D:2 * D + 1]
                h, lo, hi = higher[u % 3], u * P, (u + 1) * P
                if u >= 2:
                    dve.wait_ge(s["higher_out"], u - 1)
                done(dve.scalar_tensor_tensor(same[:, u % 2, :], score_all[:, lo:hi], own, c(k, "before"), ALU.is_equal,
                                              ALU.mult))
                if lo:
                    dve.tensor_scalar(h[:, 0:lo], score_all[:, 0:lo], own, None, ALU.is_lt)
                if hi < T:
                    dve.tensor_scalar(h[:, hi:T], score_all[:, hi:T], own, None, ALU.is_le)
                dve.scalar_tensor_tensor(h[:, lo:hi], score_all[:, lo:hi], own, same[:, u % 2, :], ALU.is_lt,
                                         ALU.add).then_inc(s["higher_out"], 1)
            dve.wait_ge(s["counted"], NT)
            dve.tensor_scalar(chosen, ps[:, 1, 0:NT], float(SEL), None, ALU.is_lt).then_inc(s["chosen"], 1)
            dve.wait_ge(s["placed"], 1)
            done(dve.tensor_copy(total, ps[:, 2, NT:2 * NT]))
            done(dve.tensor_tensor_scan(place, c(k, "ones")[:, 0:NT], total, 0.0, ALU.mult, ALU.add))
            done(dve.tensor_tensor(place, place, total, ALU.subtract))
            done(dve.tensor_tensor(place, ps[:, 2, 0:NT], place, ALU.add))
            done(dve.tensor_scalar(past, chosen, -1.0 * T, 1.0 * T, ALU.mult, ALU.add))
            done(dve.tensor_tensor(place, place, past, ALU.add))
            dve.tensor_copy(to, place).then_inc(s["place_out"], 1)


def plan_stream():
    order = [("k", i) for i in range(4)] + [("v", i) for i in range(4)]
    for step in range(NHK + 3):
        if step < NHK:
            order.append(("q", step))
        if step >= 3:
            order.append(("wo", step - 3))
    for step in range(NHK + 1):
        if step < NHK:
            order += [("gate", step), ("up", step)]
        if step:
            order.append(("down", step - 1))
    return order


CHUNKS = plan_stream()
CH = 1024
SLOTS = 8


def hidden_of(sel, j):
    return sel[:, j, D:2 * D]


def residual_of(sel, j):
    return sel[:, j, 0:D]


def selected_layer(k):
    nc, io, ps = k.nc, k.io, k.ps
    put = Place(k.arena, 0, k.arena_size)
    sel, xs, ht, kt = put(ST, ROW), put(ST, D), put(KT, SEL), put(NHK, SEL)
    v, b_v, raw, qt = put(ST, NHK * HD), put(NHK * HD), put(2, 2, SEL), put(2, 2, SEL)
    turn, cosine, t1, t2 = put(ST, 2 * P), put(2, SEL), put(2, SEL), put(2, SEL)
    prob, prob_t, attn = put(2, 3 * P), put(2, 3 * P), put(4, SEL)
    silu, hid = put(2, 2, SEL), put(3, 2, SEL)
    x1, x1s, fin, junk = put(ST, D), put(ST, D), put(ST, D), put(D)
    tiny = Place(k.small, 0, 192)
    ss, ms, rstd, gate, left = tiny(ST), tiny(ST), tiny(ST), tiny(ST), tiny(ST)
    token = tiny(ST).bitcast(U32)
    top, total, inv = tiny(2, 2), tiny(2, 2), tiny(2, 2)
    ln1, ln2, b_q, b_k = tiny(KT), tiny(KT), tiny(NHQ), tiny(NHK)
    slots = [k.xnt[:, i * CH:(i + 1) * CH] for i in range(SLOTS)]

    def chunk(what, i):
        a = slots[CHUNKS.index((what, i)) % SLOTS]
        return a.rearrange("p (a b) -> p a b", b=D if what in ("wo", "down") else 2 * P)

    tasks = [("xT", a) for a in range(2)] + [("turnT",)] + [("k", i) for i in range(4)]
    tasks += [("v", i) for i in range(4)]
    for step in range(NHK + 3):
        if step < NHK:
            tasks.append(("q", step))
        if 1 <= step <= NHK:
            tasks += [("S", step - 1, hh) for hh in range(2)]
        if 2 <= step <= NHK + 1:
            tasks += [("PT", step - 2, hh) for hh in range(2)] + [("PV", step - 2, hh) for hh in range(2)]
    tasks += [("x1T", a) for a in range(2)]
    for i in range(NHK):
        tasks += [("gate", i), ("up", i)]
    ring = Ring(k.sem, "last", [2, 3, 4, 5, 6, 7], tasks)
    s = sems(k, "last", """rows_in small_in rms_in rms_out xs_out ht_out token_out turns_in turn_out raw_out roped
             v_out masked exp_out prob_out pt_out attn_out wo_done x1_out rms2_in rms2_out x1s_out h2_out silu_out
             hid_out down_done fin_out out_stored kt_out gate_out""")
    chunk_in = [k.sem(f"chunk_in{i}") for i in range(SLOTS)]
    dve_done, act_done, pool_done = k.chain["dve"], k.chain["act"], k.chain["pool"]
    scale = float(HD) ** -0.5

    def bank(task):
        return ps[:, ring.bank(task), :]

    def two(a, n=SEL):
        return a.rearrange("p (a b) -> p a b", b=n)

    with nc.Block() as block:

        @block.sync
        def _(sp):
            sp.wait_ge(k.rows_selected, 16 * NT)
            sp.dma_start(sel, k.selected.rearrange("(a p) d -> p a d", p=P)).then_inc(s["rows_in"], 16)
            for to, what in ((ln1, "ln1"), (ln2, "ln2"), (b_q, "bq"), (b_k, "bk")):
                sp.dma_start(to, io[what]).then_inc(s["small_in"], 16)
            sp.dma_start(b_v, io["bv"].partition_broadcast(P)).then_inc(s["small_in"], 16)
            for n, (what, i) in enumerate(CHUNKS):
                if n >= SLOTS:
                    before, j = CHUNKS[n - SLOTS]
                    if before in ("wo", "down"):
                        sp.wait_ge(s[f"{before}_done"], j + 1)
                    else:
                        sp.wait_ge(ring.filled, ring.at[(before, j)] + 1)
                sp.dma_start(slots[n % SLOTS], io["chunks"][n]).then_inc(chunk_in[n % SLOTS], 16)

        @block.gpsimd
        def _(pool):
            def rsqrt(count, ready, out):
                pool.wait_ge(ready, count)
                pool_done(pool, pool.tensor_scalar(ms, ss, 1.0 / D, 1e-6, ALU.mult, ALU.add))
                pool.tensor_tensor(rstd, ms, c(k, "neghalf")[:, 0:ST], ALU.pow).then_inc(out, 1)

            rsqrt(1, s["rms_in"], s["rms_out"])
            pool.wait_ge(s["token_out"], 1)
            for j in range(ST):
                pool.indirect_dma_start(
                    out=turn[:, j, :], out_offset=None, in_=io["turns"],
                    in_offset=bass.IndirectOffsetOnAxis(ap=token[:, j:j + 1], axis=0), bounds_check=T - 1,
                    oob_is_err=False).then_inc(s["turns_in"], 16)
            rsqrt(1, s["rms2_in"], s["rms2_out"])
            pool.wait_ge(s["fin_out"], 1)
            for i in range(4):
                pool.wait_ge(k.base_in[i], 16 * (NT // 4))
            for j in range(ST):
                pool.indirect_dma_start(
                    out=io["out"], out_offset=bass.IndirectOffsetOnAxis(ap=token[:, j:j + 1], axis=0),
                    in_=fin[:, j, :], in_offset=None, bounds_check=T - 1,
                    oob_is_err=False).then_inc(s["out_stored"], 16)
            pool.wait_ge(s["out_stored"], 16 * ST)

        @block.scalar
        def _(act):
            def spread(task, ln, out):
                a = task[1]
                ring.full(act, task)
                for b in range(2):
                    m = a * 2 + b
                    ins = act.activation(ht[:, m, :], bank(task)[:, b * SEL:(b + 1) * SEL], ACT.Copy,
                                         scale=ln[:, m:m + 1])
                ins.then_inc(out, 1)
                act.wait_ge(out, a + 1)
                act.sem_inc(ring.empty(task), 1)

            def biased(task, bias, r):
                if r >= 2:
                    act.wait_ge(s["roped"], r - 1)
                ring.full(act, task)
                for hh in range(2):
                    h = 2 * task[1] + hh
                    ins = act.activation(raw[:, r % 2, hh, :], bank(task)[:, hh * SEL:(hh + 1) * SEL],
                                         ACT.Identity, bias=bias[:, h:h + 1])
                ins.then_inc(s["raw_out"], 1)
                act.wait_ge(s["raw_out"], r + 1)
                act.sem_inc(ring.empty(task), 1)

            act.wait_ge(s["rows_in"], 16)
            act.activation(gate, sel[:, :, 2 * D], ACT.Sigmoid).then_inc(s["gate_out"], 1)
            act.wait_ge(s["small_in"], 16 * 5)
            for a in range(2):
                spread(("xT", a), ln1, s["ht_out"])
            ring.full(act, ("turnT",))
            act.activation(cosine, two(bank(("turnT",))), ACT.Copy).then_inc(s["turn_out"], 1)
            act.wait_ge(s["turn_out"], 1)
            act.sem_inc(ring.empty(("turnT",)), 1)
            for i in range(4):
                biased(("k", i), b_k, i)
            for step in range(NHK + 3):
                if step < NHK:
                    biased(("q", step), b_q, 4 + step)
                if 1 <= step <= NHK:
                    for hh in range(2):
                        h = 2 * (step - 1) + hh
                        act.wait_ge(s["masked"], h + 1)
                        for part, cols in enumerate((slice(0, P), slice(P, 3 * P))):
                            ins = act.activation(prob[:, hh, cols], prob[:, hh, cols], ACT.Exp,
                                                 bias=top[:, hh, part:part + 1], scale=scale,
                                                 accum_out=total[:, hh, part:part + 1])
                        ins.then_inc(s["exp_out"], 1)
                if 2 <= step <= NHK + 1:
                    i = step - 2
                    for hh in range(2):
                        ring.full(act, ("PT", i, hh))
                        act.activation(prob_t[:, hh, :], bank(("PT", i, hh))[:, 0:3 * P],
                                       ACT.Copy).then_inc(s["pt_out"], 1)
                        act.wait_ge(s["pt_out"], 2 * i + hh + 1)
                        act.sem_inc(ring.empty(("PT", i, hh)), 1)
                    for hh in range(2):
                        if i >= 2:
                            act.wait_ge(s["wo_done"], i - 1)
                        ring.full(act, ("PV", i, hh))
                        act.activation(attn[:, (2 * i + hh) % 4, :], bank(("PV", i, hh))[:, 0:SEL],
                                       ACT.Copy).then_inc(s["attn_out"], 1)
                        act.wait_ge(s["attn_out"], 2 * i + hh + 1)
                        act.sem_inc(ring.empty(("PV", i, hh)), 1)
            for a in range(2):
                spread(("x1T", a), ln2, s["h2_out"])
            for i in range(NHK):
                if i >= 2:
                    act.wait_ge(s["hid_out"], i - 1)
                ring.full(act, ("gate", i))
                act.activation(silu[:, i % 2, :, :], two(bank(("gate", i))), ACT.Silu).then_inc(s["silu_out"], 1)
                act.wait_ge(s["silu_out"], i + 1)
                act.sem_inc(ring.empty(("gate", i)), 1)

        @block.tensor
        def _(pe):
            ident = c(k, "ident")

            def arrived(what, i):
                n = CHUNKS.index((what, i))
                pe.wait_ge(chunk_in[n % SLOTS], 16 * (n // SLOTS + 1))

            def turn_rows(name, x):
                for a in range(2):
                    ring.free(pe, (name, a))
                    for b in range(2):
                        m = a * 2 + b
                        for j in range(ST):
                            mm = pe.transpose(bank((name, a))[:, b * SEL + j * P:b * SEL + (j + 1) * P],
                                              x[:, j, m * P:(m + 1) * P], ident)
                    mm.then_inc(ring.filled, 1)

            def features(what, i):
                arrived(what, i)
                ring.free(pe, (what, i))
                for hh in range(2):
                    for j in range(KT):
                        mm = pe.matmul(bank((what, i))[:, hh * SEL:(hh + 1) * SEL],
                                       chunk(what, i)[:, j, hh * P:(hh + 1) * P], ht[:, j, :],
                                       start=(j == 0), stop=(j == KT - 1))
                mm.then_inc(ring.filled, 1)

            pe.wait_ge(s["xs_out"], 1)
            turn_rows("xT", xs)
            pe.wait_ge(s["turns_in"], 16 * ST)
            ring.free(pe, ("turnT",))
            for b in range(2):
                for j in range(ST):
                    mm = pe.transpose(bank(("turnT",))[:, b * SEL + j * P:b * SEL + (j + 1) * P],
                                      turn[:, j, b * P:(b + 1) * P], ident)
            mm.then_inc(ring.filled, 1)
            pe.wait_ge(s["ht_out"], 2)
            for i in range(4):
                features("k", i)
            for i in range(4):
                arrived("v", i)
                ring.free(pe, ("v", i))
                for a in range(ST):
                    for j in range(KT):
                        mm = pe.matmul(bank(("v", i))[:, a * 2 * P:(a + 1) * 2 * P], ht[:, j, a * P:(a + 1) * P],
                                       chunk("v", i)[:, j, :], start=(j == 0), stop=(j == KT - 1))
                mm.then_inc(ring.filled, 1)
            for step in range(NHK + 3):
                if step < NHK:
                    features("q", step)
                if 1 <= step <= NHK:
                    i = step - 1
                    pe.wait_ge(s["roped"], 4 + i + 1)
                    for hh in range(2):
                        ring.free(pe, ("S", i, hh))
                        b = bank(("S", i, hh))
                        pe.matmul(b[:, 0:P], qt[:, i % 2, hh, 0:P], kt[:, i, 0:P], start=True, stop=True)
                        pe.matmul(b[:, P:3 * P], qt[:, i % 2, hh, P:2 * P], kt[:, i, :],
                                  start=True, stop=True).then_inc(ring.filled, 1)
                if 2 <= step <= NHK + 1:
                    i = step - 2
                    for hh in range(2):
                        pe.wait_ge(s["prob_out"], 2 * i + hh + 1)
                        ring.free(pe, ("PT", i, hh))
                        for part in range(3):
                            r = slice(part * P, (part + 1) * P)
                            mm = pe.transpose(bank(("PT", i, hh))[:, r], prob[:, hh, r], ident)
                        mm.then_inc(ring.filled, 1)
                if step >= 3:
                    i = step - 3
                    arrived("wo", i)
                    pe.wait_ge(s["attn_out"], 2 * i + 2)
                    for hh in range(2):
                        for j in range(ST):
                            mm = pe.matmul(ps[:, j, :], attn[:, (2 * i + hh) % 4, j * P:(j + 1) * P],
                                           chunk("wo", i)[:, hh, :], start=(i == 0 and hh == 0),
                                           stop=(i == NHK - 1 and hh == 1), skip_group_check=True)
                    mm.then_inc(s["wo_done"], 1)
                if 2 <= step <= NHK + 1:
                    i = step - 2
                    if i == 0:
                        pe.wait_ge(s["v_out"], 4)
                    for hh in range(2):
                        pe.wait_ge(s["pt_out"], 2 * i + hh + 1)
                        ring.free(pe, ("PV", i, hh))
                        b = bank(("PV", i, hh))
                        vh = slice(i * HD, (i + 1) * HD)
                        pe.matmul(b[:, 0:SEL], v[:, 0, vh], prob_t[:, hh, 0:2 * P], start=True, stop=True)
                        pe.matmul(b[:, P:2 * P], v[:, 1, vh], prob_t[:, hh, 2 * P:3 * P], start=False,
                                  stop=True, skip_group_check=True).then_inc(ring.filled, 1)
            pe.wait_ge(s["x1s_out"], 1)
            turn_rows("x1T", x1s)
            pe.wait_ge(s["h2_out"], 2)
            for step in range(NHK + 1):
                if step < NHK:
                    features("gate", step)
                    features("up", step)
                if step:
                    i = step - 1
                    arrived("down", i)
                    pe.wait_ge(s["hid_out"], i + 1)
                    for b in range(2):
                        for j in range(ST):
                            mm = pe.matmul(ps[:, j, :], hid[:, i % 3, b, j * P:(j + 1) * P],
                                           chunk("down", i)[:, b, :], start=(i == 0 and b == 0),
                                           stop=(i == NHK - 1 and b == 1), skip_group_check=True)
                    mm.then_inc(s["down_done"], 1)

        @block.vector
        def _(dve):
            def done(ins):
                dve_done(dve, ins)

            def rope(r, out, out_sem):
                dve.wait_ge(s["raw_out"], r + 1)
                if r:
                    dve.wait_ge(s["roped"], r)
                x = raw[:, r % 2, :, :]
                lo, hi = slice(0, 64), slice(64, 128)
                co = cosine[:, 0, :].unsqueeze(1).to_broadcast((P, 2, SEL))
                si = cosine[:, 1, :].unsqueeze(1).to_broadcast((P, 2, SEL))
                dve.tensor_tensor(t1, x, co, ALU.mult)
                dve.tensor_tensor(t2[lo], x[hi], si[hi], ALU.mult)
                done(dve.tensor_tensor(t2[hi], x[lo], si[lo], ALU.mult))
                dve.tensor_tensor(out, t1, t2, ALU.add).then_inc(s["roped"], 1)

            def square_mean(x, ready):
                for j in range(ST):
                    ins = dve.tensor_tensor_reduce(junk, x(j), x(j), 1.0, 0.0, ALU.mult, ALU.add,
                                                   ss[:, j:j + 1])
                    if j == 0:
                        done(ins)
                ins.then_inc(ready, 1)

            dve.wait_ge(s["rows_in"], 16)
            dve.tensor_copy(token, sel[:, :, 2 * D + 1]).then_inc(s["token_out"], 1)
            square_mean(lambda j: hidden_of(sel, j), s["rms_in"])
            dve.wait_ge(s["rms_out"], 1)
            for j in range(ST):
                ins = dve.tensor_scalar(xs[:, j, :], hidden_of(sel, j), rstd[:, j:j + 1], None, ALU.mult)
            ins.then_inc(s["xs_out"], 1)
            dve.wait_ge(s["gate_out"], 1)
            dve.tensor_scalar(left, gate, -1.0, 1.0, ALU.mult, ALU.add)
            dve.wait_ge(s["turn_out"], 1)
            for i in range(4):
                rope(i, kt[:, 2 * i:2 * i + 2, :], s["kt_out"])
            dve.wait_ge(s["small_in"], 16 * 5)
            for i in range(4):
                r = slice(i * 2 * P, (i + 1) * 2 * P)
                ring.full(dve, ("v", i))
                dve.tensor_tensor(v[:, :, r], two(bank(("v", i))), b_v[:, r].unsqueeze(1).to_broadcast((P, ST, 2 * P)),
                                  ALU.add).then_inc(s["v_out"], 1)
                dve.wait_ge(s["v_out"], i + 1)
                dve.sem_inc(ring.empty(("v", i)), 1)
            for step in range(NHK + 1):
                if step < NHK:
                    rope(4 + step, qt[:, step % 2, :, :], None)
                if step:
                    i = step - 1
                    for hh in range(2):
                        h = 2 * i + hh
                        ring.full(dve, ("S", i, hh))
                        if h >= 2:
                            ring.full(dve, ("PT", i - 1, hh))
                        dve.tensor_tensor(prob[:, hh, :], bank(("S", i, hh))[:, 0:3 * P], c(k, "addmask"),
                                          ALU.add).then_inc(ring.empty(("S", i, hh)), 1)
                        dve.wait_ge(ring.empty(("S", i, hh)), ring.at[("S", i, hh)] // 6 + 1)
                        dve.tensor_reduce(top[:, hh, 0:1], prob[:, hh, 0:P], AX.X, ALU.max)
                        done(dve.tensor_reduce(top[:, hh, 1:2], prob[:, hh, P:3 * P], AX.X, ALU.max))
                        dve.tensor_scalar(top[:, hh, :], top[:, hh, :], -scale, None,
                                          ALU.mult).then_inc(s["masked"], 1)
                    for hh in range(2):
                        h = 2 * i + hh
                        dve.wait_ge(s["exp_out"], h + 1)
                        done(dve.reciprocal(inv[:, hh, :], total[:, hh, :]))
                        dve.tensor_scalar(prob[:, hh, 0:P], prob[:, hh, 0:P], inv[:, hh, 0:1], None, ALU.mult)
                        dve.tensor_scalar(prob[:, hh, P:3 * P], prob[:, hh, P:3 * P], inv[:, hh, 1:2], None,
                                          ALU.mult).then_inc(s["prob_out"], 1)
            dve.wait_ge(s["wo_done"], NHK)
            for j in range(ST):
                ins = dve.tensor_tensor(x1[:, j, :], ps[:, j, :], hidden_of(sel, j),
                                        ALU.add)
            done(ins)
            square_mean(lambda j: x1[:, j, :], s["rms2_in"])
            dve.wait_ge(s["rms2_out"], 1)
            for j in range(ST):
                ins = dve.tensor_scalar(x1s[:, j, :], x1[:, j, :], rstd[:, j:j + 1], None, ALU.mult)
            ins.then_inc(s["x1s_out"], 1)
            for i in range(NHK):
                ring.full(dve, ("up", i))
                dve.wait_ge(s["silu_out"], i + 1)
                if i >= 3:
                    dve.wait_ge(s["down_done"], i - 2)
                dve.tensor_tensor(hid[:, i % 3, :, :], two(bank(("up", i))), silu[:, i % 2, :, :],
                                  ALU.mult).then_inc(s["hid_out"], 1)
                dve.wait_ge(s["hid_out"], i + 1)
                dve.sem_inc(ring.empty(("up", i)), 1)
            dve.wait_ge(s["down_done"], NHK)
            for j in range(ST):
                done(dve.tensor_tensor(x1[:, j, :], ps[:, j, :], x1[:, j, :], ALU.add))
                done(dve.tensor_scalar(x1[:, j, :], x1[:, j, :], gate[:, j:j + 1], None, ALU.mult))
                done(dve.scalar_tensor_tensor(x1[:, j, :], hidden_of(sel, j), left[:, j:j + 1], x1[:, j, :],
                                              ALU.mult, ALU.add))
                ins = dve.tensor_tensor(fin[:, j, :], x1[:, j, :], residual_of(sel, j), ALU.add)
            ins.then_inc(s["fin_out"], 1)


def build(nc, io):
    with ExitStack() as ctx:
        ctx.enter_context(nc.allow_non_contiguous_dma("weights in tiles"))
        k = setup(nc, ctx, io)
        k.expert_in = nc.dram_tensor("expert_in", (NE * CAP, D), F32, kind="Internal").ap()
        k.expert_out = nc.dram_tensor("expert_out", (NE * CAP, D), F32, kind="Internal").ap()
        k.given = k.sem("rows_given")
        k.scores = nc.dram_tensor("scores", (T,), F32, kind="Internal").ap()
        k.selected = nc.dram_tensor("selected", (SEL, ROW), F32, kind="Internal").ap()
        k.rows_selected = k.sem("rows_selected")
        k.attention_in = k.sem("attention_weights_in")
        k.w_in, k.xe_in = ([k.sem(f"{n}{p}") for p in range(2)] for n in ("w_expert_in", "rows_in"))
        k.base_in = [k.sem(f"base_stored{i}") for i in range(4)]
        k.w_shared = k.arena[:, 0:KT * 2 * FI + FM * D]
        k.s_shared = k.sem("shared_in")
        k.y_stored = [k.sem(f"y_stored{p}") for p in range(2)]
        k.phase_sems.clear()
        gated_linear_attention(k)
        expert_memory(k)
        route_and_shared(k)
        experts(k)
        recycle(k)
        linear_attention_sums(k)
        linear_attention(k)
        select_tokens(k)
        selected_layer(k)


def layout(inputs):
    f = {n: np.asarray(a) for n, a in inputs.items()}

    def rows_first(w):
        return np.ascontiguousarray(w.reshape(-1, P, w.shape[1]).transpose(1, 0, 2))

    def expert(w1, w3, w2):
        up = np.concatenate([rows_first(w1.T), rows_first(w3.T)], axis=2).reshape(P, -1)
        w2t = np.concatenate([w2.T, np.zeros((FM * P - FI, D), np.float32)], axis=0)
        return np.concatenate([up, rows_first(w2t).reshape(P, -1)], axis=1)

    out = {"consts": constants(), "x": np.ascontiguousarray(f["L0_attn_hidden_states"].reshape(T, D))}
    out["w_qk"] = rows_first(np.concatenate([f["L0_attn_Wq"].T] * 4 + [f["L0_attn_Wk"].T] * 4, axis=1))
    out["w_ig"] = rows_first(f["L0_attn_Wig"].T)
    out["w_og"] = rows_first(f["L0_attn_Wog"].T)
    out["g_weight"] = f["L0_attn_g_weight"]
    out["w_shared"] = expert(f["L0_ffn_Ws1"], f["L0_ffn_Ws3"], f["L0_ffn_Ws2"])
    w = {n: f[f"L1_ffn_{n}"] for n in ("wq", "wk", "wv", "wo", "w_gate", "w_up", "w_down")}
    source = {"q": w["wq"], "k": w["wk"], "v": w["wv"], "wo": w["wo"], "gate": w["w_gate"], "up": w["w_up"],
              "down": w["w_down"]}
    chunks = []
    for what, i in CHUNKS:
        part = slice(i * 2 * P, (i + 1) * 2 * P)
        a = source[what][part, :] if what in ("wo", "down") else source[what][:, part]
        chunks.append(rows_first(a).reshape(P, CH))
    out["chunks"] = np.stack(chunks)
    for n, m in (("ln1", "ln1_w"), ("ln2", "ln2_w"), ("bq", "bq"), ("bk", "bk")):
        out[n] = np.ascontiguousarray(f[f"L1_ffn_{m}"].reshape(-1, P).T)
    out["bv"] = f["L1_ffn_bv"]
    out["turns"] = turns()
    out["w_attention"] = np.concatenate(
        [rows_first(f[f"L1_attn_W{n}"].T).reshape(P, -1) for n in "qkvo"], axis=1)
    for n in "kvo":
        out[f"b_{n}"] = f[f"L1_attn_b{n}"]
    out["b_q"] = np.ascontiguousarray(f["L1_attn_bq"].reshape(KT, P).T)
    out["decay_row"] = np.exp(-np.arange(T, dtype=np.float32) / np.float32(T))
    out["w_router"] = f["L1_ffn_w_router"]
    out["gate_w"] = rows_first(f["L0_ffn_gate_w"].T)
    out["gate_b"] = f["L0_ffn_gate_b"]
    out["w_expert"] = np.stack([expert(f["L0_ffn_W1"][e], f["L0_ffn_W3"][e], f["L0_ffn_W2"][e]) for e in range(NE)])
    return out


def kernel(**inputs):
    import concourse.bacc as _bacc
    from concourse.bass_utils import run_bass_kernel_spmd as _run

    nc = _bacc.Bacc("TRN2", target_bir_lowering=False, num_devices=1)
    arrays, io = {}, {}
    for name, a in layout(inputs).items():
        arrays[f"in_{name}_dram"] = a
        io[name] = nc.dram_tensor(f"in_{name}_dram", a.shape, mybir.dt.from_np(a.dtype), kind="ExternalInput").ap()
    io["out"] = nc.dram_tensor("out_0_dram", (T, D), F32, kind="ExternalOutput").ap()
    build(nc, io)
    r = _run(nc, [arrays], core_ids=[0])
    return r.results[0]["out_0_dram"].reshape(1, T, D)
```

```python
from contextlib import ExitStack

import numpy as np

import concourse.bass as bass
from concourse import mybir

ALU = mybir.AluOpType
ACT = mybir.ActivationFunctionType
AX = mybir.AxisListType
F32 = mybir.dt.float32
U32 = mybir.dt.uint32
BF16 = mybir.dt.bfloat16

P = 128
T = 2048
D = 512
NT = T // P
KT = D // P
NB = 4
BT = NT // NB
BW = T // NB
DK = 32
SUB = 32
NE = 16
CAP = 256
FI = 352
FM = 3
SEL = 256
ST = SEL // P
HD = 128
NHQ, NHK = 16, 8
FF = 2048
FFT = FF // P
ROW = 2 * D + 1

_AT = {}
_n = 0
for _name, _w in (("ident", P), ("causal", P), ("before", P), ("ones", P), ("own", 16), ("cq", 16), ("ck", 16),
                  ("expert", NE), ("rank", NE), ("restart", NT * NE), ("decay", NT),
                  ("neghalf", NT), ("addmask", 3 * P), ("earlier", P), ("slot", SEL),
                  ("number", 2 * NT)):
    _AT[_name] = (_n, _n + _w)
    _n += _w
NCONST = _n
SMALL = 256


def constants():
    c = np.zeros((P, NCONST), np.float32)

    def put(name, a):
        lo, hi = _AT[name]
        c[:, lo:hi] = np.asarray(a, np.float32).reshape(P, hi - lo)

    r = np.arange(P)
    put("ident", np.eye(P))
    put("causal", r[:, None] <= r[None, :])
    put("before", r[:, None] < r[None, :])
    lower = np.where(r[None, :] <= r[:, None], 0.0, -3.0e38)
    put("addmask", np.concatenate([lower, np.zeros((P, P)), lower], axis=1))
    put("ones", np.ones((P, P)))
    g = r // SUB
    own = np.zeros((P, BT, 4))
    cq = np.zeros((P, BT, 4))
    ck = np.zeros((P, BT, 4))
    for b in range(4):
        own[g == b, :, b] = 1
    cq[g == 0, :, 2] = 1
    cq[g == 1, :, 1] = 1
    cq[g == 2, :, 3] = 1
    cq[g == 3, :, 0] = 1
    put("own", own)
    put("cq", cq)
    put("ck", ck)
    put("expert", np.broadcast_to(np.arange(NE), (P, NE)))
    put("rank", np.broadcast_to(NE - np.arange(NE), (P, NE)))
    put("restart", np.broadcast_to(np.arange(NT) > 0, (P, NE, NT)))
    token = np.arange(NT)[None, :] * P + r[:, None]
    put("decay", np.exp(-token.astype(np.float32) / np.float32(T)))
    put("neghalf", np.full((P, NT), -0.5))
    put("earlier", r[None, :] < r[:, None])
    put("slot", np.broadcast_to(np.arange(SEL), (P, SEL)))
    put("number", np.stack([np.broadcast_to(r[:, None], (P, NT)), np.broadcast_to(np.arange(NT), (P, NT))], axis=2))
    return c


def turns():
    freq = (1.0 / np.float32(10000.0) ** (np.arange(0, HD, 2, dtype=np.float32) / np.float32(HD))).astype(np.float32)
    ang = np.arange(T, dtype=np.float32)[:, None] * freq
    co, si = np.cos(ang).astype(np.float32), np.sin(ang).astype(np.float32)
    return np.concatenate([co, co, si, -si], axis=1)


class Ring:

    def __init__(self, sem, name, banks, tasks):
        self.banks = banks
        self.at = {t: i for i, t in enumerate(tasks)}
        assert len(self.at) == len(tasks)
        self.filled = sem(f"{name}_filled")
        self.drained = [sem(f"{name}_drained{b}") for b in banks]

    def bank(self, task):
        return self.banks[self.at[task] % len(self.banks)]

    def free(self, pe, task):
        k, n = divmod(self.at[task], len(self.banks))
        if k:
            pe.wait_ge(self.drained[n], k)

    def full(self, eng, task):
        eng.wait_ge(self.filled, self.at[task] + 1)

    def empty(self, task):
        return self.drained[self.at[task] % len(self.banks)]

    def all_drained(self, pe):
        total = len(self.at)
        for n in range(len(self.banks)):
            uses = (total - n + len(self.banks) - 1) // len(self.banks)
            if uses:
                pe.wait_ge(self.drained[n], uses)


class Chain:

    def __init__(self, sem):
        self.sem, self.n = sem, 0

    def __call__(self, eng, ins):
        ins.then_inc(self.sem, 1)
        self.n += 1
        eng.wait_ge(self.sem, self.n)


class Build:
    pass


def setup(nc, ctx, io):
    k = Build()
    k.nc, k.ctx, k.io = nc, ctx, io
    k.phase_sems = []

    def sem(name):
        k.phase_sems.append(nc.alloc_semaphore(name))
        return k.phase_sems[-1]

    k.sem = sem
    k.rows = ctx.enter_context(nc.sbuf_tensor("rows", [P, NT, ROW], F32))
    k.xnt = ctx.enter_context(nc.sbuf_tensor("xnt", [P, KT * T], F32))
    k.con = ctx.enter_context(nc.sbuf_tensor("con", [P, NCONST], F32))
    k.small = ctx.enter_context(nc.sbuf_tensor("small", [P, SMALL], F32))
    k.token_at = SMALL - ST
    k.token = k.small[:, k.token_at:SMALL].bitcast(U32)
    k.arena_size = 26368
    k.arena = ctx.enter_context(nc.sbuf_tensor("arena", [P, k.arena_size], F32))
    k.ps = ctx.enter_context(nc.psum_tensor("ps", [P, 8, 512], F32))
    k.chain = {e: Chain(k.sem(f"{e}_done")) for e in ("dve", "act", "pool")}
    k.s_con = k.sem("constants_in")
    return k


def c(k, name, rows=slice(0, P)):
    lo, hi = _AT[name]
    return k.con[rows, lo:hi]


def recycle(k):
    k.nc.all_engine_barrier()
    k.nc.clear_and_free_semaphores(k.phase_sems)
    k.phase_sems.clear()
    k.nc.all_engine_barrier()


class Place:

    def __init__(self, tensor, at, end):
        self.tensor, self.at, self.end = tensor, at, end

    def __call__(self, *dims):
        n = int(np.prod(dims))
        a = self.tensor[:, self.at:self.at + n]
        self.at += n
        assert self.at <= self.end, (self.at, self.end)
        if len(dims) == 2:
            a = a.rearrange("p (a b) -> p a b", b=dims[1])
        if len(dims) == 3:
            a = a.rearrange("p (a b c) -> p a b c", b=dims[1], c=dims[2])
        return a


def wide(ap, n):
    return ap.unsqueeze(2).to_broadcast((ap.shape[0], ap.shape[1], n))


def sems(k, prefix, names):
    return {n: k.sem(f"{prefix}_{n}") for n in names.split()}


def gated_linear_attention(k):
    nc, io, ps, rows = k.nc, k.io, k.ps, k.rows
    put = Place(k.arena, 4352, k.arena_size)
    w_qk, w_og, w_ig, gw = put(KT, 2 * P), put(KT, D), put(KT, D), put(D)
    xn = [put(BT, D) for _ in range(2)]
    put_x = Place(k.xnt, 0, KT * T)
    xnt = [put_x(KT, BW) for _ in range(2)]
    ksig, decay, qsig, starts, prod, inv, qs = (put(BW) for _ in range(7))
    qd, kd, qx, kx = (put(BW) for _ in range(4))
    att, kst, state = put(BT, P), put(BT, DK), put(2, D)
    o, ot, sg = put(2, D), put(2, KT, P), put(2, D)
    og, gated, junk = put(D), put(D), put(D)
    tiny = Place(k.small, 0, SMALL)
    stats, mv, rstd, ve = tiny(BT, 6), tiny(BT, 2), tiny(BT), tiny(BT)
    ss, rr, ms = tiny(BT), tiny(BT), tiny(BT)
    stats2, mv2, rstd2, ve2 = tiny(BT, 6), tiny(BT, 2), tiny(BT), tiny(BT)
    cq, ck, own = c(k, "cq"), c(k, "ck"), c(k, "own")

    tasks = []
    for n in range(NB):
        tasks += [("xT", n, i) for i in range(KT)] + [("q", n), ("k", n), ("AT", n), ("KST", n)]
        tasks += [("U", n, 0), ("o", n, 0), ("U", n, 1), ("o", n, 1), ("oT", n, 0), ("U", n, 2), ("o", n, 2),
                  ("oT", n, 1), ("U", n, 3), ("o", n, 3), ("oT", n, 2), ("oT", n, 3)]
    ring = Ring(k.sem, "gla", [4, 5, 6, 7], tasks)
    x_in = [k.sem(f"x_in{n}") for n in range(NB)]
    s = sems(k, "gla", """w_qk_in w_og_in w_ig_in gw_in ln_stats ln_rstd ln_out xnt_out decay_out qsig_out
             features att_out kst_out state_out o_out square_out rr_out ot_out go_full go_empty sg_out sg_used
             og_out ln2_stats ln2_rstd zero_out zeros_in""")
    dve_done, act_done, pool_done = k.chain["dve"], k.chain["act"], k.chain["pool"]

    def bank(task):
        return ps[:, ring.bank(task), :]

    with nc.Block() as block:

        @block.sync
        def _(sp):
            sp.dma_start(k.con[:, :], io["consts"]).then_inc(k.s_con, 16)
            for n in range(NB):
                x = io["x"].rearrange("(t p) d -> p t d", p=P)[:, n * BT:(n + 1) * BT, :]
                sp.dma_start(rows[:, n * BT:(n + 1) * BT, 0:D], x).then_inc(x_in[n], 16)
                if n == 0:
                    sp.dma_start(w_qk, io["w_qk"]).then_inc(s["w_qk_in"], 16)
                    sp.dma_start(w_ig, io["w_ig"]).then_inc(s["w_ig_in"], 16)
                    sp.dma_start(w_og, io["w_og"]).then_inc(s["w_og_in"], 16)
                    sp.dma_start(gw, io["g_weight"].partition_broadcast(P)).then_inc(s["gw_in"], 16)
            sp.dma_start(k.w_shared, io["w_shared"]).then_inc(k.s_shared, 16)
            sp.wait_ge(s["zero_out"], 1)
            zeros = og.unsqueeze(1).to_broadcast((P, NE * CAP // P, D))
            sp.dma_start(k.expert_in.rearrange("(p r) d -> p r d", p=P), zeros).then_inc(s["zeros_in"], 16)

        @block.gpsimd
        def _(pool):
            pool.wait_ge(k.s_con, 16)

            def rsqrt(out, tmp, src, scale, done, eps=1e-5):
                pool_done(pool, pool.tensor_scalar(tmp, src, scale, eps, ALU.mult, ALU.add))
                n = out.shape[1]
                pool.tensor_tensor(out, tmp, c(k, "neghalf")[:, 0:n], ALU.pow).then_inc(done, 1)

            pool.wait_ge(s["ln_stats"], 1)
            rsqrt(rstd, ve, mv[:, :, 1], 1.0, s["ln_rstd"])
            for n in range(NB):
                if n + 1 < NB:
                    pool.wait_ge(s["ln_stats"], n + 2)
                    rsqrt(rstd, ve, mv[:, :, 1], 1.0, s["ln_rstd"])
                for i in range(BT):
                    pool.wait_ge(s["square_out"], n * BT + i + 1)
                    rsqrt(rr[:, i:i + 1], ms[:, i:i + 1], ss[:, i:i + 1], 1.0 / D, s["rr_out"])
                pool.wait_ge(s["ln2_stats"], n + 1)
                rsqrt(rstd2, ve2, mv2[:, :, 1], 1.0, s["ln2_rstd"])

        @block.scalar
        def _(act):
            def o_out(n, i):
                t = n * BT + i
                if t >= 2:
                    act.wait_ge(s["og_out"], t - 1)
                ring.full(act, ("o", n, i))
                act.activation(o[:, i % 2, :], bank(("o", n, i)), ACT.Copy).then_inc(s["o_out"], 1)
                act.activation(junk, bank(("o", n, i)), ACT.Square,
                               accum_out=ss[:, i:i + 1]).then_inc(s["square_out"], 1)
                act.wait_ge(s["square_out"], t + 1)
                act.sem_inc(ring.empty(("o", n, i)), 1)

            def ot_out(n, i):
                ring.full(act, ("oT", n, i))
                act.activation(ot[:, i % 2, :, :], bank(("oT", n, i)).rearrange("p (a b) -> p a b", b=P),
                               ACT.Copy).then_inc(ring.empty(("oT", n, i)), 1)

            def sg_out(n, i):
                t = n * BT + i
                act.wait_ge(s["go_full"], t + 1)
                if t >= 2:
                    act.wait_ge(s["sg_used"], t - 1)
                act.activation(sg[:, i % 2, :], ps[:, i, :], ACT.Sigmoid).then_inc(s["sg_out"], 1)

            for n in range(NB):
                for i in range(KT):
                    ring.full(act, ("xT", n, i))
                    act.activation(xnt[n % 2][:, i, :], bank(("xT", n, i)),
                                   ACT.Copy).then_inc(ring.empty(("xT", n, i)), 1)
                ring.full(act, ("k", n))
                if n:
                    act.wait_ge(s["features"], n)
                act_done(act, act.activation(ksig, bank(("k", n)), ACT.Sigmoid))
                act.activation(decay, ksig, ACT.Sigmoid, scale=-1.0).then_inc(s["decay_out"], 1)
                act.activation(qsig, bank(("q", n)), ACT.Sigmoid).then_inc(s["qsig_out"], 1)
                o_out(n, 0)
                o_out(n, 1)
                ot_out(n, 0)
                o_out(n, 2)
                ot_out(n, 1)
                sg_out(n, 0)
                o_out(n, 3)
                ot_out(n, 2)
                sg_out(n, 1)
                ot_out(n, 3)
                sg_out(n, 2)
                sg_out(n, 3)

        @block.tensor
        def _(pe):
            pe.wait_ge(k.s_con, 16)
            ident = c(k, "ident")

            def project_out(n, i):
                t = n * BT + i
                pe.wait_ge(ring.empty(("oT", n, i)), ring.at[("oT", n, i)] // 4 + 1)
                for j in range(KT):
                    mm = pe.matmul(ps[:, i, :], ot[:, i % 2, j, :], w_og[:, j, :], start=False, stop=(j == KT - 1))
                mm.then_inc(s["go_full"], 1)

            def project_in(n, i):
                t = n * BT + i
                if n:
                    pe.wait_ge(s["go_empty"], t - BT + 1)
                for j in range(KT):
                    pe.matmul(ps[:, i, :], xnt[n % 2][:, j, i * P:(i + 1) * P], w_ig[:, j, :],
                              start=(j == 0), stop=False)

            def update(n, i):
                ring.free(pe, ("U", n, i))
                pe.matmul(bank(("U", n, i))[96:128, :], kst[:, i, :], xn[n % 2][:, i, :],
                          start=True, stop=True).then_inc(ring.filled, 1)

            def output(n, i):
                t = n * BT + i
                ring.free(pe, ("o", n, i))
                pe.matmul(bank(("o", n, i)), att[:, i, :], xn[n % 2][:, i, :], start=True, stop=False)
                pe.wait_ge(s["state_out"], t + 1)
                pe.matmul(bank(("o", n, i)), qx[96:128, i * P:(i + 1) * P], state[96:128, t % 2, :],
                          start=False, stop=True).then_inc(ring.filled, 1)

            def turn(n, i):
                t = n * BT + i
                pe.wait_ge(s["o_out"], t + 1)
                ring.free(pe, ("oT", n, i))
                for j in range(KT):
                    mm = pe.transpose(bank(("oT", n, i))[:, j * P:(j + 1) * P], o[:, i % 2, j * P:(j + 1) * P], ident)
                mm.then_inc(ring.filled, 1)

            for n in range(NB):
                pe.wait_ge(s["ln_out"], n + 1)
                for j in range(KT):
                    ring.free(pe, ("xT", n, j))
                    for i in range(BT):
                        mm = pe.transpose(bank(("xT", n, j))[:, i * P:(i + 1) * P],
                                          xn[n % 2][:, i, j * P:(j + 1) * P], ident)
                    mm.then_inc(ring.filled, 1)
                if n == 0:
                    pe.wait_ge(s["w_qk_in"], 16)
                for h, what in enumerate("qk"):
                    ring.free(pe, (what, n))
                    for j in range(KT):
                        if h == 0:
                            pe.wait_ge(ring.empty(("xT", n, j)), ring.at[("xT", n, j)] // 4 + 1)
                        mm = pe.matmul(bank((what, n)), w_qk[:, j, h * P:(h + 1) * P], xnt[n % 2][:, j, :],
                                       start=(j == 0), stop=(j == KT - 1))
                    mm.then_inc(ring.filled, 1)
                if n == 0:
                    pe.wait_ge(s["w_ig_in"], 16)
                for i in range(3):
                    project_in(n, i)
                pe.wait_ge(s["features"], n + 1)
                ring.free(pe, ("AT", n))
                for i in range(BT):
                    r = slice(i * P, (i + 1) * P)
                    pe.matmul(bank(("AT", n))[:, r], kd[:, r], qd[:, r], start=True, stop=False)
                    mm = pe.matmul(bank(("AT", n))[:, r], kx[0:96, r], qx[0:96, r], start=False, stop=True)
                mm.then_inc(ring.filled, 1)
                ring.free(pe, ("KST", n))
                for i in range(BT):
                    mm = pe.transpose(bank(("KST", n))[:, i * DK:(i + 1) * DK], kx[96:128, i * P:(i + 1) * P],
                                      ident[96:128, 96:128])
                mm.then_inc(ring.filled, 1)
                project_in(n, 3)
                pe.wait_ge(s["kst_out"], n + 1)
                pe.wait_ge(s["att_out"], n + 1)
                if n == 0:
                    pe.wait_ge(s["w_og_in"], 16)
                update(n, 0)
                output(n, 0)
                update(n, 1)
                output(n, 1)
                turn(n, 0)
                update(n, 2)
                output(n, 2)
                turn(n, 1)
                project_out(n, 0)
                update(n, 3)
                output(n, 3)
                turn(n, 2)
                project_out(n, 1)
                turn(n, 3)
                project_out(n, 2)
                project_out(n, 3)

        @block.vector
        def _(dve):
            def done(ins):
                dve_done(dve, ins)

            def ln_in(n):
                dve.wait_ge(x_in[n], 16)
                for i in range(BT):
                    done(dve.bn_stats(stats[:, i, :], rows[:, n * BT + i, 0:D]))
                for i in range(BT):
                    ins = dve.bn_aggr(mv[:, i, :], stats[:, i, :])
                ins.then_inc(s["ln_stats"], 1)
                dve.wait_ge(s["ln_rstd"], n + 1)
                for i in range(BT):
                    ins = dve.tensor_scalar(xn[n % 2][:, i, :], rows[:, n * BT + i, 0:D], mv[:, i, 0:1],
                                            rstd[:, i:i + 1], ALU.subtract, ALU.mult)
                ins.then_inc(s["ln_out"], 1)

            def features(n):
                dve.wait_ge(s["decay_out"], n + 1)
                first = decay.rearrange("p (c t) -> p c t", t=SUB)[:, :, 0:1]
                done(dve.tensor_copy(starts.rearrange("p (c t) -> p c t", t=SUB)[:, :, 0:1], first))
                done(dve.memset(first, 0.0))
                done(dve.tensor_tensor_scan(prod, decay, starts, 0.0, ALU.mult, ALU.add))
                dve.reciprocal(inv, prod)
                ring.full(dve, ("q", n))
                dve.wait_ge(s["qsig_out"], n + 1)
                ins = dve.scalar_tensor_tensor(qs, bank(("q", n)), float(DK) ** -0.5, qsig, ALU.mult, ALU.mult)
                ins.then_inc(ring.empty(("q", n)), 1)
                dve.sem_inc(ring.empty(("k", n)), 1)
                end = prod.rearrange("p (c b t) -> p c b t", b=4, t=SUB)[:, :, :, SUB - 1]
                q3, k3 = (a.rearrange("p (c b) -> p c b", b=4) for a in (cq, ck))

                def whole(g, b):
                    return end[g * SUB:(g + 1) * SUB, :, b]

                def q_(g, b):
                    return q3[g * SUB:(g + 1) * SUB, :, b]

                def k_(g, b):
                    return k3[g * SUB:(g + 1) * SUB, :, b]

                dve.tensor_copy(q_(0, 3), whole(0, 2))
                dve.tensor_copy(q_(3, 1), whole(3, 0))
                dve.tensor_copy(k_(0, 1), whole(0, 1))
                dve.tensor_tensor(k_(0, 0), whole(0, 0), whole(0, 1), ALU.mult)
                dve.tensor_copy(k_(1, 0), whole(1, 0))
                dve.tensor_copy(k_(2, 2), whole(2, 2))
                done(dve.tensor_copy(k_(3, 3), whole(3, 3)))
                dve.tensor_tensor(q_(3, 2), q_(3, 1), whole(3, 1), ALU.mult)
                done(dve.tensor_tensor(k_(3, 2), k_(3, 3), whole(3, 2), ALU.mult))
                dve.tensor_tensor(q_(3, 3), q_(3, 2), whole(3, 2), ALU.mult)
                done(dve.tensor_tensor(k_(3, 1), k_(3, 2), whole(3, 1), ALU.mult))
                done(dve.tensor_tensor(k_(3, 0), k_(3, 1), whole(3, 0), ALU.mult))
                dve.tensor_tensor(qs, qs, prod, ALU.mult)
                done(dve.tensor_tensor(ksig, ksig, inv, ALU.mult))

                def scaled(out, a, by):
                    return dve.tensor_tensor(out.rearrange("p (c t) -> p c t", t=SUB),
                                             a.rearrange("p (c t) -> p c t", t=SUB), wide(by, SUB), ALU.mult)

                scaled(qd, qs, own)
                scaled(kd, ksig, own)
                scaled(qx, qs, cq)
                scaled(kx, ksig, ck).then_inc(s["features"], 1)

            def post(n, i):
                t = n * BT + i
                dve.wait_ge(s["rr_out"], t + 1)
                dve.wait_ge(s["o_out"], t + 1)
                if t == 0:
                    dve.wait_ge(s["zeros_in"], 16)
                dve.scalar_tensor_tensor(og, o[:, i % 2, :], rr[:, i:i + 1], gw, ALU.mult,
                                         ALU.mult).then_inc(s["og_out"], 1)
                dve.wait_ge(s["sg_out"], t + 1)
                dve.tensor_tensor(gated, ps[:, i, :], sg[:, i % 2, :], ALU.mult).then_inc(s["go_empty"], 1)
                dve.wait_ge(s["go_empty"], t + 1)
                dve.sem_inc(s["sg_used"], 1)
                done(dve.tensor_tensor(og, og, gated, ALU.mult))
                x = rows[:, t, 0:D]
                done(dve.tensor_tensor(x, x, og, ALU.add))
                done(dve.bn_stats(stats2[:, i, :], x))
                ins = dve.bn_aggr(mv2[:, i, :], stats2[:, i, :])
                if i == BT - 1:
                    ins.then_inc(s["ln2_stats"], 1)

            dve.wait_ge(k.s_con, 16)
            dve.memset(og, 0.0).then_inc(s["zero_out"], 1)
            dve.memset(starts, 0.0)
            dve.memset(state[96:128, 0, :], 0.0).then_inc(s["state_out"], 1)
            ln_in(0)
            for n in range(NB):
                features(n)
                if n + 1 < NB:
                    ln_in(n + 1)
                ring.full(dve, ("AT", n))
                dve.tensor_tensor(att, bank(("AT", n)).rearrange("p (a b) -> p a b", b=P),
                                  c(k, "causal").unsqueeze(1).to_broadcast((P, BT, P)),
                                  ALU.mult).then_inc(s["att_out"], 1)
                dve.wait_ge(s["att_out"], n + 1)
                dve.sem_inc(ring.empty(("AT", n)), 1)
                ring.full(dve, ("KST", n))
                dve.tensor_copy(kst, bank(("KST", n))[:, 0:BT * DK].rearrange("p (a b) -> p a b", b=DK)
                                ).then_inc(s["kst_out"], 1)
                dve.wait_ge(s["kst_out"], n + 1)
                dve.sem_inc(ring.empty(("KST", n)), 1)
                if n == 0:
                    dve.wait_ge(s["gw_in"], 16)

                def step(i):
                    t = n * BT + i
                    ring.full(dve, ("U", n, i))
                    dve.scalar_tensor_tensor(state[96:128, (t + 1) % 2, :], state[96:128, t % 2, :],
                                             ck[96:128, 4 * i:4 * i + 1], bank(("U", n, i))[96:128, :],
                                             ALU.mult, ALU.add).then_inc(s["state_out"], 1)
                    dve.wait_ge(s["state_out"], t + 2)
                    dve.sem_inc(ring.empty(("U", n, i)), 1)

                step(0)
                step(1)
                step(2)
                post(n, 0)
                step(3)
                post(n, 1)
                post(n, 2)
                post(n, 3)
                dve.wait_ge(s["ln2_rstd"], n + 1)
                for i in range(BT):
                    t = n * BT + i
                    dve.tensor_scalar(rows[:, t, D:2 * D], rows[:, t, 0:D], mv2[:, i, 0:1], rstd2[:, i:i + 1],
                                      ALU.subtract, ALU.mult)


W_UP = KT * 2 * FI
W_ALL = W_UP + FM * D
FROWS = [P, P, FI - 2 * P]


def weights(a):
    return (a[:, 0:W_UP].rearrange("p (a b) -> p a b", b=2 * FI),
            a[:, W_UP:W_ALL].rearrange("p (a b) -> p a b", b=D))


def expert_memory(k):
    put = Place(k.arena, W_ALL, k.arena_size)
    k.w_expert = [put(W_ALL) for _ in range(2)]
    k.h_shared = [put(FM, BW) for _ in range(2)]
    k.silu_shared = [put(BW) for _ in range(2)]
    k.routing_at = put.at
    k.xe = [put(ST, D) for _ in range(2)]
    k.xet, k.he, k.silu_e = put(KT, CAP), put(FM, CAP), put(FM, CAP)
    k.ye = [put(ST, D) for _ in range(2)]
    tiny = Place(k.small, 0, SMALL)
    k.weight = [tiny(NT) for _ in range(2)]
    k.take, k.give = ([tiny(NT).bitcast(U32) for _ in range(2)] for _ in range(2))
    k.tiny_at = tiny.at


def route_and_shared(k):
    nc, io, ps, rows = k.nc, k.io, k.ps, k.rows
    xnt = k.xnt[:, :].rearrange("p (a b) -> p a b", b=T)
    up, down = weights(k.w_shared)
    put = Place(k.arena, k.routing_at, k.arena_size)
    logit_rows, gate_w, gate_b = put(T), put(KT, NE), put(NE)
    E_ = NT * NE
    x, ab, ex, u, d, z, ln, score, biased, eq, first, second, m, pos, tmp, tmp2 = (put(E_) for _ in range(16))
    tiny = Place(k.small, k.tiny_at, SMALL)
    best, which, total = tiny(NT), tiny(NT), tiny(NT)
    at, es, ok = tiny(NT), tiny(NT), tiny(NT)

    def te(a):
        return a.rearrange("p (t e) -> p t e", e=NE)

    turn_tasks = []
    for n in range(NB):
        turn_tasks += [("x2T", n, j) for j in range(KT)] + [("logits", n)]
    turn_tasks += [("logitsT",)]
    for n in range(NB):
        for m_ in range(FM):
            turn_tasks += [("g", n, m_), ("u", n, m_)]
    inner = Ring(k.sem, "inner", [4, 5, 6, 7], turn_tasks)
    outer_tasks = []
    for n in range(NB):
        outer_tasks += [("down", n, i) for i in range(BT)] + ([("before",)] if n == 0 else [])
    outer = Ring(k.sem, "outer", [0, 1, 2, 3], outer_tasks)
    s = sems(k, "route", """gate_in rows_out silu_out h_out abs_in exp_out ln_in ln_out root_in
             root_out chosen logits_out""")
    dve_done, act_done = k.chain["dve"], k.chain["act"]

    with nc.Block() as block:

        @block.sync
        def _(sp):
            sp.dma_start(gate_w, io["gate_w"]).then_inc(s["gate_in"], 16)
            sp.dma_start(gate_b, io["gate_b"].partition_broadcast(P)).then_inc(s["gate_in"], 16)
            for e in range(2):
                sp.dma_start(k.w_expert[e], io["w_expert"][e]).then_inc(k.w_in[e], 16)
            sp.wait_ge(k.given, 16 * 2 * NT)
            for e in range(2):
                sp.dma_start(k.xe[e], k.expert_in[e * CAP:(e + 1) * CAP, :].rearrange("(a p) d -> p a d", p=P)
                             ).then_inc(k.xe_in[e], 16)

        @block.tensor
        def _(pe):
            ident = c(k, "ident")
            pe.wait_ge(s["gate_in"], 32)

            def turn(n):
                for j in range(KT):
                    inner.free(pe, ("x2T", n, j))
                    b = ps[:, inner.bank(("x2T", n, j)), :]
                    for i in range(BT):
                        mm = pe.transpose(b[:, i * P:(i + 1) * P], rows[:, n * BT + i, D + j * P:D + (j + 1) * P],
                                          ident)
                    mm.then_inc(inner.filled, 1)

            def logits(n):
                inner.free(pe, ("logits", n))
                for j in range(KT):
                    pe.wait_ge(inner.empty(("x2T", n, j)), inner.at[("x2T", n, j)] // 4 + 1)
                    mm = pe.matmul(ps[0:NE, inner.bank(("logits", n)), :], gate_w[:, j, :],
                                   xnt[:, j, n * BW:(n + 1) * BW], start=(j == 0), stop=(j == KT - 1))
                mm.then_inc(inner.filled, 1)

            for n in range(NB):
                turn(n)
                logits(n)
            pe.wait_ge(s["logits_out"], NB)
            inner.free(pe, ("logitsT",))
            for t in range(NT):
                mm = pe.transpose(ps[:, inner.bank(("logitsT",)), t * NE:(t + 1) * NE],
                                  logit_rows[0:NE, t * P:(t + 1) * P], ident[0:NE, 0:NE])
            mm.then_inc(inner.filled, 1)
            pe.wait_ge(k.s_shared, 16)
            for n in range(NB):
                for m_ in range(FM):
                    if (n, m_) == (1, 1):
                        pe.wait_ge(s["chosen"], 1)
                        outer.free(pe, ("before",))
                        b = ps[:, outer.bank(("before",)), :]
                        pe.matmul(b[:, 0:E_], c(k, "before"), m, start=True, stop=True)
                        pe.matmul(b[:, E_:2 * E_], c(k, "ones"), m, start=True, stop=True).then_inc(outer.filled, 1)
                    for h, what in enumerate("gu"):
                        inner.free(pe, (what, n, m_))
                        for j in range(KT):
                            lo = h * FI + m_ * P
                            mm = pe.matmul(ps[0:FROWS[m_], inner.bank((what, n, m_)), :],
                                           up[:, j, lo:lo + FROWS[m_]], xnt[:, j, n * BW:(n + 1) * BW],
                                           start=(j == 0), stop=(j == KT - 1))
                        mm.then_inc(inner.filled, 1)
                for i in range(BT):
                    outer.free(pe, ("down", n, i))
                    for m_ in range(FM):
                        pe.wait_ge(s["h_out"], n * FM + m_ + 1)
                        mm = pe.matmul(ps[:, outer.bank(("down", n, i)), :],
                                       k.h_shared[n % 2][0:FROWS[m_], m_, i * P:(i + 1) * P],
                                       down[0:FROWS[m_], m_, :], start=(m_ == 0), stop=(m_ == FM - 1))
                    mm.then_inc(outer.filled, 1)

        @block.scalar
        def _(act):
            for n in range(NB):
                for j in range(KT):
                    inner.full(act, ("x2T", n, j))
                    act.activation(xnt[:, j, n * BW:(n + 1) * BW], ps[:, inner.bank(("x2T", n, j)), :],
                                   ACT.Copy).then_inc(inner.empty(("x2T", n, j)), 1)
                inner.full(act, ("logits", n))
                act.activation(logit_rows[0:NE, n * BW:(n + 1) * BW], ps[0:NE, inner.bank(("logits", n)), :],
                               ACT.Copy).then_inc(s["logits_out"], 1)
                act.wait_ge(s["logits_out"], n + 1)
                act.sem_inc(inner.empty(("logits", n)), 1)
            act.wait_ge(s["abs_in"], 1)
            act_done(act, act.activation(ab, x, ACT.Abs))
            act.activation(ex, ab, ACT.Exp, scale=-1.0).then_inc(s["exp_out"], 1)
            for n in range(NB):
                for m_ in range(FM):
                    q = n * FM + m_
                    if q == 1:
                        act.wait_ge(s["ln_in"], 1)
                        act.activation(ln, u, ACT.Ln).then_inc(s["ln_out"], 1)
                    if q == 2:
                        act.wait_ge(s["root_in"], 1)
                        act.activation(score, tmp, ACT.Sqrt).then_inc(s["root_out"], 1)
                    if q >= 2:
                        act.wait_ge(s["h_out"], q - 1)
                    inner.full(act, ("g", n, m_))
                    r = FROWS[m_]
                    act.activation(k.silu_shared[q % 2][0:r, :], ps[0:r, inner.bank(("g", n, m_)), :],
                                   ACT.Silu).then_inc(s["silu_out"], 1)
                    act.wait_ge(s["silu_out"], q + 1)
                    act.sem_inc(inner.empty(("g", n, m_)), 1)

        @block.gpsimd
        def _(pool):
            for slot in range(2):
                pool.wait_ge(s["rows_out"], slot + 1)
                for t in range(NT):
                    pool.indirect_dma_start(
                        out=k.expert_in[:, :],
                        out_offset=bass.IndirectOffsetOnAxis(ap=k.give[slot][:, t:t + 1], axis=0),
                        in_=rows[:, t, D:2 * D], in_offset=None, bounds_check=NE * CAP - 1,
                        oob_is_err=False).then_inc(k.given, 16)

        @block.vector
        def _(dve):
            def done(ins):
                dve_done(dve, ins)

            def per_token(a):
                return wide(a, NE)

            def per_expert(a):
                return a.unsqueeze(1).to_broadcast((P, NT, NE))

            def hidden(n, m_):
                q = n * FM + m_
                r = FROWS[m_]
                inner.full(dve, ("u", n, m_))
                dve.wait_ge(s["silu_out"], q + 1)
                dve.tensor_tensor(k.h_shared[n % 2][0:r, m_, :], ps[0:r, inner.bank(("u", n, m_)), :],
                                  k.silu_shared[q % 2][0:r, :], ALU.mult).then_inc(s["h_out"], 1)
                dve.wait_ge(s["h_out"], q + 1)
                dve.sem_inc(inner.empty(("u", n, m_)), 1)

            def add_shared(n, i):
                xr = rows[:, n * BT + i, 0:D]
                outer.full(dve, ("down", n, i))
                dve.tensor_tensor(xr, ps[:, outer.bank(("down", n, i)), :], xr,
                                  ALU.add).then_inc(outer.empty(("down", n, i)), 1)

            def choose(slot, onehot):
                done(dve.tensor_reduce(best, te(biased), AX.X, ALU.max))
                done(dve.tensor_tensor(te(eq), te(biased), per_token(best), ALU.is_equal))
                done(dve.tensor_tensor(te(eq), te(eq), per_expert(c(k, "rank")), ALU.mult))
                done(dve.tensor_reduce(which, te(eq), AX.X, ALU.max))
                done(dve.tensor_tensor(te(onehot), te(eq), per_token(which), ALU.is_equal))
                if slot == 0:
                    done(dve.scalar_tensor_tensor(biased, onehot, -3.0e38, biased, ALU.mult, ALU.add))
                done(dve.tensor_tensor(tmp, score, onehot, ALU.mult))
                done(dve.tensor_reduce(k.weight[slot], te(tmp), AX.X, ALU.add))

            def give(slot, onehot):
                done(dve.tensor_tensor(tmp, pos, onehot, ALU.mult))
                done(dve.tensor_reduce(at, te(tmp), AX.X, ALU.add))
                done(dve.tensor_tensor(te(tmp), te(onehot), per_expert(c(k, "expert")), ALU.mult))
                done(dve.tensor_reduce(es, te(tmp), AX.X, ALU.add))
                done(dve.tensor_scalar(ok, at, float(CAP), None, ALU.is_lt))
                done(dve.tensor_tensor(at, at, ok, ALU.mult))
                done(dve.tensor_tensor(k.weight[slot], k.weight[slot], ok, ALU.mult))
                done(dve.scalar_tensor_tensor(at, es, float(CAP), at, ALU.mult, ALU.add))
                done(dve.tensor_copy(k.take[slot], at))
                done(dve.tensor_scalar(ok, ok, -2.0 * NE * CAP, 2.0 * NE * CAP, ALU.mult, ALU.add))
                done(dve.tensor_tensor(at, at, ok, ALU.add))
                done(dve.tensor_copy(k.give[slot], at))
                dve.sem_inc(s["rows_out"], 1)

            inner.full(dve, ("logitsT",))
            dve.tensor_copy(x, ps[:, inner.bank(("logitsT",)), 0:E_]).then_inc(s["abs_in"], 1)
            dve.wait_ge(s["abs_in"], 1)
            dve.sem_inc(inner.empty(("logitsT",)), 1)
            dve.wait_ge(s["exp_out"], 1)
            dve.tensor_scalar(u, ex, 1.0, None, ALU.add).then_inc(s["ln_in"], 1)
            dve.wait_ge(s["ln_in"], 1)
            hidden(0, 0)
            done(dve.tensor_scalar(d, u, -1.0, None, ALU.add))
            done(dve.tensor_scalar(z, d, 0.0, None, ALU.is_equal))
            done(dve.tensor_tensor(d, d, z, ALU.add))
            done(dve.reciprocal(tmp2, d))
            done(dve.tensor_tensor(tmp2, tmp2, ex, ALU.mult))
            done(dve.tensor_tensor(z, z, ex, ALU.mult))
            dve.wait_ge(s["ln_out"], 1)
            done(dve.tensor_tensor(tmp2, tmp2, ln, ALU.mult))
            done(dve.tensor_tensor(tmp2, tmp2, z, ALU.add))
            dve.scalar_tensor_tensor(tmp, x, 0.0, tmp2, ALU.max, ALU.add).then_inc(s["root_in"], 1)
            dve.wait_ge(s["root_in"], 1)
            hidden(0, 1)
            dve.wait_ge(s["root_out"], 1)
            done(dve.tensor_scalar(tmp2, score, 1e-30, None, ALU.max))
            done(dve.reciprocal(tmp2, tmp2))
            done(dve.tensor_tensor(tmp, tmp, tmp2, ALU.mult))
            done(dve.tensor_tensor(tmp, tmp, score, ALU.add))
            done(dve.tensor_scalar(score, tmp, 0.5, None, ALU.mult))
            dve.wait_ge(s["gate_in"], 32)
            done(dve.tensor_tensor(te(biased), te(score), per_expert(gate_b), ALU.add))
            hidden(0, 2)
            choose(0, first)
            for i in range(BT):
                add_shared(0, i)
            hidden(1, 0)
            choose(1, second)
            dve.tensor_tensor(m, first, second, ALU.add).then_inc(s["chosen"], 1)
            done(dve.tensor_tensor(total, k.weight[0], k.weight[1], ALU.add))
            done(dve.reciprocal(total, total))
            for slot in range(2):
                done(dve.tensor_tensor(k.weight[slot], k.weight[slot], total, ALU.mult))
            hidden(1, 1)
            outer.full(dve, ("before",))
            b = ps[:, outer.bank(("before",)), :]
            within, whole = b[:, 0:E_], b[:, E_:2 * E_]
            done(dve.tensor_copy(tmp.rearrange("p (e t) -> p t e", t=NT), te(whole)))
            done(dve.tensor_tensor_scan(tmp2, c(k, "restart"), tmp, 0.0, ALU.mult, ALU.add))
            done(dve.tensor_tensor(tmp2, tmp2, tmp, ALU.subtract))
            dve.tensor_tensor(te(pos), te(within), tmp2.rearrange("p (e t) -> p t e", t=NT),
                              ALU.add).then_inc(outer.empty(("before",)), 1)
            dve.wait_ge(outer.empty(("before",)), outer.at[("before",)] // 4 + 1)
            give(0, first)
            hidden(1, 2)
            give(1, second)
            for i in range(BT):
                add_shared(1, i)
            for n in range(2, NB):
                for m_ in range(FM):
                    hidden(n, m_)
                for i in range(BT):
                    add_shared(n, i)


def experts(k):
    nc, io, ps = k.nc, k.io, k.ps
    s = sems(k, "expert", "turned xt_out gu_full silu_out h_out down_full y_used")
    y_stored = k.y_stored
    turn_bank, up_bank, down_bank = (4, 5), (6, 7, 0), (1, 2)
    pairs = NE // 2

    def each_pair(eng, body):
        with eng.Fori(0, pairs - 1) as it:
            body(it, 0, False)
            body(it, 1, False)
        body(pairs - 1, 0, False)
        body(pairs - 1, 1, True)

    with nc.Block() as block:

        @block.sync
        def _(sp):
            sp.dma_start(k.xnt[:, :], io["w_attention"]).then_inc(k.attention_in, 16)
            with sp.Fori(0, pairs - 1) as it:
                for p in range(2):
                    e = it * 2 + (p + 2)
                    sp.wait_ge(s["turned"], it * 4 + 2 * (p + 1))
                    sp.dma_start(k.xe[p], k.expert_in.rearrange("(e a p) d -> e p a d", p=P, a=ST)[e]
                                 ).then_inc(k.xe_in[p], 16)
                    sp.wait_ge(s["down_full"], it * 4 + 2 * (p + 1))
                    sp.dma_start(k.w_expert[p], io["w_expert"][e]).then_inc(k.w_in[p], 16)

        @block.tensor
        def _(pe):
            ident = c(k, "ident")

            def turn(p):
                for a in range(ST):
                    for j in range(KT):
                        mm = pe.transpose(ps[:, turn_bank[a], j * P:(j + 1) * P],
                                          k.xe[p][:, a, j * P:(j + 1) * P], ident)
                    mm.then_inc(s["turned"], 1)

            def body(it, p, last):
                up, down = weights(k.w_expert[p])
                pe.wait_ge(k.w_in[p], it * 16 + 16)
                pe.wait_ge(s["xt_out"], it * 4 + 2 * (p + 1))
                for m in range(FM):
                    for h in range(2):
                        for j in range(KT):
                            lo = h * FI + m * P
                            mm = pe.matmul(ps[0:FROWS[m], up_bank[m], h * CAP:(h + 1) * CAP],
                                           up[:, j, lo:lo + FROWS[m]], k.xet[:, j, :],
                                           start=(j == 0), stop=(j == KT - 1))
                    mm.then_inc(s["gu_full"], 1)
                if not last:
                    pe.wait_ge(k.xe_in[1 - p], it * 16 + (16 if p == 0 else 32))
                    turn(1 - p)
                for a in range(ST):
                    pe.wait_ge(s["y_used"], it * 4 + 2 * p + a + 1)
                    for m in range(FM):
                        if a == 0:
                            pe.wait_ge(s["h_out"], it * 6 + 3 * p + m + 1)
                        mm = pe.matmul(ps[:, down_bank[a], :], k.he[0:FROWS[m], m, a * P:(a + 1) * P],
                                       down[0:FROWS[m], m, :], start=(m == 0), stop=(m == FM - 1))
                    mm.then_inc(s["down_full"], 1)

            pe.wait_ge(k.xe_in[0], 16)
            turn(0)
            each_pair(pe, body)

        @block.scalar
        def _(act):
            act.sem_inc(s["y_used"], ST)
            for p in range(2):
                act.sem_inc(y_stored[p], 16)

            def xt(count, a):
                act.wait_ge(s["turned"], count)
                act.activation(k.xet[:, :, a * P:(a + 1) * P],
                               ps[:, turn_bank[a], :].rearrange("p (a b) -> p a b", b=P),
                               ACT.Copy).then_inc(s["xt_out"], 1)

            def body(it, p, last):
                for m in range(FM):
                    act.wait_ge(s["gu_full"], it * 6 + 3 * p + m + 1)
                    r = FROWS[m]
                    act.activation(k.silu_e[0:r, m, :], ps[0:r, up_bank[m], 0:CAP],
                                   ACT.Silu).then_inc(s["silu_out"], 1)
                if not last:
                    for a in range(ST):
                        xt(it * 4 + 2 * (p + 1) + a + 1, a)
                act.wait_ge(y_stored[p], it * 16 + 16)
                for a in range(ST):
                    act.wait_ge(s["down_full"], it * 4 + 2 * p + a + 1)
                    act.activation(k.ye[p][:, a, :], ps[:, down_bank[a], :], ACT.Copy).then_inc(s["y_used"], 1)
                act.wait_ge(s["y_used"], it * 4 + 2 * p + 2 * ST)
                e = it * 2 + p
                act.dma_start(k.expert_out.rearrange("(e a p) d -> e p a d", p=P, a=ST)[e], k.ye[p]
                              ).then_inc(y_stored[p], 16)

            for a in range(ST):
                xt(a + 1, a)
            each_pair(act, body)

        @block.vector
        def _(dve):
            def body(it, p, last):
                for m in range(FM):
                    r = FROWS[m]
                    dve.wait_ge(s["silu_out"], it * 6 + 3 * p + m + 1)
                    dve.tensor_tensor(k.he[0:r, m, :], ps[0:r, up_bank[m], CAP:2 * CAP], k.silu_e[0:r, m, :],
                                      ALU.mult).then_inc(s["h_out"], 1)

            each_pair(dve, body)


def attention_memory(k):
    k.w_attn = [k.xnt[:, i * KT * D:(i + 1) * KT * D].rearrange("p (a b) -> p a b", b=D) for i in range(4)]
    put = Place(k.arena, 0, k.arena_size)
    k.qt, k.vk, k.ksum = put(KT, T), put(KT, P), put(KT, P)
    k.attention_at = put.at


def linear_attention_sums(k):
    nc, io, ps, rows = k.nc, k.io, k.ps, k.rows
    attention_memory(k)
    w_q, w_k, w_v, _ = k.w_attn
    put = Place(k.arena, k.attention_at, k.arena_size)
    taken = [put(D) for _ in range(8)]
    xnt = [put(KT, BW) for _ in range(2)]
    k_biased, kt, vt = put(D), put(2, D), put(2, D)
    b_k, b_v, b_o, decay_row = put(D), put(D), put(D), put(T)
    tiny = Place(k.small, k.tiny_at, SMALL)
    stats, mv, rstd, ve, b_q = tiny(BT, 6), tiny(BT, 2), tiny(BT), tiny(BT), tiny(KT)

    tasks = []
    for n in range(NB):
        tasks += [("xT", n, j) for j in range(KT)] + [("Q", n, m) for m in range(KT)]
        for i in range(BT):
            tasks += [("K", n, i), ("V", n, i)]
    ring = Ring(k.sem, "sums", [2, 3, 4, 5, 6, 7], tasks)
    s = sems(k, "sums", """biases_in taken_used ln_stats ln_rstd ln_out kb_out k_out v_out kv_used q_out
             kv_full zeroed""")
    taken_in = [k.sem(f"taken_in{i}") for i in range(8)]
    dve_done, pool_done = k.chain["dve"], k.chain["pool"]

    def bank(task):
        return ps[:, ring.bank(task), :]

    with nc.Block() as block:

        @block.sync
        def _(sp):
            for p in range(2):
                sp.wait_ge(k.y_stored[p], 16 * (NE // 2 + 1))
            for to, what in ((b_k, "b_k"), (b_v, "b_v"), (b_o, "b_o"), (decay_row, "decay_row")):
                sp.dma_start(to, io[what].partition_broadcast(P)).then_inc(s["biases_in"], 16)
            sp.dma_start(b_q, io["b_q"]).then_inc(s["biases_in"], 16)

        @block.gpsimd
        def _(pool):
            pool.memset(k.vk, 0.0).then_inc(s["zeroed"], 1)
            pool.memset(k.ksum, 0.0).then_inc(s["zeroed"], 1)
            for p in range(2):
                pool.wait_ge(k.y_stored[p], 16 * (NE // 2 + 1))

            def take(n):
                for i in range(BT):
                    for slot in range(2):
                        q = (n * BT + i) * 2 + slot
                        if q >= 8:
                            pool.wait_ge(s["taken_used"], q - 7)
                        pool.indirect_dma_start(
                            out=taken[q % 8], out_offset=None, in_=k.expert_out[:, :],
                            in_offset=bass.IndirectOffsetOnAxis(
                                ap=k.take[slot][:, n * BT + i:n * BT + i + 1], axis=0),
                            bounds_check=NE * CAP - 1, oob_is_err=False).then_inc(taken_in[q % 8], 16)

            take(0)
            for n in range(NB):
                pool.wait_ge(s["ln_stats"], n + 1)
                pool_done(pool, pool.tensor_scalar(ve, mv[:, :, 1], 1.0, 1e-5, ALU.mult, ALU.add))
                pool.tensor_tensor(rstd, ve, c(k, "neghalf")[:, 0:BT], ALU.pow).then_inc(s["ln_rstd"], 1)
                if n == 0:
                    pool.wait_ge(s["biases_in"], 16 * 5)
                if n + 1 < NB:
                    take(n + 1)
                pool.wait_ge(s["ln_out"], n + 1)
                for i in range(BT):
                    x = rows[:, n * BT + i, 0:D]
                    pool.tensor_tensor(x, x, b_o, ALU.add)
                for m in range(KT):
                    pool.wait_ge(s["q_out"], n * KT + m + 1)
                    q = k.qt[:, m, n * BW:(n + 1) * BW]
                    pool.tensor_tensor(q, q, decay_row[:, n * BW:(n + 1) * BW], ALU.mult)

        @block.scalar
        def _(act):
            act.wait_ge(s["biases_in"], 16 * 5)
            for n in range(NB):
                for j in range(KT):
                    ring.full(act, ("xT", n, j))
                    act.activation(xnt[n % 2][:, j, :], bank(("xT", n, j)),
                                   ACT.Copy).then_inc(ring.empty(("xT", n, j)), 1)
                for m in range(KT):
                    ring.full(act, ("Q", n, m))
                    act.activation(k.qt[:, m, n * BW:(n + 1) * BW], bank(("Q", n, m)), ACT.Relu,
                                   bias=b_q[:, m:m + 1]).then_inc(s["q_out"], 1)
                    act.wait_ge(s["q_out"], n * KT + m + 1)
                    act.sem_inc(ring.empty(("Q", n, m)), 1)
                for i in range(BT):
                    t = n * BT + i
                    act.wait_ge(s["kb_out"], t + 1)
                    if t >= 2:
                        act.wait_ge(s["kv_used"], t - 1)
                    act.activation(kt[:, t % 2, :], k_biased, ACT.Relu,
                                   scale=c(k, "decay")[:, t:t + 1]).then_inc(s["k_out"], 1)

        @block.tensor
        def _(pe):
            ident = c(k, "ident")

            def add_tile(t):
                pe.wait_ge(s["k_out"], t + 1)
                pe.wait_ge(s["v_out"], t + 1)
                for m in range(KT):
                    r = slice(m * P, (m + 1) * P)
                    pe.matmul(ps[:, 0, r], vt[:, t % 2, r], kt[:, t % 2, r], start=(t == 0 and m == 0),
                              stop=(t == NT - 1), skip_group_check=True)
                for m in range(KT):
                    mm = pe.matmul(ps[:, 1, m * DK:(m + 1) * DK], kt[:, t % 2, m * P:(m + 1) * P],
                                   c(k, "ones")[:, 0:DK], start=(t == 0 and m == 0), stop=(t == NT - 1),
                                   skip_group_check=True)
                mm.then_inc(s["kv_used"], 1)

            pe.wait_ge(k.attention_in, 16)
            for n in range(NB):
                pe.wait_ge(s["ln_out"], n + 1)
                for j in range(KT):
                    ring.free(pe, ("xT", n, j))
                    for i in range(BT):
                        mm = pe.transpose(bank(("xT", n, j))[:, i * P:(i + 1) * P],
                                          rows[:, n * BT + i, D + j * P:D + (j + 1) * P], ident)
                    mm.then_inc(ring.filled, 1)
                if n:
                    add_tile(n * BT - 1)
                for m in range(KT):
                    ring.free(pe, ("Q", n, m))
                    for j in range(KT):
                        if m == 0:
                            pe.wait_ge(ring.empty(("xT", n, j)), ring.at[("xT", n, j)] // 6 + 1)
                        mm = pe.matmul(bank(("Q", n, m)), w_q[:, j, m * P:(m + 1) * P], xnt[n % 2][:, j, :],
                                       start=(j == 0), stop=(j == KT - 1))
                    mm.then_inc(ring.filled, 1)
                for i in range(BT):
                    for what, w in (("K", w_k), ("V", w_v)):
                        ring.free(pe, (what, n, i))
                        for j in range(KT):
                            mm = pe.matmul(bank((what, n, i)), xnt[n % 2][:, j, i * P:(i + 1) * P], w[:, j, :],
                                           start=(j == 0), stop=(j == KT - 1))
                        mm.then_inc(ring.filled, 1)
                    if i:
                        add_tile(n * BT + i - 1)
            add_tile(NT - 1)

        @block.vector
        def _(dve):
            def done(ins):
                dve_done(dve, ins)

            def combine_and_norm(n):
                for i in range(BT):
                    t = n * BT + i
                    x = rows[:, t, 0:D]
                    for slot in range(2):
                        q = 2 * t + slot
                        dve.wait_ge(taken_in[q % 8], 16 * (q // 8 + 1))
                        dve.scalar_tensor_tensor(x, taken[q % 8], k.weight[slot][:, t:t + 1], x, ALU.mult,
                                                 ALU.add).then_inc(s["taken_used"], 1)
                        dve.wait_ge(s["taken_used"], q + 1)
                    done(dve.bn_stats(stats[:, i, :], x))
                    ins = dve.bn_aggr(mv[:, i, :], stats[:, i, :])
                ins.then_inc(s["ln_stats"], 1)
                dve.wait_ge(s["ln_rstd"], n + 1)
                for i in range(BT):
                    t = n * BT + i
                    ins = dve.tensor_scalar(rows[:, t, D:2 * D], rows[:, t, 0:D], mv[:, i, 0:1],
                                            rstd[:, i:i + 1], ALU.subtract, ALU.mult)
                ins.then_inc(s["ln_out"], 1)

            combine_and_norm(0)
            dve.wait_ge(s["biases_in"], 16 * 5)
            for n in range(NB):
                if n + 1 < NB:
                    combine_and_norm(n + 1)
                for i in range(BT):
                    t = n * BT + i
                    ring.full(dve, ("K", n, i))
                    if t:
                        dve.wait_ge(s["k_out"], t)
                    dve.tensor_tensor(k_biased, bank(("K", n, i)), b_k, ALU.add).then_inc(s["kb_out"], 1)
                    dve.wait_ge(s["kb_out"], t + 1)
                    dve.sem_inc(ring.empty(("K", n, i)), 1)
                    ring.full(dve, ("V", n, i))
                    if t >= 2:
                        dve.wait_ge(s["kv_used"], t - 1)
                    dve.tensor_tensor(vt[:, t % 2, :], bank(("V", n, i)), b_v, ALU.add).then_inc(s["v_out"], 1)
                    dve.wait_ge(s["v_out"], t + 1)
                    dve.sem_inc(ring.empty(("V", n, i)), 1)
            dve.wait_ge(s["kv_used"], NT)
            dve.wait_ge(s["zeroed"], 2)
            vk = ps[:, 0, :].rearrange("p (a b) -> p a b", b=P)
            ksum = ps[:, 1, 0:KT * DK].rearrange("p (a b) -> p a b", b=DK)
            for g in range(4):
                r = slice(g * DK, (g + 1) * DK)
                dve.tensor_copy(k.vk[r, :, r], vk[r, :, r])
                dve.tensor_copy(k.ksum[r, :, r], ksum[r, :, :])


def linear_attention(k):
    nc, io, ps, rows = k.nc, k.io, k.ps, k.rows
    w_o = k.w_attn[3]
    put = Place(k.arena, k.attention_at, k.arena_size)
    out_t = [put(KT, BW) for _ in range(2)]
    free = Place(k.xnt, 0, 3 * KT * D)
    den = [free(KT, BW), free(KT, BW)]
    guess, product, inv = [free(KT, BW), put(KT, BW)], put(2, BW), put(2, BW)
    kvo, router, junk, diagonal, base = put(KT, D), put(D), put(D), put(BT, P), put(2, D)
    onehot = [put(SEL // 2).bitcast(BF16) for _ in range(4)]
    number = put(NT).bitcast(BF16).rearrange("p (a b) -> p a b", b=2)
    compared = [put(BW // 2).bitcast(BF16) for _ in range(8)]
    tiny = Place(k.small, 0, k.token_at)
    stats, mv, rstd, ve, shift = tiny(BT, 6), tiny(BT, 2), tiny(BT), tiny(BT), tiny(BT)
    chosen, total, place, past = tiny(NT), tiny(NT), tiny(NT), tiny(NT)
    found = tiny(ST)
    PARTS = NB + 1
    one, tied = put(1).bitcast(BF16)[:, 0:1], put(P)

    def comparisons(n):
        return ([(u, n * BW, (n + 1) * BW, False) for u in range(n * BT)] +
                [(u, u * P, (n + 1) * BW, True) for u in range(n * BT, (n + 1) * BT - 1)])

    def compared_before(n):
        return sum(len(comparisons(i)) for i in range(n))

    higher = tiny(NT, PARTS)
    ahead = tiny(NT)
    tasks = []
    tasks += [("den", n, m) for n in range(2) for m in range(KT)] + [("kvo", m) for m in range(KT)]
    for n in range(NB):
        for i in range(BT):
            tasks += [("out", n, i)] + ([("den", n + 2, i)] if n + 2 < NB else [])
    ring = Ring(k.sem, "attention", [5, 6, 7], tasks)
    s = sems(k, "attention", """router_in den_out ln_out guess_out product_out inverse_out out_t kvo_out ln_stats
             ln_rstd shift_out norm_out score_out diagonal_out broadcast chosen placed place_out onehot_out found
             number_out base_out compared counted count_in""")
    k.rows_stored = k.sem("rows_stored")
    dve_done, act_done, pool_done = k.chain["dve"], k.chain["act"], k.chain["pool"]

    def bank(task):
        return ps[:, ring.bank(task), :]

    with nc.Block() as block:

        @block.sync
        def _(sp):
            sp.dma_start(router, io["w_router"].partition_broadcast(P)).then_inc(s["router_in"], 16)
            for n in range(NB):
                sp.wait_ge(s["score_out"], (n + 1) * BT)
                sp.dma_start(k.kept.rearrange("(t p) d -> p t d", p=P)[:, n * BT:(n + 1) * BT, :],
                             rows[:, n * BT:(n + 1) * BT, :]).then_inc(k.rows_stored, 16)
                for i in range(BT):
                    t = n * BT + i
                    sp.wait_ge(s["base_out"], t + 1)
                    sp.dma_start(io["out"][t * P:(t + 1) * P, :], base[:, t % 2, :]).then_inc(k.base_in[t % 2], 16)
            for i in range(2):
                sp.wait_ge(k.base_in[i], 16 * (NT // 2))

        @block.gpsimd
        def _(pool):
            pool.tensor_copy(number, c(k, "number").rearrange("p (a b) -> p a b", b=2)).then_inc(s["number_out"], 1)

            def bases(n):
                for i in range(BT):
                    t = n * BT + i
                    pool.wait_ge(s["norm_out"], t + 1)
                    if t >= 2:
                        pool.wait_ge(k.base_in[t % 2], 16 * (t // 2))
                    pool.tensor_tensor(base[:, t % 2, :], rows[:, t, 0:D], rows[:, t, D:2 * D],
                                       ALU.add).then_inc(s["base_out"], 1)

            def product_of(n, m):
                q = n * KT + m
                pool.wait_ge(s["guess_out"], q + 1)
                if q >= 2:
                    pool.wait_ge(s["inverse_out"], q - 1)
                pool.tensor_tensor(product[:, q % 2, :], den[n % 2][:, m, :], guess[n % 2][:, m, :],
                                   ALU.mult).then_inc(s["product_out"], 1)

            def quotient(n, m):
                pool.wait_ge(s["inverse_out"], n * KT + m + 1)
                if n >= 2:
                    ring.full(pool, ("out", n - 2, BT - 1))
                pool.tensor_tensor(out_t[n % 2][:, m, :], inv[:, m % 2, :], k.qt[:, m, n * BW:(n + 1) * BW],
                                   ALU.mult).then_inc(s["out_t"], 1)

            for n in range(NB + 1):
                if n < NB:
                    product_of(n, 0)
                    for m in range(1, KT):
                        product_of(n, m)
                        quotient(n, m - 1)
                    quotient(n, KT - 1)
                if n:
                    pool.wait_ge(s["ln_stats"], n)
                    pool_done(pool, pool.tensor_scalar(ve, mv[:, :, 1], 1.0, 1e-5, ALU.mult, ALU.add))
                    pool.tensor_tensor(rstd, ve, c(k, "neghalf")[:, 0:BT], ALU.pow).then_inc(s["ln_rstd"], 1)
                if n >= 2:
                    bases(n - 2)
            bases(NB - 1)

        @block.scalar
        def _(act):
            def norm(n):
                act.wait_ge(s["shift_out"], n + 1)
                for i in range(BT):
                    t = n * BT + i
                    act.activation(rows[:, t, D:2 * D], rows[:, t, 0:D], ACT.Identity, bias=shift[:, i:i + 1],
                                   scale=rstd[:, i:i + 1]).then_inc(s["norm_out"], 1)

            def diagonals(n):
                for i in range(BT):
                    t = n * BT + i
                    act.wait_ge(s["score_out"], t + 1)
                    if n:
                        act.wait_ge(s["broadcast"], t - BT + 1)
                    act.activation(diagonal[:, i, :], c(k, "ident"), ACT.Copy,
                                   scale=rows[:, t, 2 * D:2 * D + 1]).then_inc(s["diagonal_out"], 1)

            def guesses(n):
                for m in range(KT):
                    q = n * KT + m
                    if n >= 2:
                        act.wait_ge(s["product_out"], q - 2 * KT + 1)
                        act.wait_ge(s["inverse_out"], q - 2 * KT + 1)
                    ring.full(act, ("den", n, m))
                    act.activation(den[n % 2][:, m, :], bank(("den", n, m)), ACT.Copy,
                                   bias=1e-6).then_inc(s["den_out"], 1)
                    act.wait_ge(s["den_out"], q + 1)
                    act.sem_inc(ring.empty(("den", n, m)), 1)
                    act.activation(guess[n % 2][:, m, :], den[n % 2][:, m, :], ACT.Ln).then_inc(s["ln_out"], 1)
                for m in range(KT):
                    act.wait_ge(s["ln_out"], n * KT + m + 1)
                    act.activation(guess[n % 2][:, m, :], guess[n % 2][:, m, :], ACT.Exp,
                                   scale=-1.0).then_inc(s["guess_out"], 1)

            guesses(0)
            guesses(1)
            for m in range(KT):
                ring.full(act, ("kvo", m))
                act.activation(kvo[:, m, :], bank(("kvo", m)), ACT.Copy, scale=-1.0).then_inc(s["kvo_out"], 1)
                act.wait_ge(s["kvo_out"], m + 1)
                act.sem_inc(ring.empty(("kvo", m)), 1)
            for n in range(NB):
                if n + 2 < NB:
                    guesses(n + 2)
                norm(n)
                diagonals(n)

        @block.tensor
        def _(pe):
            def spread(n):
                for i in range(BT):
                    t = n * BT + i
                    pe.wait_ge(s["diagonal_out"], t + 1)
                    pe.matmul(ps[:, n, i * P:(i + 1) * P], c(k, "ones"), diagonal[:, i, :], start=True,
                              stop=True).then_inc(s["broadcast"], 1)

            def count(n):
                for j, (u, start, end, own) in enumerate(comparisons(n)):
                    pe.wait_ge(s["compared"], compared_before(n) + j + 1)
                    for t in range(start // P + own, end // P):
                        at = t * P - start
                        mm = pe.matmul(ps[:, 4, t:t + 1], compared[(compared_before(n) + j) % 8][:, at:at + P], one,
                                       start=(n == 0 and u == 0 and t == 1), stop=(u == t - 1), skip_group_check=True)
                    mm.then_inc(s["counted"], 1)

            def denominator(n, m):
                ring.free(pe, ("den", n, m))
                pe.matmul(bank(("den", n, m)), k.ksum[:, m, :], k.qt[:, m, n * BW:(n + 1) * BW],
                          start=True, stop=True).then_inc(ring.filled, 1)

            for n in range(2):
                for m in range(KT):
                    denominator(n, m)
            for m in range(KT):
                ring.free(pe, ("kvo", m))
                pe.matmul(bank(("kvo", m)), k.vk[:, m, :], w_o[:, m, :], start=True,
                          stop=True).then_inc(ring.filled, 1)
            pe.wait_ge(s["kvo_out"], KT)
            for n in range(NB):
                for i in range(BT):
                    ring.free(pe, ("out", n, i))
                    for m in range(KT):
                        if i == 0:
                            pe.wait_ge(s["out_t"], n * KT + m + 1)
                        mm = pe.matmul(bank(("out", n, i)), out_t[n % 2][:, m, i * P:(i + 1) * P],
                                       kvo[:, m, :], start=(m == 0), stop=(m == KT - 1))
                    mm.then_inc(ring.filled, 1)
                    if n + 2 < NB:
                        denominator(n + 2, i)
                if n >= 1:
                    spread(n - 1)
                if n >= 2:
                    count(n - 2)
            spread(NB - 1)
            count(NB - 2)
            count(NB - 1)
            ring.all_drained(pe)
            pe.wait_ge(s["chosen"], 1)
            pe.matmul(ps[:, 5, 0:NT], c(k, "before"), chosen, start=True, stop=True)
            pe.matmul(ps[:, 5, NT:2 * NT], c(k, "ones"), chosen, start=True, stop=True).then_inc(s["placed"], 1)
            pe.wait_ge(s["number_out"], 1)
            for t in range(NT):
                pe.wait_ge(s["onehot_out"], t + 1)
                for a in range(ST):
                    mm = pe.matmul(ps[:, 6 + a, 0:2], onehot[t % 4][:, a * P:(a + 1) * P], number[:, t, :],
                                   start=(t == 0), stop=(t == NT - 1))
                mm.then_inc(s["found"], 1)

        @block.vector
        def _(dve):
            def done(ins):
                dve_done(dve, ins)

            def residual(n, i):
                t = n * BT + i
                x = rows[:, t, 0:D]
                ring.full(dve, ("out", n, i))
                dve.tensor_tensor(x, bank(("out", n, i)), x, ALU.add).then_inc(ring.empty(("out", n, i)), 1)
                dve.wait_ge(ring.empty(("out", n, i)), ring.at[("out", n, i)] // 3 + 1)
                done(dve.bn_stats(stats[:, i, :], x))
                ins = dve.bn_aggr(mv[:, i, :], stats[:, i, :])
                if i == BT - 1:
                    ins.then_inc(s["ln_stats"], 1)

            def inverse(n, m):
                q = n * KT + m
                dve.wait_ge(s["product_out"], q + 1)
                if q >= 2:
                    dve.wait_ge(s["out_t"], q - 1)
                dve.scalar_tensor_tensor(inv[:, q % 2, :], product[:, q % 2, :], -2.0, guess[n % 2][:, m, :],
                                         ALU.add, ALU.mult).then_inc(s["inverse_out"], 1)

            def shifts(n):
                dve.wait_ge(s["ln_rstd"], n + 1)
                dve.scalar_tensor_tensor(shift, mv[:, :, 0], -1.0, rstd, ALU.mult,
                                         ALU.mult).then_inc(s["shift_out"], 1)

            def score(n):
                if n == 0:
                    dve.wait_ge(s["router_in"], 16)
                for i in range(BT):
                    t = n * BT + i
                    dve.wait_ge(s["norm_out"], t + 1)
                    if t:
                        dve.wait_ge(s["score_out"], t)
                    dve.tensor_tensor_reduce(junk, rows[:, t, D:2 * D], router, 1.0, 0.0, ALU.mult, ALU.add,
                                             rows[:, t, 2 * D:2 * D + 1]).then_inc(s["score_out"], 1)

            def compare(n):
                dve.wait_ge(s["broadcast"], (n + 1) * BT)
                for j, (u, start, end, own) in enumerate(comparisons(n)):
                    q = compared_before(n) + j
                    if q >= 8:
                        dve.wait_ge(s["counted"], q - 7)
                        dve.wait_ge(s["compared"], q - 7)
                    mine = rows[:, u, 2 * D:2 * D + 1]
                    if own:
                        ties(u)
                    part = 1 + n - u // BT
                    dve.tensor_scalar(compared[q % 8][:, 0:end - start], spread_scores[:, start:end], mine, 0.0,
                                      ALU.is_gt, ALU.add, accum_out=higher[:, u, part:part + 1]
                                      ).then_inc(s["compared"], 1)
                u = (n + 1) * BT - 1
                ties(u)
                done(dve.tensor_scalar(tied, spread_scores[:, u * P:(u + 1) * P], rows[:, u, 2 * D:2 * D + 1], 0.0,
                                       ALU.is_gt, ALU.add, accum_out=higher[:, u, 1:2]))

            def ties(u):
                done(dve.scalar_tensor_tensor(tied, spread_scores[:, u * P:(u + 1) * P],
                                              rows[:, u, 2 * D:2 * D + 1], c(k, "earlier"), ALU.is_equal,
                                              ALU.mult, accum_out=higher[:, u, 0:1]))

            spread_scores = ps.rearrange("p a b -> p (a b)")[:, 0:T]
            done(dve.memset(higher, 0.0))
            done(dve.memset(one, 1.0))
            for n in range(NB + 1):
                for i in range(BT):
                    if n:
                        residual(n - 1, i)
                    if n < NB:
                        inverse(n, i)
                if n:
                    shifts(n - 1)
                    score(n - 1)
                if n >= 2:
                    compare(n - 2)
            compare(NB - 1)
            dve.wait_ge(s["compared"], compared_before(NB))
            done(dve.tensor_reduce(ahead, higher, AX.X, ALU.add))
            dve.wait_ge(s["counted"], compared_before(NB))
            done(dve.tensor_tensor(ahead[:, 1:NT], ahead[:, 1:NT], ps[:, 4, 1:NT], ALU.subtract))
            done(dve.scalar_tensor_tensor(ahead, c(k, "number")[:, 1:2 * NT:2], 1.0 * P, ahead, ALU.mult, ALU.add))
            dve.tensor_scalar(chosen, ahead, float(SEL), None, ALU.is_lt).then_inc(s["chosen"], 1)
            dve.wait_ge(s["chosen"], 1)
            done(dve.tensor_scalar(past, chosen, -1.0 * T, 1.0 * T, ALU.mult, ALU.add))
            dve.wait_ge(s["placed"], 1)
            done(dve.tensor_copy(total, ps[:, 5, NT:2 * NT]))
            done(dve.tensor_tensor_scan(place, c(k, "ones")[:, 0:NT], total, 0.0, ALU.mult, ALU.add))
            done(dve.tensor_tensor(place, place, total, ALU.subtract))
            done(dve.tensor_tensor(place, ps[:, 5, 0:NT], place, ALU.add))
            done(dve.tensor_tensor(place, place, past, ALU.add))
            for t in range(NT):
                if t >= 4:
                    dve.wait_ge(s["found"], t - 3)
                dve.tensor_scalar(onehot[t % 4], c(k, "slot"), place[:, t:t + 1], None,
                                  ALU.is_equal).then_inc(s["onehot_out"], 1)
            dve.wait_ge(s["found"], NT)
            for a in range(ST):
                ins = dve.tensor_copy(found[:, a:a + 1], ps[:, 6 + a, 0:1])
            done(ins)
            for a in range(ST):
                ins = dve.scalar_tensor_tensor(found[:, a:a + 1], ps[:, 6 + a, 1:2], float(P), found[:, a:a + 1],
                                               ALU.mult, ALU.add)
            done(ins)
            done(dve.tensor_copy(k.token, found))


def plan_stream():
    order = [("k", i) for i in range(4)] + [("v", i) for i in range(4)]
    for step in range(NHK + 3):
        if step < NHK:
            order.append(("q", step))
        if step >= 3:
            order.append(("wo", step - 3))
    for step in range(NHK + 1):
        if step < NHK:
            order += [("gate", step), ("up", step)]
        if step:
            order.append(("down", step - 1))
    return order


CHUNKS = plan_stream()
CH = 1024
SLOTS = 8


def hidden_of(sel, j):
    return sel[:, j, D:2 * D]


def residual_of(sel, j):
    return sel[:, j, 0:D]


def selected_layer(k):
    nc, io, ps = k.nc, k.io, k.ps
    put = Place(k.arena, 0, k.arena_size)
    sel, xs, ht, kt = put(ST, ROW), put(ST, D), put(KT, SEL), put(NHK, SEL)
    v, b_v, raw, qt = put(ST, NHK * HD), put(NHK * HD), put(2, 2, SEL), put(2, 2, SEL)
    turn, cosine, t1, t2 = put(ST, 2 * P), put(2, SEL), put(2, SEL), put(2, SEL)
    prob, prob_t, attn = put(2, 3 * P), put(2, 3 * P), put(4, SEL)
    silu, hid = put(2, 2, SEL), put(3, 2, SEL)
    x1, x1s, fin, junk = put(ST, D), put(ST, D), put(ST, D), put(D)
    tiny = Place(k.small, 0, k.token_at)
    ss, ms, rstd, gate, left = tiny(ST), tiny(ST), tiny(ST), tiny(ST), tiny(ST)
    token = k.token
    top, total, inv = tiny(2, 2), tiny(2, 2), tiny(2, 2)
    ln1, ln2, b_q, b_k = tiny(KT), tiny(KT), tiny(NHQ), tiny(NHK)
    slots = [k.xnt[:, i * CH:(i + 1) * CH] for i in range(SLOTS)]

    def chunk(what, i):
        a = slots[CHUNKS.index((what, i)) % SLOTS]
        return a.rearrange("p (a b) -> p a b", b=D if what in ("wo", "down") else 2 * P)

    tasks = [("xT", a) for a in range(2)] + [("turnT",)] + [("k", i) for i in range(4)]
    tasks += [("v", i) for i in range(4)]
    for step in range(NHK + 3):
        if step < NHK:
            tasks.append(("q", step))
        if 1 <= step <= NHK:
            tasks += [("S", step - 1, hh) for hh in range(2)]
        if 2 <= step <= NHK + 1:
            tasks += [("PT", step - 2, hh) for hh in range(2)] + [("PV", step - 2, hh) for hh in range(2)]
    tasks += [("x1T", a) for a in range(2)]
    for i in range(NHK):
        tasks += [("gate", i), ("up", i)]
    ring = Ring(k.sem, "last", [2, 3, 4, 5, 6, 7], tasks)
    s = sems(k, "last", """rows_in small_in rms_in rms_out xs_out ht_out turns_in turn_out raw_out roped
             v_out masked exp_out prob_out pt_out attn_out wo_done x1_out rms2_in rms2_out x1s_out h2_out silu_out
             hid_out down_done fin_out out_stored kt_out gate_out""")
    chunk_in = [k.sem(f"chunk_in{i}") for i in range(SLOTS)]
    dve_done, act_done, pool_done = k.chain["dve"], k.chain["act"], k.chain["pool"]
    scale = float(HD) ** -0.5

    def bank(task):
        return ps[:, ring.bank(task), :]

    def two(a, n=SEL):
        return a.rearrange("p (a b) -> p a b", b=n)

    with nc.Block() as block:

        @block.sync
        def _(sp):
            for to, what in ((ln1, "ln1"), (ln2, "ln2"), (b_q, "bq"), (b_k, "bk")):
                sp.dma_start(to, io[what]).then_inc(s["small_in"], 16)
            sp.dma_start(b_v, io["bv"].partition_broadcast(P)).then_inc(s["small_in"], 16)
            for n, (what, i) in enumerate(CHUNKS):
                if n >= SLOTS:
                    before, j = CHUNKS[n - SLOTS]
                    if before in ("wo", "down"):
                        sp.wait_ge(s[f"{before}_done"], j + 1)
                    else:
                        sp.wait_ge(ring.filled, ring.at[(before, j)] + 1)
                sp.dma_start(slots[n % SLOTS], io["chunks"][n]).then_inc(chunk_in[n % SLOTS], 16)

        @block.gpsimd
        def _(pool):
            def rsqrt(count, ready, out):
                pool.wait_ge(ready, count)
                pool_done(pool, pool.tensor_scalar(ms, ss, 1.0 / D, 1e-6, ALU.mult, ALU.add))
                pool.tensor_tensor(rstd, ms, c(k, "neghalf")[:, 0:ST], ALU.pow).then_inc(out, 1)

            pool.wait_ge(k.rows_stored, 16 * NB)
            for j in range(ST):
                pool.indirect_dma_start(
                    out=sel[:, j, :], out_offset=None, in_=k.kept[:, :],
                    in_offset=bass.IndirectOffsetOnAxis(ap=token[:, j:j + 1], axis=0), bounds_check=T - 1,
                    oob_is_err=False).then_inc(s["rows_in"], 16)
            for j in range(ST):
                pool.indirect_dma_start(
                    out=turn[:, j, :], out_offset=None, in_=io["turns"],
                    in_offset=bass.IndirectOffsetOnAxis(ap=token[:, j:j + 1], axis=0), bounds_check=T - 1,
                    oob_is_err=False).then_inc(s["turns_in"], 16)
            rsqrt(1, s["rms_in"], s["rms_out"])
            rsqrt(1, s["rms2_in"], s["rms2_out"])
            pool.wait_ge(s["fin_out"], 1)
            for i in range(2):
                pool.wait_ge(k.base_in[i], 16 * (NT // 2))
            for j in range(ST):
                pool.indirect_dma_start(
                    out=io["out"], out_offset=bass.IndirectOffsetOnAxis(ap=token[:, j:j + 1], axis=0),
                    in_=fin[:, j, :], in_offset=None, bounds_check=T - 1,
                    oob_is_err=False).then_inc(s["out_stored"], 16)
            pool.wait_ge(s["out_stored"], 16 * ST)

        @block.scalar
        def _(act):
            def spread(task, ln, out):
                a = task[1]
                ring.full(act, task)
                for b in range(2):
                    m = a * 2 + b
                    ins = act.activation(ht[:, m, :], bank(task)[:, b * SEL:(b + 1) * SEL], ACT.Copy,
                                         scale=ln[:, m:m + 1])
                ins.then_inc(out, 1)
                act.wait_ge(out, a + 1)
                act.sem_inc(ring.empty(task), 1)

            def biased(task, bias, r):
                if r >= 2:
                    act.wait_ge(s["roped"], r - 1)
                ring.full(act, task)
                for hh in range(2):
                    h = 2 * task[1] + hh
                    ins = act.activation(raw[:, r % 2, hh, :], bank(task)[:, hh * SEL:(hh + 1) * SEL],
                                         ACT.Identity, bias=bias[:, h:h + 1])
                ins.then_inc(s["raw_out"], 1)
                act.wait_ge(s["raw_out"], r + 1)
                act.sem_inc(ring.empty(task), 1)

            act.wait_ge(s["rows_in"], 16 * ST)
            act.activation(gate, sel[:, :, 2 * D], ACT.Sigmoid).then_inc(s["gate_out"], 1)
            act.wait_ge(s["small_in"], 16 * 5)
            for a in range(2):
                spread(("xT", a), ln1, s["ht_out"])
            ring.full(act, ("turnT",))
            act.activation(cosine, two(bank(("turnT",))), ACT.Copy).then_inc(s["turn_out"], 1)
            act.wait_ge(s["turn_out"], 1)
            act.sem_inc(ring.empty(("turnT",)), 1)
            for i in range(4):
                biased(("k", i), b_k, i)
            for step in range(NHK + 3):
                if step < NHK:
                    biased(("q", step), b_q, 4 + step)
                if 1 <= step <= NHK:
                    for hh in range(2):
                        h = 2 * (step - 1) + hh
                        act.wait_ge(s["masked"], h + 1)
                        for part, cols in enumerate((slice(0, P), slice(P, 3 * P))):
                            ins = act.activation(prob[:, hh, cols], prob[:, hh, cols], ACT.Exp,
                                                 bias=top[:, hh, part:part + 1], scale=scale,
                                                 accum_out=total[:, hh, part:part + 1])
                        ins.then_inc(s["exp_out"], 1)
                if 2 <= step <= NHK + 1:
                    i = step - 2
                    for hh in range(2):
                        ring.full(act, ("PT", i, hh))
                        act.activation(prob_t[:, hh, :], bank(("PT", i, hh))[:, 0:3 * P],
                                       ACT.Copy).then_inc(s["pt_out"], 1)
                        act.wait_ge(s["pt_out"], 2 * i + hh + 1)
                        act.sem_inc(ring.empty(("PT", i, hh)), 1)
                    for hh in range(2):
                        if i >= 2:
                            act.wait_ge(s["wo_done"], i - 1)
                        ring.full(act, ("PV", i, hh))
                        act.activation(attn[:, (2 * i + hh) % 4, :], bank(("PV", i, hh))[:, 0:SEL],
                                       ACT.Copy).then_inc(s["attn_out"], 1)
                        act.wait_ge(s["attn_out"], 2 * i + hh + 1)
                        act.sem_inc(ring.empty(("PV", i, hh)), 1)
            for a in range(2):
                spread(("x1T", a), ln2, s["h2_out"])
            for i in range(NHK):
                if i >= 2:
                    act.wait_ge(s["hid_out"], i - 1)
                ring.full(act, ("gate", i))
                act.activation(silu[:, i % 2, :, :], two(bank(("gate", i))), ACT.Silu).then_inc(s["silu_out"], 1)
                act.wait_ge(s["silu_out"], i + 1)
                act.sem_inc(ring.empty(("gate", i)), 1)

        @block.tensor
        def _(pe):
            ident = c(k, "ident")

            def arrived(what, i):
                n = CHUNKS.index((what, i))
                pe.wait_ge(chunk_in[n % SLOTS], 16 * (n // SLOTS + 1))

            def turn_rows(name, x):
                for a in range(2):
                    ring.free(pe, (name, a))
                    for b in range(2):
                        m = a * 2 + b
                        for j in range(ST):
                            mm = pe.transpose(bank((name, a))[:, b * SEL + j * P:b * SEL + (j + 1) * P],
                                              x[:, j, m * P:(m + 1) * P], ident)
                    mm.then_inc(ring.filled, 1)

            def features(what, i):
                arrived(what, i)
                ring.free(pe, (what, i))
                for hh in range(2):
                    for j in range(KT):
                        mm = pe.matmul(bank((what, i))[:, hh * SEL:(hh + 1) * SEL],
                                       chunk(what, i)[:, j, hh * P:(hh + 1) * P], ht[:, j, :],
                                       start=(j == 0), stop=(j == KT - 1))
                mm.then_inc(ring.filled, 1)

            pe.wait_ge(s["xs_out"], 1)
            turn_rows("xT", xs)
            pe.wait_ge(s["turns_in"], 16 * ST)
            ring.free(pe, ("turnT",))
            for b in range(2):
                for j in range(ST):
                    mm = pe.transpose(bank(("turnT",))[:, b * SEL + j * P:b * SEL + (j + 1) * P],
                                      turn[:, j, b * P:(b + 1) * P], ident)
            mm.then_inc(ring.filled, 1)
            pe.wait_ge(s["ht_out"], 2)
            for i in range(4):
                features("k", i)
            for i in range(4):
                arrived("v", i)
                ring.free(pe, ("v", i))
                for a in range(ST):
                    for j in range(KT):
                        mm = pe.matmul(bank(("v", i))[:, a * 2 * P:(a + 1) * 2 * P], ht[:, j, a * P:(a + 1) * P],
                                       chunk("v", i)[:, j, :], start=(j == 0), stop=(j == KT - 1))
                mm.then_inc(ring.filled, 1)
            for step in range(NHK + 3):
                if step < NHK:
                    features("q", step)
                if 1 <= step <= NHK:
                    i = step - 1
                    pe.wait_ge(s["roped"], 4 + i + 1)
                    for hh in range(2):
                        ring.free(pe, ("S", i, hh))
                        b = bank(("S", i, hh))
                        pe.matmul(b[:, 0:P], qt[:, i % 2, hh, 0:P], kt[:, i, 0:P], start=True, stop=True)
                        pe.matmul(b[:, P:3 * P], qt[:, i % 2, hh, P:2 * P], kt[:, i, :],
                                  start=True, stop=True).then_inc(ring.filled, 1)
                if 2 <= step <= NHK + 1:
                    i = step - 2
                    for hh in range(2):
                        pe.wait_ge(s["prob_out"], 2 * i + hh + 1)
                        ring.free(pe, ("PT", i, hh))
                        for part in range(3):
                            r = slice(part * P, (part + 1) * P)
                            mm = pe.transpose(bank(("PT", i, hh))[:, r], prob[:, hh, r], ident)
                        mm.then_inc(ring.filled, 1)
                if step >= 3:
                    i = step - 3
                    arrived("wo", i)
                    pe.wait_ge(s["attn_out"], 2 * i + 2)
                    for hh in range(2):
                        for j in range(ST):
                            mm = pe.matmul(ps[:, j, :], attn[:, (2 * i + hh) % 4, j * P:(j + 1) * P],
                                           chunk("wo", i)[:, hh, :], start=(i == 0 and hh == 0),
                                           stop=(i == NHK - 1 and hh == 1), skip_group_check=True)
                    mm.then_inc(s["wo_done"], 1)
                if 2 <= step <= NHK + 1:
                    i = step - 2
                    if i == 0:
                        pe.wait_ge(s["v_out"], 4)
                    for hh in range(2):
                        pe.wait_ge(s["pt_out"], 2 * i + hh + 1)
                        ring.free(pe, ("PV", i, hh))
                        b = bank(("PV", i, hh))
                        vh = slice(i * HD, (i + 1) * HD)
                        pe.matmul(b[:, 0:SEL], v[:, 0, vh], prob_t[:, hh, 0:2 * P], start=True, stop=True)
                        pe.matmul(b[:, P:2 * P], v[:, 1, vh], prob_t[:, hh, 2 * P:3 * P], start=False,
                                  stop=True, skip_group_check=True).then_inc(ring.filled, 1)
            pe.wait_ge(s["x1s_out"], 1)
            turn_rows("x1T", x1s)
            pe.wait_ge(s["h2_out"], 2)
            for step in range(NHK + 1):
                if step < NHK:
                    features("gate", step)
                    features("up", step)
                if step:
                    i = step - 1
                    arrived("down", i)
                    pe.wait_ge(s["hid_out"], i + 1)
                    for b in range(2):
                        for j in range(ST):
                            mm = pe.matmul(ps[:, j, :], hid[:, i % 3, b, j * P:(j + 1) * P],
                                           chunk("down", i)[:, b, :], start=(i == 0 and b == 0),
                                           stop=(i == NHK - 1 and b == 1), skip_group_check=True)
                    mm.then_inc(s["down_done"], 1)

        @block.vector
        def _(dve):
            def done(ins):
                dve_done(dve, ins)

            def rope(r, out, out_sem):
                dve.wait_ge(s["raw_out"], r + 1)
                if r:
                    dve.wait_ge(s["roped"], r)
                x = raw[:, r % 2, :, :]
                lo, hi = slice(0, 64), slice(64, 128)
                co = cosine[:, 0, :].unsqueeze(1).to_broadcast((P, 2, SEL))
                si = cosine[:, 1, :].unsqueeze(1).to_broadcast((P, 2, SEL))
                dve.tensor_tensor(t1, x, co, ALU.mult)
                dve.tensor_tensor(t2[lo], x[hi], si[hi], ALU.mult)
                done(dve.tensor_tensor(t2[hi], x[lo], si[lo], ALU.mult))
                dve.tensor_tensor(out, t1, t2, ALU.add).then_inc(s["roped"], 1)

            def square_mean(x, ready):
                for j in range(ST):
                    ins = dve.tensor_tensor_reduce(junk, x(j), x(j), 1.0, 0.0, ALU.mult, ALU.add,
                                                   ss[:, j:j + 1])
                    if j == 0:
                        done(ins)
                ins.then_inc(ready, 1)

            dve.wait_ge(s["rows_in"], 16 * ST)
            square_mean(lambda j: hidden_of(sel, j), s["rms_in"])
            dve.wait_ge(s["rms_out"], 1)
            for j in range(ST):
                ins = dve.tensor_scalar(xs[:, j, :], hidden_of(sel, j), rstd[:, j:j + 1], None, ALU.mult)
            ins.then_inc(s["xs_out"], 1)
            dve.wait_ge(s["gate_out"], 1)
            dve.tensor_scalar(left, gate, -1.0, 1.0, ALU.mult, ALU.add)
            dve.wait_ge(s["turn_out"], 1)
            for i in range(4):
                rope(i, kt[:, 2 * i:2 * i + 2, :], s["kt_out"])
            dve.wait_ge(s["small_in"], 16 * 5)
            for i in range(4):
                r = slice(i * 2 * P, (i + 1) * 2 * P)
                ring.full(dve, ("v", i))
                dve.tensor_tensor(v[:, :, r], two(bank(("v", i))), b_v[:, r].unsqueeze(1).to_broadcast((P, ST, 2 * P)),
                                  ALU.add).then_inc(s["v_out"], 1)
                dve.wait_ge(s["v_out"], i + 1)
                dve.sem_inc(ring.empty(("v", i)), 1)
            for step in range(NHK + 1):
                if step < NHK:
                    rope(4 + step, qt[:, step % 2, :, :], None)
                if step:
                    i = step - 1
                    for hh in range(2):
                        h = 2 * i + hh
                        ring.full(dve, ("S", i, hh))
                        if h >= 2:
                            ring.full(dve, ("PT", i - 1, hh))
                        dve.tensor_tensor(prob[:, hh, :], bank(("S", i, hh))[:, 0:3 * P], c(k, "addmask"),
                                          ALU.add).then_inc(ring.empty(("S", i, hh)), 1)
                        dve.wait_ge(ring.empty(("S", i, hh)), ring.at[("S", i, hh)] // 6 + 1)
                        dve.tensor_reduce(top[:, hh, 0:1], prob[:, hh, 0:P], AX.X, ALU.max)
                        done(dve.tensor_reduce(top[:, hh, 1:2], prob[:, hh, P:3 * P], AX.X, ALU.max))
                        dve.tensor_scalar(top[:, hh, :], top[:, hh, :], -scale, None,
                                          ALU.mult).then_inc(s["masked"], 1)
                    for hh in range(2):
                        h = 2 * i + hh
                        dve.wait_ge(s["exp_out"], h + 1)
                        done(dve.reciprocal(inv[:, hh, :], total[:, hh, :]))
                        dve.tensor_scalar(prob[:, hh, 0:P], prob[:, hh, 0:P], inv[:, hh, 0:1], None, ALU.mult)
                        dve.tensor_scalar(prob[:, hh, P:3 * P], prob[:, hh, P:3 * P], inv[:, hh, 1:2], None,
                                          ALU.mult).then_inc(s["prob_out"], 1)
            dve.wait_ge(s["wo_done"], NHK)
            for j in range(ST):
                ins = dve.tensor_tensor(x1[:, j, :], ps[:, j, :], hidden_of(sel, j),
                                        ALU.add)
            done(ins)
            square_mean(lambda j: x1[:, j, :], s["rms2_in"])
            dve.wait_ge(s["rms2_out"], 1)
            for j in range(ST):
                ins = dve.tensor_scalar(x1s[:, j, :], x1[:, j, :], rstd[:, j:j + 1], None, ALU.mult)
            ins.then_inc(s["x1s_out"], 1)
            for i in range(NHK):
                ring.full(dve, ("up", i))
                dve.wait_ge(s["silu_out"], i + 1)
                if i >= 3:
                    dve.wait_ge(s["down_done"], i - 2)
                dve.tensor_tensor(hid[:, i % 3, :, :], two(bank(("up", i))), silu[:, i % 2, :, :],
                                  ALU.mult).then_inc(s["hid_out"], 1)
                dve.wait_ge(s["hid_out"], i + 1)
                dve.sem_inc(ring.empty(("up", i)), 1)
            dve.wait_ge(s["down_done"], NHK)
            for j in range(ST):
                done(dve.tensor_tensor(x1[:, j, :], ps[:, j, :], x1[:, j, :], ALU.add))
                done(dve.tensor_scalar(x1[:, j, :], x1[:, j, :], gate[:, j:j + 1], None, ALU.mult))
                done(dve.scalar_tensor_tensor(x1[:, j, :], hidden_of(sel, j), left[:, j:j + 1], x1[:, j, :],
                                              ALU.mult, ALU.add))
                ins = dve.tensor_tensor(fin[:, j, :], x1[:, j, :], residual_of(sel, j), ALU.add)
            ins.then_inc(s["fin_out"], 1)


def build(nc, io):
    with ExitStack() as ctx:
        ctx.enter_context(nc.allow_non_contiguous_dma("weights in tiles"))
        k = setup(nc, ctx, io)
        k.expert_in = nc.dram_tensor("expert_in", (NE * CAP, D), F32, kind="Internal").ap()
        k.expert_out = nc.dram_tensor("expert_out", (NE * CAP, D), F32, kind="Internal").ap()
        k.given = k.sem("rows_given")
        k.kept = nc.dram_tensor("rows_kept", (T, ROW), F32, kind="Internal").ap()
        k.attention_in = k.sem("attention_weights_in")
        k.w_in, k.xe_in = ([k.sem(f"{n}{p}") for p in range(2)] for n in ("w_expert_in", "rows_in"))
        k.base_in = [k.sem(f"base_stored{i}") for i in range(2)]
        k.w_shared = k.arena[:, 0:KT * 2 * FI + FM * D]
        k.s_shared = k.sem("shared_in")
        k.y_stored = [k.sem(f"y_stored{p}") for p in range(2)]
        k.phase_sems.clear()
        gated_linear_attention(k)
        expert_memory(k)
        route_and_shared(k)
        experts(k)
        recycle(k)
        linear_attention_sums(k)
        linear_attention(k)
        selected_layer(k)


def layout(inputs):
    f = {n: np.asarray(a) for n, a in inputs.items()}

    def rows_first(w):
        return np.ascontiguousarray(w.reshape(-1, P, w.shape[1]).transpose(1, 0, 2))

    def expert(w1, w3, w2):
        up = np.concatenate([rows_first(w1.T), rows_first(w3.T)], axis=2).reshape(P, -1)
        w2t = np.concatenate([w2.T, np.zeros((FM * P - FI, D), np.float32)], axis=0)
        return np.concatenate([up, rows_first(w2t).reshape(P, -1)], axis=1)

    out = {"consts": constants(), "x": np.ascontiguousarray(f["L0_attn_hidden_states"].reshape(T, D))}
    out["w_qk"] = rows_first(np.concatenate([f["L0_attn_Wq"].T] * 4 + [f["L0_attn_Wk"].T] * 4, axis=1))
    out["w_ig"] = rows_first(f["L0_attn_Wig"].T)
    out["w_og"] = rows_first(f["L0_attn_Wog"].T)
    out["g_weight"] = f["L0_attn_g_weight"]
    out["w_shared"] = expert(f["L0_ffn_Ws1"], f["L0_ffn_Ws3"], f["L0_ffn_Ws2"])
    w = {n: f[f"L1_ffn_{n}"] for n in ("wq", "wk", "wv", "wo", "w_gate", "w_up", "w_down")}
    source = {"q": w["wq"], "k": w["wk"], "v": w["wv"], "wo": w["wo"], "gate": w["w_gate"], "up": w["w_up"],
              "down": w["w_down"]}
    chunks = []
    for what, i in CHUNKS:
        part = slice(i * 2 * P, (i + 1) * 2 * P)
        a = source[what][part, :] if what in ("wo", "down") else source[what][:, part]
        chunks.append(rows_first(a).reshape(P, CH))
    out["chunks"] = np.stack(chunks)
    for n, m in (("ln1", "ln1_w"), ("ln2", "ln2_w"), ("bq", "bq"), ("bk", "bk")):
        out[n] = np.ascontiguousarray(f[f"L1_ffn_{m}"].reshape(-1, P).T)
    out["bv"] = f["L1_ffn_bv"]
    out["turns"] = turns()
    out["w_attention"] = np.concatenate(
        [rows_first(f[f"L1_attn_W{n}"].T).reshape(P, -1) for n in "qkvo"], axis=1)
    for n in "kvo":
        out[f"b_{n}"] = f[f"L1_attn_b{n}"]
    out["b_q"] = np.ascontiguousarray(f["L1_attn_bq"].reshape(KT, P).T)
    out["decay_row"] = np.exp(-np.arange(T, dtype=np.float32) / np.float32(T))
    out["w_router"] = f["L1_ffn_w_router"]
    out["gate_w"] = rows_first(f["L0_ffn_gate_w"].T)
    out["gate_b"] = f["L0_ffn_gate_b"]
    out["w_expert"] = np.stack([expert(f["L0_ffn_W1"][e], f["L0_ffn_W3"][e], f["L0_ffn_W2"][e]) for e in range(NE)])
    return out


def kernel(**inputs):
    import concourse.bacc as _bacc
    from concourse.bass_utils import run_bass_kernel_spmd as _run

    nc = _bacc.Bacc("TRN2", target_bir_lowering=False, num_devices=1)
    arrays, io = {}, {}
    for name, a in layout(inputs).items():
        arrays[f"in_{name}_dram"] = a
        io[name] = nc.dram_tensor(f"in_{name}_dram", a.shape, mybir.dt.from_np(a.dtype), kind="ExternalInput").ap()
    io["out"] = nc.dram_tensor("out_0_dram", (T, D), F32, kind="ExternalOutput").ap()
    build(nc, io)
    r = _run(nc, [arrays], core_ids=[0])
    return r.results[0]["out_0_dram"].reshape(1, T, D)
```

```python
from contextlib import ExitStack

import numpy as np

import concourse.bass as bass
from concourse import mybir

ALU = mybir.AluOpType
ACT = mybir.ActivationFunctionType
AX = mybir.AxisListType
F32 = mybir.dt.float32
U32 = mybir.dt.uint32
BF16 = mybir.dt.bfloat16

P = 128
T = 2048
D = 512
NT = T // P
KT = D // P
NB = 4
BT = NT // NB
BW = T // NB
DK = 32
SUB = 32
NE = 16
CAP = 256
FI = 352
FM = 3
SEL = 256
ST = SEL // P
HD = 128
NHQ, NHK = 16, 8
FF = 2048
FFT = FF // P
ROW = 2 * D + 1

_AT = {}
_n = 0
for _name, _w in (("ident", P), ("causal", P), ("before", P), ("ones", P), ("own", 16), ("cq", 16), ("ck", 16),
                  ("expert", NE), ("rank", NE), ("restart", NT * NE), ("decay", NT),
                  ("neghalf", NT), ("addmask", 3 * P), ("earlier", P), ("slot", SEL),
                  ("number", 2 * NT)):
    _AT[_name] = (_n, _n + _w)
    _n += _w
NCONST = _n
SMALL = 256


def constants():
    c = np.zeros((P, NCONST), np.float32)

    def put(name, a):
        lo, hi = _AT[name]
        c[:, lo:hi] = np.asarray(a, np.float32).reshape(P, hi - lo)

    r = np.arange(P)
    put("ident", np.eye(P))
    put("causal", r[:, None] <= r[None, :])
    put("before", r[:, None] < r[None, :])
    lower = np.where(r[None, :] <= r[:, None], 0.0, -3.0e38)
    put("addmask", np.concatenate([lower, np.zeros((P, P)), lower], axis=1))
    put("ones", np.ones((P, P)))
    g = r // SUB
    own = np.zeros((P, BT, 4))
    cq = np.zeros((P, BT, 4))
    ck = np.zeros((P, BT, 4))
    for b in range(4):
        own[g == b, :, b] = 1
    cq[g == 0, :, 2] = 1
    cq[g == 1, :, 1] = 1
    cq[g == 2, :, 3] = 1
    cq[g == 3, :, 0] = 1
    put("own", own)
    put("cq", cq)
    put("ck", ck)
    put("expert", np.broadcast_to(np.arange(NE), (P, NE)))
    put("rank", np.broadcast_to(NE - np.arange(NE), (P, NE)))
    put("restart", np.broadcast_to(np.arange(NT) > 0, (P, NE, NT)))
    token = np.arange(NT)[None, :] * P + r[:, None]
    put("decay", np.exp(-token.astype(np.float32) / np.float32(T)))
    put("neghalf", np.full((P, NT), -0.5))
    put("earlier", r[None, :] < r[:, None])
    put("slot", np.broadcast_to(np.arange(SEL), (P, SEL)))
    put("number", np.stack([np.broadcast_to(r[:, None], (P, NT)), np.broadcast_to(np.arange(NT), (P, NT))], axis=2))
    return c


def turns():
    freq = (1.0 / np.float32(10000.0) ** (np.arange(0, HD, 2, dtype=np.float32) / np.float32(HD))).astype(np.float32)
    ang = np.arange(T, dtype=np.float32)[:, None] * freq
    co, si = np.cos(ang).astype(np.float32), np.sin(ang).astype(np.float32)
    return np.concatenate([co, co, si, -si], axis=1)


class Ring:

    def __init__(self, sem, name, banks, tasks):
        self.banks = banks
        self.at = {t: i for i, t in enumerate(tasks)}
        assert len(self.at) == len(tasks)
        self.filled = sem(f"{name}_filled")
        self.drained = [sem(f"{name}_drained{b}") for b in banks]

    def bank(self, task):
        return self.banks[self.at[task] % len(self.banks)]

    def free(self, pe, task):
        k, n = divmod(self.at[task], len(self.banks))
        if k:
            pe.wait_ge(self.drained[n], k)

    def full(self, eng, task):
        eng.wait_ge(self.filled, self.at[task] + 1)

    def empty(self, task):
        return self.drained[self.at[task] % len(self.banks)]

    def all_drained(self, pe):
        total = len(self.at)
        for n in range(len(self.banks)):
            uses = (total - n + len(self.banks) - 1) // len(self.banks)
            if uses:
                pe.wait_ge(self.drained[n], uses)


class Chain:

    def __init__(self, sem):
        self.sem, self.n = sem, 0

    def __call__(self, eng, ins):
        ins.then_inc(self.sem, 1)
        self.n += 1
        eng.wait_ge(self.sem, self.n)


class Build:
    pass


def setup(nc, ctx, io):
    k = Build()
    k.nc, k.ctx, k.io = nc, ctx, io
    k.phase_sems = []

    def sem(name):
        k.phase_sems.append(nc.alloc_semaphore(name))
        return k.phase_sems[-1]

    k.sem = sem
    k.rows = ctx.enter_context(nc.sbuf_tensor("rows", [P, NT, ROW], F32))
    k.xnt = ctx.enter_context(nc.sbuf_tensor("xnt", [P, KT * T], F32))
    k.con = ctx.enter_context(nc.sbuf_tensor("con", [P, NCONST], F32))
    k.small = ctx.enter_context(nc.sbuf_tensor("small", [P, SMALL], F32))
    k.token_at = SMALL - ST
    k.token = k.small[:, k.token_at:SMALL].bitcast(U32)
    k.arena_size = 26368
    k.arena = ctx.enter_context(nc.sbuf_tensor("arena", [P, k.arena_size], F32))
    k.ps = ctx.enter_context(nc.psum_tensor("ps", [P, 8, 512], F32))
    k.chain = {e: Chain(k.sem(f"{e}_done")) for e in ("dve", "act", "pool")}
    k.s_con = k.sem("constants_in")
    return k


def c(k, name, rows=slice(0, P)):
    lo, hi = _AT[name]
    return k.con[rows, lo:hi]


def recycle(k):
    k.nc.all_engine_barrier()
    k.nc.clear_and_free_semaphores(k.phase_sems)
    k.phase_sems.clear()
    k.nc.all_engine_barrier()


class Place:

    def __init__(self, tensor, at, end):
        self.tensor, self.at, self.end = tensor, at, end

    def __call__(self, *dims):
        n = int(np.prod(dims))
        a = self.tensor[:, self.at:self.at + n]
        self.at += n
        assert self.at <= self.end, (self.at, self.end)
        if len(dims) == 2:
            a = a.rearrange("p (a b) -> p a b", b=dims[1])
        if len(dims) == 3:
            a = a.rearrange("p (a b c) -> p a b c", b=dims[1], c=dims[2])
        return a


def wide(ap, n):
    return ap.unsqueeze(2).to_broadcast((ap.shape[0], ap.shape[1], n))


def sems(k, prefix, names):
    return {n: k.sem(f"{prefix}_{n}") for n in names.split()}


def turn_rows(k, pe, ring, n):
    for j in range(KT):
        ring.free(pe, ("x2T", n, j))
        b = k.ps[:, ring.bank(("x2T", n, j)), :]
        for i in range(BT):
            mm = pe.transpose(b[:, i * P:(i + 1) * P], k.rows[:, n * BT + i, D + j * P:D + (j + 1) * P],
                              c(k, "ident"))
        mm.then_inc(ring.filled, 1)


def keep_turned(k, act, ring, n, j):
    ring.full(act, ("x2T", n, j))
    act.activation(k.x2nt[n][:, j, :], k.ps[:, ring.bank(("x2T", n, j)), :],
                   ACT.Copy).then_inc(ring.empty(("x2T", n, j)), 1)


def logits(k, pe, ring, n):
    for j in range(KT):
        pe.wait_ge(ring.empty(("x2T", n, j)), ring.at[("x2T", n, j)] // len(ring.banks) + 1)
        mm = pe.matmul(k.ps[0:NE, n, :], k.gate_w[:, j, :], k.x2nt[n][:, j, :], start=(j == 0), stop=(j == KT - 1))
    return mm


def gated_linear_attention(k):
    nc, io, ps, rows = k.nc, k.io, k.ps, k.rows
    put = Place(k.arena, 4352, k.arena_size)
    w_qk, w_og, w_ig, gw = put(KT, 2 * P), put(KT, D), put(KT, D), put(D)
    xn = [put(BT, D) for _ in range(2)]
    put_x = Place(k.xnt, 0, KT * T)
    xnt = [put_x(KT, BW) for _ in range(2)]
    ksig, decay, qsig, starts, prod, inv, qs = (put(BW) for _ in range(7))
    qd, kd, qx, kx = (put(BW) for _ in range(4))
    att, kst, state = put(BT, P), put(BT, DK), put(2, D)
    o, ot, sg = put(2, D), put(2, KT, P), put(2, D)
    og, gated, junk = put(D), put(D), put(D)
    tiny = Place(k.small, 0, SMALL)
    stats, mv, rstd, ve = tiny(BT, 6), tiny(BT, 2), tiny(BT), tiny(BT)
    ss, rr, ms = tiny(BT), tiny(BT), tiny(BT)
    stats2, mv2, rstd2, ve2 = tiny(BT, 6), tiny(BT, 2), tiny(BT), tiny(BT)
    assert put.at <= k.arena_size - KT * NE
    cq, ck, own = c(k, "cq"), c(k, "ck"), c(k, "own")

    tasks = []
    for n in range(NB):
        tasks += [("xT", n, i) for i in range(KT)] + [("q", n), ("k", n), ("AT", n), ("KST", n)]
        tasks += [("U", n, 0), ("o", n, 0), ("U", n, 1), ("o", n, 1), ("oT", n, 0), ("U", n, 2), ("o", n, 2),
                  ("oT", n, 1), ("U", n, 3), ("o", n, 3), ("oT", n, 2), ("oT", n, 3)]
    tasks += [("x2T", n, j) for n in range(NB - 1) for j in range(KT)]
    ring = Ring(k.sem, "gla", [4, 5, 6, 7], tasks)
    x_in = [k.sem(f"x_in{n}") for n in range(NB)]
    s = sems(k, "gla", """w_qk_in w_og_in w_ig_in gw_in ln_stats ln_rstd ln_out xnt_out decay_out qsig_out
             features att_out kst_out state_out o_out square_out rr_out ot_out go_full go_empty sg_out sg_used
             og_out ln2_stats ln2_rstd ln2_out zero_out zeros_in""")
    dve_done, act_done, pool_done = k.chain["dve"], k.chain["act"], k.chain["pool"]

    def bank(task):
        return ps[:, ring.bank(task), :]

    with nc.Block() as block:

        @block.sync
        def _(sp):
            sp.dma_start(k.con[:, :], io["consts"]).then_inc(k.s_con, 16)
            for n in range(NB):
                x = io["x"].rearrange("(t p) d -> p t d", p=P)[:, n * BT:(n + 1) * BT, :]
                sp.dma_start(rows[:, n * BT:(n + 1) * BT, 0:D], x).then_inc(x_in[n], 16)
                if n == 0:
                    sp.dma_start(w_qk, io["w_qk"]).then_inc(s["w_qk_in"], 16)
                    sp.dma_start(w_ig, io["w_ig"]).then_inc(s["w_ig_in"], 16)
                    sp.dma_start(w_og, io["w_og"]).then_inc(s["w_og_in"], 16)
                    sp.dma_start(gw, io["g_weight"].partition_broadcast(P)).then_inc(s["gw_in"], 16)
            sp.dma_start(k.w_shared, io["w_shared"]).then_inc(k.s_shared, 16)
            sp.dma_start(k.gate_w, io["gate_w"]).then_inc(k.gate_in, 16)
            sp.wait_ge(s["zero_out"], 1)
            zeros = og.unsqueeze(1).to_broadcast((P, NE * CAP // P, D))
            sp.dma_start(k.expert_in.rearrange("(p r) d -> p r d", p=P), zeros).then_inc(s["zeros_in"], 16)

        @block.gpsimd
        def _(pool):
            pool.wait_ge(k.s_con, 16)

            def rsqrt(out, tmp, src, scale, done, eps=1e-5):
                pool_done(pool, pool.tensor_scalar(tmp, src, scale, eps, ALU.mult, ALU.add))
                n = out.shape[1]
                pool.tensor_tensor(out, tmp, c(k, "neghalf")[:, 0:n], ALU.pow).then_inc(done, 1)

            pool.wait_ge(s["ln_stats"], 1)
            rsqrt(rstd, ve, mv[:, :, 1], 1.0, s["ln_rstd"])
            for n in range(NB):
                if n + 1 < NB:
                    pool.wait_ge(s["ln_stats"], n + 2)
                    rsqrt(rstd, ve, mv[:, :, 1], 1.0, s["ln_rstd"])
                for i in range(BT):
                    pool.wait_ge(s["square_out"], n * BT + i + 1)
                    rsqrt(rr[:, i:i + 1], ms[:, i:i + 1], ss[:, i:i + 1], 1.0 / D, s["rr_out"])
                pool.wait_ge(s["ln2_stats"], n + 1)
                rsqrt(rstd2, ve2, mv2[:, :, 1], 1.0, s["ln2_rstd"])

        @block.scalar
        def _(act):
            def o_out(n, i):
                t = n * BT + i
                if t >= 2:
                    act.wait_ge(s["og_out"], t - 1)
                ring.full(act, ("o", n, i))
                act.activation(o[:, i % 2, :], bank(("o", n, i)), ACT.Copy).then_inc(s["o_out"], 1)
                act.activation(junk, bank(("o", n, i)), ACT.Square,
                               accum_out=ss[:, i:i + 1]).then_inc(s["square_out"], 1)
                act.wait_ge(s["square_out"], t + 1)
                act.sem_inc(ring.empty(("o", n, i)), 1)

            def ot_out(n, i):
                ring.full(act, ("oT", n, i))
                act.activation(ot[:, i % 2, :, :], bank(("oT", n, i)).rearrange("p (a b) -> p a b", b=P),
                               ACT.Copy).then_inc(ring.empty(("oT", n, i)), 1)

            def sg_out(n, i):
                t = n * BT + i
                act.wait_ge(s["go_full"], t + 1)
                if t >= 2:
                    act.wait_ge(s["sg_used"], t - 1)
                act.activation(sg[:, i % 2, :], ps[:, i, :], ACT.Sigmoid).then_inc(s["sg_out"], 1)

            for n in range(NB):
                for i in range(KT):
                    ring.full(act, ("xT", n, i))
                    act.activation(xnt[n % 2][:, i, :], bank(("xT", n, i)),
                                   ACT.Copy).then_inc(ring.empty(("xT", n, i)), 1)
                ring.full(act, ("k", n))
                if n:
                    act.wait_ge(s["features"], n)
                act_done(act, act.activation(ksig, bank(("k", n)), ACT.Sigmoid))
                act.activation(decay, ksig, ACT.Sigmoid, scale=-1.0).then_inc(s["decay_out"], 1)
                act.activation(qsig, bank(("q", n)), ACT.Sigmoid).then_inc(s["qsig_out"], 1)
                o_out(n, 0)
                o_out(n, 1)
                ot_out(n, 0)
                o_out(n, 2)
                ot_out(n, 1)
                sg_out(n, 0)
                o_out(n, 3)
                ot_out(n, 2)
                sg_out(n, 1)
                ot_out(n, 3)
                sg_out(n, 2)
                sg_out(n, 3)
            for n in range(NB - 1):
                for j in range(KT):
                    keep_turned(k, act, ring, n, j)

        @block.tensor
        def _(pe):
            pe.wait_ge(k.s_con, 16)
            ident = c(k, "ident")

            def project_out(n, i):
                t = n * BT + i
                pe.wait_ge(ring.empty(("oT", n, i)), ring.at[("oT", n, i)] // 4 + 1)
                for j in range(KT):
                    mm = pe.matmul(ps[:, i, :], ot[:, i % 2, j, :], w_og[:, j, :], start=False, stop=(j == KT - 1))
                mm.then_inc(s["go_full"], 1)

            def project_in(n, i):
                t = n * BT + i
                if n:
                    pe.wait_ge(s["go_empty"], t - BT + 1)
                for j in range(KT):
                    pe.matmul(ps[:, i, :], xnt[n % 2][:, j, i * P:(i + 1) * P], w_ig[:, j, :],
                              start=(j == 0), stop=False)

            def update(n, i):
                ring.free(pe, ("U", n, i))
                pe.matmul(bank(("U", n, i))[96:128, :], kst[:, i, :], xn[n % 2][:, i, :],
                          start=True, stop=True).then_inc(ring.filled, 1)

            def output(n, i):
                t = n * BT + i
                ring.free(pe, ("o", n, i))
                pe.matmul(bank(("o", n, i)), att[:, i, :], xn[n % 2][:, i, :], start=True, stop=False)
                pe.wait_ge(s["state_out"], t + 1)
                pe.matmul(bank(("o", n, i)), qx[96:128, i * P:(i + 1) * P], state[96:128, t % 2, :],
                          start=False, stop=True).then_inc(ring.filled, 1)

            def turn(n, i):
                t = n * BT + i
                pe.wait_ge(s["o_out"], t + 1)
                ring.free(pe, ("oT", n, i))
                for j in range(KT):
                    mm = pe.transpose(bank(("oT", n, i))[:, j * P:(j + 1) * P], o[:, i % 2, j * P:(j + 1) * P], ident)
                mm.then_inc(ring.filled, 1)

            for n in range(NB):
                pe.wait_ge(s["ln_out"], n + 1)
                for j in range(KT):
                    ring.free(pe, ("xT", n, j))
                    for i in range(BT):
                        mm = pe.transpose(bank(("xT", n, j))[:, i * P:(i + 1) * P],
                                          xn[n % 2][:, i, j * P:(j + 1) * P], ident)
                    mm.then_inc(ring.filled, 1)
                if n == 0:
                    pe.wait_ge(s["w_qk_in"], 16)
                for h, what in enumerate("qk"):
                    ring.free(pe, (what, n))
                    for j in range(KT):
                        if h == 0:
                            pe.wait_ge(ring.empty(("xT", n, j)), ring.at[("xT", n, j)] // 4 + 1)
                        mm = pe.matmul(bank((what, n)), w_qk[:, j, h * P:(h + 1) * P], xnt[n % 2][:, j, :],
                                       start=(j == 0), stop=(j == KT - 1))
                    mm.then_inc(ring.filled, 1)
                if n == 0:
                    pe.wait_ge(s["w_ig_in"], 16)
                for i in range(3):
                    project_in(n, i)
                pe.wait_ge(s["features"], n + 1)
                ring.free(pe, ("AT", n))
                for i in range(BT):
                    r = slice(i * P, (i + 1) * P)
                    pe.matmul(bank(("AT", n))[:, r], kd[:, r], qd[:, r], start=True, stop=False)
                    mm = pe.matmul(bank(("AT", n))[:, r], kx[0:96, r], qx[0:96, r], start=False, stop=True)
                mm.then_inc(ring.filled, 1)
                ring.free(pe, ("KST", n))
                for i in range(BT):
                    mm = pe.transpose(bank(("KST", n))[:, i * DK:(i + 1) * DK], kx[96:128, i * P:(i + 1) * P],
                                      ident[96:128, 96:128])
                mm.then_inc(ring.filled, 1)
                project_in(n, 3)
                pe.wait_ge(s["kst_out"], n + 1)
                pe.wait_ge(s["att_out"], n + 1)
                if n == 0:
                    pe.wait_ge(s["w_og_in"], 16)
                update(n, 0)
                output(n, 0)
                update(n, 1)
                output(n, 1)
                turn(n, 0)
                update(n, 2)
                output(n, 2)
                turn(n, 1)
                project_out(n, 0)
                update(n, 3)
                output(n, 3)
                turn(n, 2)
                project_out(n, 1)
                turn(n, 3)
                project_out(n, 2)
                project_out(n, 3)
            for n in range(NB - 1):
                pe.wait_ge(s["ln2_out"], n + 1)
                turn_rows(k, pe, ring, n)
            pe.wait_ge(k.gate_in, 16)
            for n in range(NB - 1):
                pe.wait_ge(s["go_empty"], NT - BT + n + 1)
                logits(k, pe, ring, n)

        @block.vector
        def _(dve):
            def done(ins):
                dve_done(dve, ins)

            def ln_in(n):
                dve.wait_ge(x_in[n], 16)
                for i in range(BT):
                    done(dve.bn_stats(stats[:, i, :], rows[:, n * BT + i, 0:D]))
                for i in range(BT):
                    ins = dve.bn_aggr(mv[:, i, :], stats[:, i, :])
                ins.then_inc(s["ln_stats"], 1)
                dve.wait_ge(s["ln_rstd"], n + 1)
                for i in range(BT):
                    ins = dve.tensor_scalar(xn[n % 2][:, i, :], rows[:, n * BT + i, 0:D], mv[:, i, 0:1],
                                            rstd[:, i:i + 1], ALU.subtract, ALU.mult)
                ins.then_inc(s["ln_out"], 1)

            def features(n):
                dve.wait_ge(s["decay_out"], n + 1)
                first = decay.rearrange("p (c t) -> p c t", t=SUB)[:, :, 0:1]
                done(dve.tensor_copy(starts.rearrange("p (c t) -> p c t", t=SUB)[:, :, 0:1], first))
                done(dve.memset(first, 0.0))
                done(dve.tensor_tensor_scan(prod, decay, starts, 0.0, ALU.mult, ALU.add))
                dve.reciprocal(inv, prod)
                ring.full(dve, ("q", n))
                dve.wait_ge(s["qsig_out"], n + 1)
                ins = dve.scalar_tensor_tensor(qs, bank(("q", n)), float(DK) ** -0.5, qsig, ALU.mult, ALU.mult)
                ins.then_inc(ring.empty(("q", n)), 1)
                dve.sem_inc(ring.empty(("k", n)), 1)
                end = prod.rearrange("p (c b t) -> p c b t", b=4, t=SUB)[:, :, :, SUB - 1]
                q3, k3 = (a.rearrange("p (c b) -> p c b", b=4) for a in (cq, ck))

                def whole(g, b):
                    return end[g * SUB:(g + 1) * SUB, :, b]

                def q_(g, b):
                    return q3[g * SUB:(g + 1) * SUB, :, b]

                def k_(g, b):
                    return k3[g * SUB:(g + 1) * SUB, :, b]

                dve.tensor_copy(q_(0, 3), whole(0, 2))
                dve.tensor_copy(q_(3, 1), whole(3, 0))
                dve.tensor_copy(k_(0, 1), whole(0, 1))
                dve.tensor_tensor(k_(0, 0), whole(0, 0), whole(0, 1), ALU.mult)
                dve.tensor_copy(k_(1, 0), whole(1, 0))
                dve.tensor_copy(k_(2, 2), whole(2, 2))
                done(dve.tensor_copy(k_(3, 3), whole(3, 3)))
                dve.tensor_tensor(q_(3, 2), q_(3, 1), whole(3, 1), ALU.mult)
                done(dve.tensor_tensor(k_(3, 2), k_(3, 3), whole(3, 2), ALU.mult))
                dve.tensor_tensor(q_(3, 3), q_(3, 2), whole(3, 2), ALU.mult)
                done(dve.tensor_tensor(k_(3, 1), k_(3, 2), whole(3, 1), ALU.mult))
                done(dve.tensor_tensor(k_(3, 0), k_(3, 1), whole(3, 0), ALU.mult))
                dve.tensor_tensor(qs, qs, prod, ALU.mult)
                done(dve.tensor_tensor(ksig, ksig, inv, ALU.mult))

                def scaled(out, a, by):
                    return dve.tensor_tensor(out.rearrange("p (c t) -> p c t", t=SUB),
                                             a.rearrange("p (c t) -> p c t", t=SUB), wide(by, SUB), ALU.mult)

                scaled(qd, qs, own)
                scaled(kd, ksig, own)
                scaled(qx, qs, cq)
                scaled(kx, ksig, ck).then_inc(s["features"], 1)

            def post(n, i):
                t = n * BT + i
                dve.wait_ge(s["rr_out"], t + 1)
                dve.wait_ge(s["o_out"], t + 1)
                if t == 0:
                    dve.wait_ge(s["zeros_in"], 16)
                dve.scalar_tensor_tensor(og, o[:, i % 2, :], rr[:, i:i + 1], gw, ALU.mult,
                                         ALU.mult).then_inc(s["og_out"], 1)
                dve.wait_ge(s["sg_out"], t + 1)
                dve.tensor_tensor(gated, ps[:, i, :], sg[:, i % 2, :], ALU.mult).then_inc(s["go_empty"], 1)
                dve.wait_ge(s["go_empty"], t + 1)
                dve.sem_inc(s["sg_used"], 1)
                done(dve.tensor_tensor(og, og, gated, ALU.mult))
                x = rows[:, t, 0:D]
                done(dve.tensor_tensor(x, x, og, ALU.add))
                done(dve.bn_stats(stats2[:, i, :], x))
                ins = dve.bn_aggr(mv2[:, i, :], stats2[:, i, :])
                if i == BT - 1:
                    ins.then_inc(s["ln2_stats"], 1)

            dve.wait_ge(k.s_con, 16)
            dve.memset(og, 0.0).then_inc(s["zero_out"], 1)
            dve.memset(starts, 0.0)
            dve.memset(state[96:128, 0, :], 0.0).then_inc(s["state_out"], 1)
            ln_in(0)
            for n in range(NB):
                features(n)
                if n + 1 < NB:
                    ln_in(n + 1)
                ring.full(dve, ("AT", n))
                dve.tensor_tensor(att, bank(("AT", n)).rearrange("p (a b) -> p a b", b=P),
                                  c(k, "causal").unsqueeze(1).to_broadcast((P, BT, P)),
                                  ALU.mult).then_inc(s["att_out"], 1)
                dve.wait_ge(s["att_out"], n + 1)
                dve.sem_inc(ring.empty(("AT", n)), 1)
                ring.full(dve, ("KST", n))
                dve.tensor_copy(kst, bank(("KST", n))[:, 0:BT * DK].rearrange("p (a b) -> p a b", b=DK)
                                ).then_inc(s["kst_out"], 1)
                dve.wait_ge(s["kst_out"], n + 1)
                dve.sem_inc(ring.empty(("KST", n)), 1)
                if n == 0:
                    dve.wait_ge(s["gw_in"], 16)

                def step(i):
                    t = n * BT + i
                    ring.full(dve, ("U", n, i))
                    dve.scalar_tensor_tensor(state[96:128, (t + 1) % 2, :], state[96:128, t % 2, :],
                                             ck[96:128, 4 * i:4 * i + 1], bank(("U", n, i))[96:128, :],
                                             ALU.mult, ALU.add).then_inc(s["state_out"], 1)
                    dve.wait_ge(s["state_out"], t + 2)
                    dve.sem_inc(ring.empty(("U", n, i)), 1)

                step(0)
                step(1)
                step(2)
                post(n, 0)
                step(3)
                post(n, 1)
                post(n, 2)
                post(n, 3)
                dve.wait_ge(s["ln2_rstd"], n + 1)
                for i in range(BT):
                    t = n * BT + i
                    ins = dve.tensor_scalar(rows[:, t, D:2 * D], rows[:, t, 0:D], mv2[:, i, 0:1],
                                            rstd2[:, i:i + 1], ALU.subtract, ALU.mult)
                ins.then_inc(s["ln2_out"], 1)


W_UP = KT * 2 * FI
W_ALL = W_UP + FM * D
FROWS = [P, P, FI - 2 * P]


def weights(a):
    return (a[:, 0:W_UP].rearrange("p (a b) -> p a b", b=2 * FI),
            a[:, W_UP:W_ALL].rearrange("p (a b) -> p a b", b=D))


def expert_memory(k):
    put = Place(k.arena, W_ALL, k.arena_size)
    k.w_expert = [put(W_ALL) for _ in range(2)]
    k.h_shared = [put(FM, BW) for _ in range(2)]
    k.silu_shared = [put(BW) for _ in range(2)]
    k.routing_at = put.at
    k.xe = [put(ST, D) for _ in range(2)]
    k.xet, k.he, k.silu_e = put(KT, CAP), put(FM, CAP), put(FM, CAP)
    k.ye = [put(ST, D) for _ in range(2)]
    tiny = Place(k.small, 0, SMALL)
    k.weight = [tiny(NT) for _ in range(2)]
    k.take, k.give = ([tiny(NT).bitcast(U32) for _ in range(2)] for _ in range(2))
    k.tiny_at = tiny.at


def shared_tasks(n):
    return [(what, n, m) for m in range(FM) for what in "gu"], [("down", n, i) for i in range(BT)]


def shared_up(k, pe, inner, n, m):
    up, _ = weights(k.w_shared)
    for h, what in enumerate("gu"):
        inner.free(pe, (what, n, m))
        for j in range(KT):
            lo = h * FI + m * P
            mm = pe.matmul(k.ps[0:FROWS[m], inner.bank((what, n, m)), :], up[:, j, lo:lo + FROWS[m]],
                           k.x2nt[n][:, j, :], start=(j == 0), stop=(j == KT - 1))
        mm.then_inc(inner.filled, 1)


def shared_down(k, pe, outer, n, i, h_out, q):
    _, down = weights(k.w_shared)
    outer.free(pe, ("down", n, i))
    for m in range(FM):
        if i == 0:
            pe.wait_ge(h_out, q + m + 1)
        mm = pe.matmul(k.ps[:, outer.bank(("down", n, i)), :], k.h_shared[n % 2][0:FROWS[m], m, i * P:(i + 1) * P],
                       down[0:FROWS[m], m, :], start=(m == 0), stop=(m == FM - 1))
    mm.then_inc(outer.filled, 1)


def shared_silu(k, act, inner, n, m, s, q):
    if q >= 2:
        act.wait_ge(s["h_out"], q - 1)
    inner.full(act, ("g", n, m))
    r = FROWS[m]
    act.activation(k.silu_shared[q % 2][0:r, :], k.ps[0:r, inner.bank(("g", n, m)), :],
                   ACT.Silu).then_inc(s["silu_out"], 1)
    act.wait_ge(s["silu_out"], q + 1)
    act.sem_inc(inner.empty(("g", n, m)), 1)


def shared_hidden(k, dve, inner, n, m, s, q):
    r = FROWS[m]
    inner.full(dve, ("u", n, m))
    dve.wait_ge(s["silu_out"], q + 1)
    dve.tensor_tensor(k.h_shared[n % 2][0:r, m, :], k.ps[0:r, inner.bank(("u", n, m)), :],
                      k.silu_shared[q % 2][0:r, :], ALU.mult).then_inc(s["h_out"], 1)
    dve.wait_ge(s["h_out"], q + 1)
    dve.sem_inc(inner.empty(("u", n, m)), 1)


def shared_add(k, dve, outer, n, i):
    x = k.rows[:, n * BT + i, 0:D]
    outer.full(dve, ("down", n, i))
    dve.tensor_tensor(x, k.ps[:, outer.bank(("down", n, i)), :], x, ALU.add).then_inc(outer.empty(("down", n, i)), 1)


def route_and_shared(k):
    nc, io, ps, rows = k.nc, k.io, k.ps, k.rows
    put = Place(k.arena, k.routing_at, k.arena_size)
    logit_rows, gate_b = put(T), put(NE)
    E_ = NT * NE
    x, ab, ex, u, d, z, ln, score, biased, eq, first, second, m, pos, tmp, tmp2 = (put(E_) for _ in range(16))
    tiny = Place(k.small, k.tiny_at, SMALL)
    best, which, total = tiny(NT), tiny(NT), tiny(NT)
    at, es, ok = tiny(NT), tiny(NT), tiny(NT)

    def te(a):
        return a.rearrange("p (t e) -> p t e", e=NE)

    turn_tasks = [("x2T", NB - 1, j) for j in range(KT)] + [("logitsT",)]
    outer_tasks = []
    for n in range(NB - 1):
        inner_n, outer_n = shared_tasks(n)
        turn_tasks += inner_n
        outer_tasks += outer_n + ([("before",)] if n == 0 else [])
    inner = Ring(k.sem, "inner", [4, 5, 6, 7], turn_tasks)
    outer = Ring(k.sem, "outer", [1, 2, 3, 0], outer_tasks)
    s = sems(k, "route", """bias_in logits_full logits_out rows_out silu_out h_out abs_in exp_out ln_in ln_out root_in
             root_out chosen""")
    dve_done, act_done = k.chain["dve"], k.chain["act"]

    with nc.Block() as block:

        @block.sync
        def _(sp):
            sp.dma_start(gate_b, io["gate_b"].partition_broadcast(P)).then_inc(s["bias_in"], 16)
            for e in range(2):
                sp.dma_start(k.w_expert[e], io["w_expert"][e]).then_inc(k.w_in[e], 16)
            sp.wait_ge(k.given, 16 * 2 * NT)
            for e in range(2):
                sp.dma_start(k.xe[e], k.expert_in[e * CAP:(e + 1) * CAP, :].rearrange("(a p) d -> p a d", p=P)
                             ).then_inc(k.xe_in[e], 16)

        @block.tensor
        def _(pe):
            turn_rows(k, pe, inner, NB - 1)
            logits(k, pe, inner, NB - 1).then_inc(s["logits_full"], 1)
            inner.free(pe, ("logitsT",))
            for t in range(NT):
                if t % BT == 0:
                    pe.wait_ge(s["logits_out"], t // BT + 1)
                mm = pe.transpose(ps[:, inner.bank(("logitsT",)), t * NE:(t + 1) * NE],
                                  logit_rows[0:NE, t * P:(t + 1) * P], c(k, "ident")[0:NE, 0:NE])
            mm.then_inc(inner.filled, 1)
            pe.wait_ge(k.s_shared, 16)
            for n in range(NB - 1):
                for m_ in range(FM):
                    if (n, m_) == (1, 2):
                        pe.wait_ge(s["chosen"], 1)
                        outer.free(pe, ("before",))
                        b = ps[:, outer.bank(("before",)), :]
                        pe.matmul(b[:, 0:E_], c(k, "before"), m, start=True, stop=True)
                        pe.matmul(b[:, E_:2 * E_], c(k, "ones"), m, start=True, stop=True).then_inc(outer.filled, 1)
                    shared_up(k, pe, inner, n, m_)
                if n == 0:
                    pe.wait_ge(s["abs_in"], 1)
                for i in range(BT):
                    shared_down(k, pe, outer, n, i, s["h_out"], n * FM)

        @block.scalar
        def _(act):
            for j in range(KT):
                keep_turned(k, act, inner, NB - 1, j)
            for n in range(NB):
                if n == NB - 1:
                    act.wait_ge(s["logits_full"], 1)
                act.activation(logit_rows[0:NE, n * BW:(n + 1) * BW], ps[0:NE, n, :],
                               ACT.Copy).then_inc(s["logits_out"], 1)
            act.wait_ge(s["abs_in"], 1)
            act_done(act, act.activation(ab, x, ACT.Abs))
            act.activation(ex, ab, ACT.Exp, scale=-1.0).then_inc(s["exp_out"], 1)
            for n in range(NB - 1):
                for m_ in range(FM):
                    q = n * FM + m_
                    if q == 1:
                        act.wait_ge(s["ln_in"], 1)
                        act.activation(ln, u, ACT.Ln).then_inc(s["ln_out"], 1)
                    if q == 2:
                        act.wait_ge(s["root_in"], 1)
                        act.activation(score, tmp, ACT.Sqrt).then_inc(s["root_out"], 1)
                    shared_silu(k, act, inner, n, m_, s, q)

        @block.gpsimd
        def _(pool):
            for slot in range(2):
                pool.wait_ge(s["rows_out"], slot + 1)
                for t in range(NT):
                    pool.indirect_dma_start(
                        out=k.expert_in[:, :],
                        out_offset=bass.IndirectOffsetOnAxis(ap=k.give[slot][:, t:t + 1], axis=0),
                        in_=rows[:, t, D:2 * D], in_offset=None, bounds_check=NE * CAP - 1,
                        oob_is_err=False).then_inc(k.given, 16)

        @block.vector
        def _(dve):
            def done(ins):
                dve_done(dve, ins)

            def per_token(a):
                return wide(a, NE)

            def per_expert(a):
                return a.unsqueeze(1).to_broadcast((P, NT, NE))

            def hidden(n, m_):
                shared_hidden(k, dve, inner, n, m_, s, n * FM + m_)

            def add_shared(n, i):
                shared_add(k, dve, outer, n, i)

            def choose(slot, onehot):
                done(dve.tensor_reduce(best, te(biased), AX.X, ALU.max))
                done(dve.tensor_tensor(te(eq), te(biased), per_token(best), ALU.is_equal))
                done(dve.tensor_tensor(te(eq), te(eq), per_expert(c(k, "rank")), ALU.mult))
                done(dve.tensor_reduce(which, te(eq), AX.X, ALU.max))
                done(dve.tensor_tensor(te(onehot), te(eq), per_token(which), ALU.is_equal))
                if slot == 0:
                    done(dve.scalar_tensor_tensor(biased, onehot, -3.0e38, biased, ALU.mult, ALU.add))
                done(dve.tensor_tensor(tmp, score, onehot, ALU.mult))
                done(dve.tensor_reduce(k.weight[slot], te(tmp), AX.X, ALU.add))

            def give(slot, onehot):
                done(dve.tensor_tensor(tmp, pos, onehot, ALU.mult))
                done(dve.tensor_reduce(at, te(tmp), AX.X, ALU.add))
                done(dve.tensor_tensor(te(tmp), te(onehot), per_expert(c(k, "expert")), ALU.mult))
                done(dve.tensor_reduce(es, te(tmp), AX.X, ALU.add))
                done(dve.tensor_scalar(ok, at, float(CAP), None, ALU.is_lt))
                done(dve.tensor_tensor(at, at, ok, ALU.mult))
                done(dve.tensor_tensor(k.weight[slot], k.weight[slot], ok, ALU.mult))
                done(dve.scalar_tensor_tensor(at, es, float(CAP), at, ALU.mult, ALU.add))
                done(dve.tensor_copy(k.take[slot], at))
                done(dve.tensor_scalar(ok, ok, -2.0 * NE * CAP, 2.0 * NE * CAP, ALU.mult, ALU.add))
                done(dve.tensor_tensor(at, at, ok, ALU.add))
                done(dve.tensor_copy(k.give[slot], at))
                dve.sem_inc(s["rows_out"], 1)

            inner.full(dve, ("logitsT",))
            dve.tensor_copy(x, ps[:, inner.bank(("logitsT",)), 0:E_]).then_inc(s["abs_in"], 1)
            dve.wait_ge(s["abs_in"], 1)
            dve.sem_inc(inner.empty(("logitsT",)), 1)
            dve.wait_ge(s["exp_out"], 1)
            dve.tensor_scalar(u, ex, 1.0, None, ALU.add).then_inc(s["ln_in"], 1)
            dve.wait_ge(s["ln_in"], 1)
            hidden(0, 0)
            done(dve.tensor_scalar(d, u, -1.0, None, ALU.add))
            done(dve.tensor_scalar(z, d, 0.0, None, ALU.is_equal))
            done(dve.tensor_tensor(d, d, z, ALU.add))
            done(dve.reciprocal(tmp2, d))
            done(dve.tensor_tensor(tmp2, tmp2, ex, ALU.mult))
            done(dve.tensor_tensor(z, z, ex, ALU.mult))
            dve.wait_ge(s["ln_out"], 1)
            done(dve.tensor_tensor(tmp2, tmp2, ln, ALU.mult))
            done(dve.tensor_tensor(tmp2, tmp2, z, ALU.add))
            dve.scalar_tensor_tensor(tmp, x, 0.0, tmp2, ALU.max, ALU.add).then_inc(s["root_in"], 1)
            dve.wait_ge(s["root_in"], 1)
            hidden(0, 1)
            dve.wait_ge(s["root_out"], 1)
            done(dve.tensor_scalar(tmp2, score, 1e-30, None, ALU.max))
            done(dve.reciprocal(tmp2, tmp2))
            done(dve.tensor_tensor(tmp, tmp, tmp2, ALU.mult))
            done(dve.tensor_tensor(tmp, tmp, score, ALU.add))
            done(dve.tensor_scalar(score, tmp, 0.5, None, ALU.mult))
            dve.wait_ge(s["bias_in"], 16)
            done(dve.tensor_tensor(te(biased), te(score), per_expert(gate_b), ALU.add))
            hidden(0, 2)
            choose(0, first)
            for i in range(BT):
                add_shared(0, i)
            hidden(1, 0)
            choose(1, second)
            dve.tensor_tensor(m, first, second, ALU.add).then_inc(s["chosen"], 1)
            done(dve.tensor_tensor(total, k.weight[0], k.weight[1], ALU.add))
            done(dve.reciprocal(total, total))
            for slot in range(2):
                done(dve.tensor_tensor(k.weight[slot], k.weight[slot], total, ALU.mult))
            hidden(1, 1)
            outer.full(dve, ("before",))
            b = ps[:, outer.bank(("before",)), :]
            within, whole = b[:, 0:E_], b[:, E_:2 * E_]
            done(dve.tensor_copy(tmp.rearrange("p (e t) -> p t e", t=NT), te(whole)))
            done(dve.tensor_tensor_scan(tmp2, c(k, "restart"), tmp, 0.0, ALU.mult, ALU.add))
            done(dve.tensor_tensor(tmp2, tmp2, tmp, ALU.subtract))
            dve.tensor_tensor(te(pos), te(within), tmp2.rearrange("p (e t) -> p t e", t=NT),
                              ALU.add).then_inc(outer.empty(("before",)), 1)
            dve.wait_ge(outer.empty(("before",)), outer.at[("before",)] // 4 + 1)
            give(0, first)
            hidden(1, 2)
            give(1, second)
            for i in range(BT):
                add_shared(1, i)
            for n in range(2, NB - 1):
                for m_ in range(FM):
                    hidden(n, m_)
                for i in range(BT):
                    add_shared(n, i)


def experts(k):
    nc, io, ps = k.nc, k.io, k.ps
    s = sems(k, "expert", "turned xt_out gu_full silu_out h_out down_full y_used")
    last_block = NB - 1
    inner_tasks, outer_tasks = shared_tasks(last_block)
    inner = Ring(k.sem, "last_inner", [4, 5, 6, 7], inner_tasks)
    outer = Ring(k.sem, "last_outer", [3, 0, 1, 2], outer_tasks)
    shared = sems(k, "last_shared", "silu_out h_out")
    y_stored = k.y_stored
    turn_bank, up_bank, down_bank = (4, 5), (6, 7, 0), (1, 2)
    pairs = NE // 2

    def each_pair(eng, body):
        with eng.Fori(0, pairs - 1) as it:
            body(it, 0, False)
            body(it, 1, False)
        body(pairs - 1, 0, False)
        body(pairs - 1, 1, True)

    with nc.Block() as block:

        @block.sync
        def _(sp):
            sp.dma_start(k.xnt[:, 0:3 * KT * D], io["w_attention"][:, 0:3 * KT * D]).then_inc(k.attention_in, 16)
            with sp.Fori(0, pairs - 1) as it:
                for p in range(2):
                    e = it * 2 + (p + 2)
                    sp.wait_ge(s["turned"], it * 4 + 2 * (p + 1))
                    sp.dma_start(k.xe[p], k.expert_in.rearrange("(e a p) d -> e p a d", p=P, a=ST)[e]
                                 ).then_inc(k.xe_in[p], 16)
                    sp.wait_ge(s["down_full"], it * 4 + 2 * (p + 1))
                    sp.dma_start(k.w_expert[p], io["w_expert"][e]).then_inc(k.w_in[p], 16)
            for p in range(2):
                sp.wait_ge(k.y_stored[p], 16 * (NE // 2 + 1))
            for to, what in ((k.b_k, "b_k"), (k.b_v, "b_v"), (k.b_o, "b_o"), (k.decay_row, "decay_row")):
                sp.dma_start(to, io[what].partition_broadcast(P)).then_inc(k.combined["biases_in"], 16)
            sp.dma_start(k.b_q, io["b_q"]).then_inc(k.combined["biases_in"], 16)

        @block.gpsimd
        def _(pool):
            for p in range(2):
                pool.wait_ge(k.y_stored[p], 16 * (NE // 2 + 1))
            take(k, pool, 0)
            norm_scale(k, pool, 0)

        @block.tensor
        def _(pe):
            ident = c(k, "ident")

            def turn(p):
                for a in range(ST):
                    for j in range(KT):
                        mm = pe.transpose(ps[:, turn_bank[a], j * P:(j + 1) * P],
                                          k.xe[p][:, a, j * P:(j + 1) * P], ident)
                    mm.then_inc(s["turned"], 1)

            def body(it, p, last):
                up, down = weights(k.w_expert[p])
                pe.wait_ge(k.w_in[p], it * 16 + 16)
                pe.wait_ge(s["xt_out"], it * 4 + 2 * (p + 1))
                for m in range(FM):
                    for h in range(2):
                        for j in range(KT):
                            lo = h * FI + m * P
                            mm = pe.matmul(ps[0:FROWS[m], up_bank[m], h * CAP:(h + 1) * CAP],
                                           up[:, j, lo:lo + FROWS[m]], k.xet[:, j, :],
                                           start=(j == 0), stop=(j == KT - 1))
                    mm.then_inc(s["gu_full"], 1)
                if not last:
                    pe.wait_ge(k.xe_in[1 - p], it * 16 + (16 if p == 0 else 32))
                    turn(1 - p)
                for a in range(ST):
                    pe.wait_ge(s["y_used"], it * 4 + 2 * p + a + 1)
                    for m in range(FM):
                        if a == 0:
                            pe.wait_ge(s["h_out"], it * 6 + 3 * p + m + 1)
                        mm = pe.matmul(ps[:, down_bank[a], :], k.he[0:FROWS[m], m, a * P:(a + 1) * P],
                                       down[0:FROWS[m], m, :], start=(m == 0), stop=(m == FM - 1))
                    mm.then_inc(s["down_full"], 1)

            pe.wait_ge(k.xe_in[0], 16)
            turn(0)
            each_pair(pe, body)
            for m in range(FM):
                shared_up(k, pe, inner, last_block, m)
            pe.wait_ge(s["y_used"], ST * (NE + 1))
            for i in range(BT):
                shared_down(k, pe, outer, last_block, i, shared["h_out"], 0)

        @block.scalar
        def _(act):
            act.sem_inc(s["y_used"], ST)
            for p in range(2):
                act.sem_inc(y_stored[p], 16)

            def xt(count, a):
                act.wait_ge(s["turned"], count)
                act.activation(k.xet[:, :, a * P:(a + 1) * P],
                               ps[:, turn_bank[a], :].rearrange("p (a b) -> p a b", b=P),
                               ACT.Copy).then_inc(s["xt_out"], 1)

            def body(it, p, last):
                for m in range(FM):
                    act.wait_ge(s["gu_full"], it * 6 + 3 * p + m + 1)
                    r = FROWS[m]
                    act.activation(k.silu_e[0:r, m, :], ps[0:r, up_bank[m], 0:CAP],
                                   ACT.Silu).then_inc(s["silu_out"], 1)
                if not last:
                    for a in range(ST):
                        xt(it * 4 + 2 * (p + 1) + a + 1, a)
                act.wait_ge(y_stored[p], it * 16 + 16)
                for a in range(ST):
                    act.wait_ge(s["down_full"], it * 4 + 2 * p + a + 1)
                    act.activation(k.ye[p][:, a, :], ps[:, down_bank[a], :], ACT.Copy).then_inc(s["y_used"], 1)
                act.wait_ge(s["y_used"], it * 4 + 2 * p + 2 * ST)
                e = it * 2 + p
                act.dma_start(k.expert_out.rearrange("(e a p) d -> e p a d", p=P, a=ST)[e], k.ye[p]
                              ).then_inc(y_stored[p], 16)

            for a in range(ST):
                xt(a + 1, a)
            each_pair(act, body)
            for m in range(FM):
                shared_silu(k, act, inner, last_block, m, shared, m)

        @block.vector
        def _(dve):
            def body(it, p, last):
                for m in range(FM):
                    r = FROWS[m]
                    dve.wait_ge(s["silu_out"], it * 6 + 3 * p + m + 1)
                    dve.tensor_tensor(k.he[0:r, m, :], ps[0:r, up_bank[m], CAP:2 * CAP], k.silu_e[0:r, m, :],
                                      ALU.mult).then_inc(s["h_out"], 1)

            each_pair(dve, body)
            for m in range(FM):
                shared_hidden(k, dve, inner, last_block, m, shared, m)
                if m:
                    for i in range(2 * (m - 1), 2 * m):
                        combine(k, dve, i)
            normalise(k, dve, 0)
            for i in range(BT):
                shared_add(k, dve, outer, last_block, i)


def attention_memory(k):
    k.w_attn = [k.xnt[:, i * KT * D:(i + 1) * KT * D].rearrange("p (a b) -> p a b", b=D) for i in range(4)]
    put = Place(k.arena, 0, k.arena_size)
    k.qt, k.vk, k.ksum = put(KT, T), put(KT, P), put(KT, P)
    k.attention_at = put.at
    k.taken = [put(D) for _ in range(8)]
    k.x3nt = [put(KT, BW) for _ in range(2)]
    k.k_biased, k.kt, k.vt, k.k_total = put(D), put(2, D), put(2, D), put(D)
    k.b_k, k.b_v, k.b_o, k.decay_row = put(D), put(D), put(D), put(T)
    tiny = Place(k.small, k.tiny_at, SMALL)
    k.stats, k.mv, k.rstd, k.ve, k.b_q = tiny(BT, 6), tiny(BT, 2), tiny(BT), tiny(BT), tiny(KT)
    k.combined = sems(k, "combined", "biases_in taken_used ln_stats ln_rstd ln_out")
    k.taken_in = [k.sem(f"taken_in{i}") for i in range(8)]


def take(k, pool, n):
    for i in range(BT):
        for slot in range(2):
            q = (n * BT + i) * 2 + slot
            if q >= 8:
                pool.wait_ge(k.combined["taken_used"], q - 7)
            pool.indirect_dma_start(
                out=k.taken[q % 8], out_offset=None, in_=k.expert_out[:, :],
                in_offset=bass.IndirectOffsetOnAxis(ap=k.take[slot][:, n * BT + i:n * BT + i + 1], axis=0),
                bounds_check=NE * CAP - 1, oob_is_err=False).then_inc(k.taken_in[q % 8], 16)


def norm_scale(k, pool, n):
    pool.wait_ge(k.combined["ln_stats"], n + 1)
    k.chain["pool"](pool, pool.tensor_scalar(k.ve, k.mv[:, :, 1], 1.0, 1e-5, ALU.mult, ALU.add))
    pool.tensor_tensor(k.rstd, k.ve, c(k, "neghalf")[:, 0:BT], ALU.pow).then_inc(k.combined["ln_rstd"], 1)


def combine(k, dve, t):
    x, i = k.rows[:, t, 0:D], t % BT
    for slot in range(2):
        q = 2 * t + slot
        dve.wait_ge(k.taken_in[q % 8], 16 * (q // 8 + 1))
        dve.scalar_tensor_tensor(x, k.taken[q % 8], k.weight[slot][:, t:t + 1], x, ALU.mult,
                                 ALU.add).then_inc(k.combined["taken_used"], 1)
        dve.wait_ge(k.combined["taken_used"], q + 1)
    k.chain["dve"](dve, dve.bn_stats(k.stats[:, i, :], x))
    ins = dve.bn_aggr(k.mv[:, i, :], k.stats[:, i, :])
    if i == BT - 1:
        ins.then_inc(k.combined["ln_stats"], 1)


def normalise(k, dve, n):
    dve.wait_ge(k.combined["ln_rstd"], n + 1)
    for i in range(BT):
        t = n * BT + i
        ins = dve.tensor_scalar(k.rows[:, t, D:2 * D], k.rows[:, t, 0:D], k.mv[:, i, 0:1], k.rstd[:, i:i + 1],
                                ALU.subtract, ALU.mult)
    ins.then_inc(k.combined["ln_out"], 1)


def linear_attention_sums(k):
    nc, io, ps, rows = k.nc, k.io, k.ps, k.rows
    w_q, w_k, w_v, _ = k.w_attn
    xnt, k_biased, kt, vt, decay_row, b_q = k.x3nt, k.k_biased, k.kt, k.vt, k.decay_row, k.b_q
    b_k, b_v, b_o = k.b_k, k.b_v, k.b_o

    tasks = []
    for n in range(NB):
        tasks += [("xT", n, j) for j in range(KT)] + [("Q", n, m) for m in range(KT)]
        for i in range(BT):
            tasks += [("K", n, i), ("V", n, i)]
    ring = Ring(k.sem, "sums", [2, 3, 4, 5, 6, 7], tasks)
    k_total = k.k_total
    s = sems(k, "sums", "kb_out k_out v_out kv_used q_out zeroed k_added k_full")
    s.update(k.combined)
    dve_done, pool_done = k.chain["dve"], k.chain["pool"]

    def bank(task):
        return ps[:, ring.bank(task), :]

    with nc.Block() as block:

        @block.sync
        def _(sp):
            sp.dma_start(k.xnt[:, 3 * KT * D:4 * KT * D], io["w_attention"][:, 3 * KT * D:4 * KT * D]
                         ).then_inc(k.wo_in, 16)

        @block.gpsimd
        def _(pool):
            pool.memset(k.vk, 0.0).then_inc(s["zeroed"], 1)
            pool.memset(k.ksum, 0.0).then_inc(s["zeroed"], 1)
            pool.memset(k_total, 0.0).then_inc(s["zeroed"], 1)
            for n in range(NB):
                if n == 0:
                    pool.wait_ge(s["biases_in"], 16 * 5)
                if n + 1 < NB:
                    take(k, pool, n + 1)
                pool.wait_ge(s["ln_out"], n + 1)
                for i in range(BT):
                    x = rows[:, n * BT + i, 0:D]
                    pool.tensor_tensor(x, x, b_o, ALU.add)
                for m in range(KT):
                    pool.wait_ge(s["q_out"], n * KT + m + 1)
                    q = k.qt[:, m, n * BW:(n + 1) * BW]
                    pool.tensor_tensor(q, q, decay_row[:, n * BW:(n + 1) * BW], ALU.mult)
                if n + 1 < NB:
                    norm_scale(k, pool, n + 1)
                for i in range(BT):
                    t = n * BT + i
                    pool.wait_ge(s["k_out"], t + 1)
                    if t:
                        pool.wait_ge(s["k_added"], t)
                    else:
                        pool.wait_ge(s["zeroed"], 3)
                    pool.tensor_tensor(k_total, k_total, kt[:, t % 2, :], ALU.add).then_inc(s["k_added"], 1)

        @block.scalar
        def _(act):
            for n in range(NB):
                for j in range(KT):
                    ring.full(act, ("xT", n, j))
                    act.activation(xnt[n % 2][:, j, :], bank(("xT", n, j)),
                                   ACT.Copy).then_inc(ring.empty(("xT", n, j)), 1)
                if n == 0:
                    act.wait_ge(s["biases_in"], 16 * 5)
                for m in range(KT):
                    ring.full(act, ("Q", n, m))
                    act.activation(k.qt[:, m, n * BW:(n + 1) * BW], bank(("Q", n, m)), ACT.Relu,
                                   bias=b_q[:, m:m + 1]).then_inc(s["q_out"], 1)
                    act.wait_ge(s["q_out"], n * KT + m + 1)
                    act.sem_inc(ring.empty(("Q", n, m)), 1)
                for i in range(BT):
                    t = n * BT + i
                    act.wait_ge(s["kb_out"], t + 1)
                    if t >= 2:
                        act.wait_ge(s["kv_used"], t - 1)
                        act.wait_ge(s["k_added"], t - 1)
                    act.activation(kt[:, t % 2, :], k_biased, ACT.Relu,
                                   scale=c(k, "decay")[:, t:t + 1]).then_inc(s["k_out"], 1)

        @block.tensor
        def _(pe):
            ident = c(k, "ident")

            def add_tile(t):
                pe.wait_ge(s["k_out"], t + 1)
                pe.wait_ge(s["v_out"], t + 1)
                for m in range(KT):
                    r = slice(m * P, (m + 1) * P)
                    mm = pe.matmul(ps[:, 0, r], vt[:, t % 2, r], kt[:, t % 2, r], start=(t == 0 and m == 0),
                                   stop=(t == NT - 1), skip_group_check=True)
                mm.then_inc(s["kv_used"], 1)

            pe.wait_ge(k.attention_in, 16)
            for n in range(NB):
                pe.wait_ge(s["ln_out"], n + 1)
                for j in range(KT):
                    ring.free(pe, ("xT", n, j))
                    for i in range(BT):
                        mm = pe.transpose(bank(("xT", n, j))[:, i * P:(i + 1) * P],
                                          rows[:, n * BT + i, D + j * P:D + (j + 1) * P], ident)
                    mm.then_inc(ring.filled, 1)
                if n:
                    add_tile(n * BT - 1)
                for m in range(KT):
                    ring.free(pe, ("Q", n, m))
                    for j in range(KT):
                        if m == 0:
                            pe.wait_ge(ring.empty(("xT", n, j)), ring.at[("xT", n, j)] // 6 + 1)
                        mm = pe.matmul(bank(("Q", n, m)), w_q[:, j, m * P:(m + 1) * P], xnt[n % 2][:, j, :],
                                       start=(j == 0), stop=(j == KT - 1))
                    mm.then_inc(ring.filled, 1)
                for i in range(BT):
                    for what, w in (("K", w_k), ("V", w_v)):
                        ring.free(pe, (what, n, i))
                        for j in range(KT):
                            mm = pe.matmul(bank((what, n, i)), xnt[n % 2][:, j, i * P:(i + 1) * P], w[:, j, :],
                                           start=(j == 0), stop=(j == KT - 1))
                        mm.then_inc(ring.filled, 1)
                    if i:
                        add_tile(n * BT + i - 1)
            add_tile(NT - 1)
            pe.wait_ge(s["k_added"], NT)
            for m in range(KT):
                mm = pe.matmul(ps[:, 1, m * DK:(m + 1) * DK], k_total[:, m * P:(m + 1) * P],
                               c(k, "ones")[:, 0:DK], start=(m == 0), stop=True, skip_group_check=True)
            mm.then_inc(s["k_full"], 1)

        @block.vector
        def _(dve):
            def done(ins):
                dve_done(dve, ins)

            def combine_and_norm(n):
                for i in range(BT):
                    combine(k, dve, n * BT + i)
                normalise(k, dve, n)

            dve.wait_ge(s["biases_in"], 16 * 5)
            for n in range(NB):
                if n + 1 < NB:
                    combine_and_norm(n + 1)
                for i in range(BT):
                    t = n * BT + i
                    ring.full(dve, ("K", n, i))
                    if t:
                        dve.wait_ge(s["k_out"], t)
                    dve.tensor_tensor(k_biased, bank(("K", n, i)), b_k, ALU.add).then_inc(s["kb_out"], 1)
                    dve.wait_ge(s["kb_out"], t + 1)
                    dve.sem_inc(ring.empty(("K", n, i)), 1)
                    ring.full(dve, ("V", n, i))
                    if t >= 2:
                        dve.wait_ge(s["kv_used"], t - 1)
                    dve.tensor_tensor(vt[:, t % 2, :], bank(("V", n, i)), b_v, ALU.add).then_inc(s["v_out"], 1)
                    dve.wait_ge(s["v_out"], t + 1)
                    dve.sem_inc(ring.empty(("V", n, i)), 1)
            dve.wait_ge(s["kv_used"], NT)
            dve.wait_ge(s["k_full"], 1)
            dve.wait_ge(s["zeroed"], 3)
            vk = ps[:, 0, :].rearrange("p (a b) -> p a b", b=P)
            ksum = ps[:, 1, 0:KT * DK].rearrange("p (a b) -> p a b", b=DK)
            for g in range(4):
                r = slice(g * DK, (g + 1) * DK)
                dve.tensor_copy(k.vk[r, :, r], vk[r, :, r])
                dve.tensor_copy(k.ksum[r, :, r], ksum[r, :, :])


def linear_attention(k):
    nc, io, ps, rows = k.nc, k.io, k.ps, k.rows
    w_o = k.w_attn[3]
    put = Place(k.arena, k.attention_at, k.arena_size)
    out_t = [put(KT, BW) for _ in range(2)]
    free = Place(k.xnt, 0, 3 * KT * D)
    den = [free(KT, BW), free(KT, BW)]
    guess, product, inv = [free(KT, BW), put(KT, BW)], put(2, BW), put(2, BW)
    kvo, router, junk, diagonal, base = put(KT, D), put(D), put(D), put(BT, P), put(2, D)
    onehot = [put(SEL // 2).bitcast(BF16) for _ in range(4)]
    number = put(NT).bitcast(BF16).rearrange("p (a b) -> p a b", b=2)
    compared = {"dve": [put(BW // 2).bitcast(BF16) for _ in range(8)],
                "act": [put(BW // 2).bitcast(BF16) for _ in range(4)]}
    sign = put(2, BW // 2)
    tiny = Place(k.small, 0, k.token_at)
    stats, mv, rstd, ve, shift = tiny(BT, 6), tiny(BT, 2), tiny(BT), tiny(BT), tiny(BT)
    chosen, total, place, past = tiny(NT), tiny(NT), tiny(NT), tiny(NT)
    found = tiny(ST)
    PARTS = NB + 1
    one, tied = put(1).bitcast(BF16)[:, 0:1], put(P)

    on_scalar = (0, BT, 2 * BT, 0)

    def comparisons(n):
        return ([("act" if u < on_scalar[n] else "dve", u, n * BW, (n + 1) * BW, False) for u in range(n * BT)] +
                [("dve", u, u * P, (n + 1) * BW, True) for u in range(n * BT, (n + 1) * BT - 1)])

    def numbered(n, engine):
        before = sum(which == engine for i in range(n) for which, *_ in comparisons(i))
        mine = [rest for which, *rest in comparisons(n) if which == engine]
        return [(before + j, *rest) for j, rest in enumerate(mine)]

    def all_of(engine):
        return sum(which == engine for n in range(NB) for which, *_ in comparisons(n))

    higher, ahead = tiny(NT, PARTS), tiny(NT)

    tasks = []
    tasks += [("den", 0, m) for m in range(KT)] + [("kvo", m) for m in range(KT)]
    after = {(0, 0): [(1, 0), (1, 1)], (0, 1): [(1, 2), (1, 3)], (0, 2): [(2, 0), (2, 1)], (0, 3): [(2, 2), (2, 3)]}
    after.update({(1, i): [(3, i)] for i in range(BT)})
    for n in range(NB):
        for i in range(BT):
            tasks += [("out", n, i)] + [("den", *which) for which in after.get((n, i), [])]
    ring = Ring(k.sem, "attention", [5, 6, 7], tasks)
    s = sems(k, "attention", """router_in den_out ln_out guess_out product_out inverse_out out_t kvo_out ln_stats
             ln_rstd shift_out norm_out score_out diagonal_out broadcast chosen placed place_out onehot_out found
             number_out base_out sign_out bank_read""")
    k.rows_stored = k.sem("rows_stored")
    compared_out, counted = ({e: k.sem(f"{what}_{e}") for e in ("dve", "act")} for what in ("compared", "counted"))
    dve_done, act_done, pool_done = k.chain["dve"], k.chain["act"], k.chain["pool"]

    spread_scores = ps.rearrange("p a b -> p (a b)")[:, 0:T]

    def bank(task):
        return ps[:, ring.bank(task), :]

    with nc.Block() as block:

        @block.sync
        def _(sp):
            sp.dma_start(router, io["w_router"].partition_broadcast(P)).then_inc(s["router_in"], 16)
            for n in range(NB):
                sp.wait_ge(s["score_out"], (n + 1) * BT)
                sp.dma_start(k.kept.rearrange("(t p) d -> p t d", p=P)[:, n * BT:(n + 1) * BT, :],
                             rows[:, n * BT:(n + 1) * BT, :]).then_inc(k.rows_stored, 16)
                for i in range(BT):
                    t = n * BT + i
                    sp.wait_ge(s["base_out"], t + 1)
                    sp.dma_start(io["out"][t * P:(t + 1) * P, :], base[:, t % 2, :]).then_inc(k.base_in[t % 2], 16)
            for i in range(2):
                sp.wait_ge(k.base_in[i], 16 * (NT // 2))

        @block.gpsimd
        def _(pool):
            pool.tensor_copy(number, c(k, "number").rearrange("p (a b) -> p a b", b=2)).then_inc(s["number_out"], 1)

            def bases(n):
                for i in range(BT):
                    t = n * BT + i
                    pool.wait_ge(s["norm_out"], t + 1)
                    if t >= 2:
                        pool.wait_ge(k.base_in[t % 2], 16 * (t // 2))
                    pool.tensor_tensor(base[:, t % 2, :], rows[:, t, 0:D], rows[:, t, D:2 * D],
                                       ALU.add).then_inc(s["base_out"], 1)

            def product_of(n, m):
                q = n * KT + m
                pool.wait_ge(s["guess_out"], q + 1)
                if q >= 2:
                    pool.wait_ge(s["inverse_out"], q - 1)
                pool.tensor_tensor(product[:, q % 2, :], den[n % 2][:, m, :], guess[n % 2][:, m, :],
                                   ALU.mult).then_inc(s["product_out"], 1)

            def quotient(n, m):
                pool.wait_ge(s["inverse_out"], n * KT + m + 1)
                if n >= 2:
                    ring.full(pool, ("out", n - 2, BT - 1))
                pool.tensor_tensor(out_t[n % 2][:, m, :], inv[:, m % 2, :], k.qt[:, m, n * BW:(n + 1) * BW],
                                   ALU.mult).then_inc(s["out_t"], 1)

            for n in range(NB + 1):
                if n < 2:
                    for m in range(KT):
                        product_of(n, m)
                elif n < NB:
                    product_of(n, 0)
                    for m in range(1, KT):
                        product_of(n, m)
                        quotient(n, m - 1)
                    quotient(n, KT - 1)
                if n:
                    pool.wait_ge(s["ln_stats"], n)
                    pool_done(pool, pool.tensor_scalar(ve, mv[:, :, 1], 1.0, 1e-5, ALU.mult, ALU.add))
                    pool.tensor_tensor(rstd, ve, c(k, "neghalf")[:, 0:BT], ALU.pow).then_inc(s["ln_rstd"], 1)
                if n >= 2:
                    bases(n - 2)
            bases(NB - 1)

        @block.scalar
        def _(act):
            def norm(n):
                act.wait_ge(s["shift_out"], n + 1)
                for i in range(BT):
                    t = n * BT + i
                    act.activation(rows[:, t, D:2 * D], rows[:, t, 0:D], ACT.Identity, bias=shift[:, i:i + 1],
                                   scale=rstd[:, i:i + 1]).then_inc(s["norm_out"], 1)

            def diagonals(n):
                for i in range(BT):
                    t = n * BT + i
                    act.wait_ge(s["score_out"], t + 1)
                    if n:
                        act.wait_ge(s["broadcast"], t - BT + 1)
                    act.activation(diagonal[:, i, :], c(k, "ident"), ACT.Copy,
                                   scale=rows[:, t, 2 * D:2 * D + 1]).then_inc(s["diagonal_out"], 1)

            def guesses(n):
                for m in range(KT):
                    q = n * KT + m
                    if n >= 2:
                        act.wait_ge(s["product_out"], q - 2 * KT + 1)
                        act.wait_ge(s["inverse_out"], q - 2 * KT + 1)
                    ring.full(act, ("den", n, m))
                    act.activation(den[n % 2][:, m, :], bank(("den", n, m)), ACT.Copy,
                                   bias=1e-6).then_inc(s["den_out"], 1)
                    act.wait_ge(s["den_out"], q + 1)
                    act.sem_inc(ring.empty(("den", n, m)), 1)
                    act.activation(guess[n % 2][:, m, :], den[n % 2][:, m, :], ACT.Ln).then_inc(s["ln_out"], 1)
                for m in range(KT):
                    act.wait_ge(s["ln_out"], n * KT + m + 1)
                    act.activation(guess[n % 2][:, m, :], guess[n % 2][:, m, :], ACT.Exp,
                                   scale=-1.0).then_inc(s["guess_out"], 1)

            def compare(n):
                for q, u, start, end, _ in numbered(n, "act"):
                    act.wait_ge(s["bank_read"], n + 1)
                    if q >= 2:
                        act.wait_ge(compared_out["act"], q - 1)
                    act.activation(sign[:, q % 2, :].bitcast(BF16), spread_scores[:, start:end], ACT.Sign,
                                   bias=rows[:, u, 2 * D:2 * D + 1], scale=-1.0).then_inc(s["sign_out"], 1)
                    act.wait_ge(s["sign_out"], q + 1)
                    if q >= 4:
                        act.wait_ge(counted["act"], q - 3)
                    part = 1 + n - u // BT
                    act.activation(compared["act"][q % 4], sign[:, q % 2, :].bitcast(BF16), ACT.Relu, scale=-1.0,
                                   accum_out=higher[:, u, part:part + 1]).then_inc(compared_out["act"], 1)

            guesses(0)
            for m in range(KT):
                ring.full(act, ("kvo", m))
                act.activation(kvo[:, m, :], bank(("kvo", m)), ACT.Copy, scale=-1.0).then_inc(s["kvo_out"], 1)
                act.wait_ge(s["kvo_out"], m + 1)
                act.sem_inc(ring.empty(("kvo", m)), 1)
            guesses(1)
            for n in range(NB):
                if n + 2 < NB:
                    guesses(n + 2)
                norm(n)
                diagonals(n)
                if n:
                    compare(n - 1)

        @block.tensor
        def _(pe):
            def spread(n):
                for i in range(BT):
                    t = n * BT + i
                    pe.wait_ge(s["diagonal_out"], t + 1)
                    pe.matmul(ps[:, n, i * P:(i + 1) * P], c(k, "ones"), diagonal[:, i, :], start=True,
                              stop=True).then_inc(s["broadcast"], 1)

            def count(engine, q, u, start, end, own):
                pe.wait_ge(compared_out[engine], q + 1)
                which = compared[engine][q % len(compared[engine])]
                for t in range(start // P + own, end // P):
                    at = t * P - start
                    mm = pe.matmul(ps[:, 4, t:t + 1], which[:, at:at + P], one, start=(u == 0 and t == 1),
                                   stop=(u == t - 1), skip_group_check=True)
                mm.then_inc(counted[engine], 1)

            def denominator(n, m):
                ring.free(pe, ("den", n, m))
                pe.matmul(bank(("den", n, m)), k.ksum[:, m, :], k.qt[:, m, n * BW:(n + 1) * BW],
                          start=True, stop=True).then_inc(ring.filled, 1)

            for m in range(KT):
                denominator(0, m)
            for m in range(KT):
                if m == 0:
                    pe.wait_ge(k.wo_in, 16)
                ring.free(pe, ("kvo", m))
                pe.matmul(bank(("kvo", m)), k.vk[:, m, :], w_o[:, m, :], start=True,
                          stop=True).then_inc(ring.filled, 1)
            pe.wait_ge(s["kvo_out"], KT)
            for n in range(NB):
                for i in range(BT):
                    ring.free(pe, ("out", n, i))
                    for m in range(KT):
                        if i == 0:
                            pe.wait_ge(s["out_t"], n * KT + m + 1)
                        mm = pe.matmul(bank(("out", n, i)), out_t[n % 2][:, m, i * P:(i + 1) * P],
                                       kvo[:, m, :], start=(m == 0), stop=(m == KT - 1))
                    mm.then_inc(ring.filled, 1)
                    for which in after.get((n, i), []):
                        denominator(*which)
                if n >= 1:
                    spread(n - 1)
                if n >= 2:
                    for engine in ("dve", "act"):
                        for comparison in numbered(n - 2, engine):
                            count(engine, *comparison)
            spread(NB - 1)
            for comparison in numbered(NB - 2, "dve"):
                count("dve", *comparison)
            on_act = numbered(NB - 2, "act")
            for j, comparison in enumerate(numbered(NB - 1, "dve")):
                count("dve", *comparison)
                if j % 2 and j // 2 < len(on_act):
                    count("act", *on_act[j // 2])
            for comparison in on_act[len(numbered(NB - 1, "dve")) // 2:]:
                count("act", *comparison)
            ring.all_drained(pe)
            pe.wait_ge(s["chosen"], 1)
            pe.matmul(ps[:, 5, 0:NT], c(k, "before"), chosen, start=True, stop=True)
            pe.matmul(ps[:, 5, NT:2 * NT], c(k, "ones"), chosen, start=True, stop=True).then_inc(s["placed"], 1)
            pe.wait_ge(s["number_out"], 1)
            for t in range(NT):
                pe.wait_ge(s["onehot_out"], t + 1)
                for a in range(ST):
                    mm = pe.matmul(ps[:, 6 + a, 0:2], onehot[t % 4][:, a * P:(a + 1) * P], number[:, t, :],
                                   start=(t == 0), stop=(t == NT - 1))
                mm.then_inc(s["found"], 1)

        @block.vector
        def _(dve):
            def done(ins):
                dve_done(dve, ins)

            def residual(n, i):
                t = n * BT + i
                x = rows[:, t, 0:D]
                ring.full(dve, ("out", n, i))
                dve.tensor_tensor(x, bank(("out", n, i)), x, ALU.add).then_inc(ring.empty(("out", n, i)), 1)
                dve.wait_ge(ring.empty(("out", n, i)), ring.at[("out", n, i)] // 3 + 1)
                done(dve.bn_stats(stats[:, i, :], x))
                ins = dve.bn_aggr(mv[:, i, :], stats[:, i, :])
                if i == BT - 1:
                    ins.then_inc(s["ln_stats"], 1)

            def inverse(n, m):
                q = n * KT + m
                dve.wait_ge(s["product_out"], q + 1)
                if q >= 2:
                    dve.wait_ge(s["out_t"], q - 1)
                dve.scalar_tensor_tensor(inv[:, q % 2, :], product[:, q % 2, :], -2.0, guess[n % 2][:, m, :],
                                         ALU.add, ALU.mult).then_inc(s["inverse_out"], 1)
                if n < 2:
                    dve.wait_ge(s["inverse_out"], q + 1)
                    dve.tensor_tensor(out_t[n % 2][:, m, :], inv[:, q % 2, :], k.qt[:, m, n * BW:(n + 1) * BW],
                                      ALU.mult).then_inc(s["out_t"], 1)

            def shifts(n):
                dve.wait_ge(s["ln_rstd"], n + 1)
                dve.scalar_tensor_tensor(shift, mv[:, :, 0], -1.0, rstd, ALU.mult,
                                         ALU.mult).then_inc(s["shift_out"], 1)

            def score(n):
                if n == 0:
                    dve.wait_ge(s["router_in"], 16)
                for i in range(BT):
                    t = n * BT + i
                    dve.wait_ge(s["norm_out"], t + 1)
                    if t:
                        dve.wait_ge(s["score_out"], t)
                    dve.tensor_tensor_reduce(junk, rows[:, t, D:2 * D], router, 1.0, 0.0, ALU.mult, ALU.add,
                                             rows[:, t, 2 * D:2 * D + 1]).then_inc(s["score_out"], 1)

            def compare(n):
                dve.wait_ge(s["broadcast"], (n + 1) * BT)
                for q, u, start, end, own in numbered(n, "dve"):
                    if q >= 8:
                        dve.wait_ge(counted["dve"], q - 7)
                        dve.wait_ge(compared_out["dve"], q - 7)
                    if own:
                        ties(u)
                    part = 1 + n - u // BT
                    dve.tensor_scalar(compared["dve"][q % 8][:, 0:end - start], spread_scores[:, start:end],
                                      rows[:, u, 2 * D:2 * D + 1], 0.0, ALU.is_gt, ALU.add,
                                      accum_out=higher[:, u, part:part + 1]).then_inc(compared_out["dve"], 1)
                u = (n + 1) * BT - 1
                ties(u)
                done(dve.tensor_scalar(tied, spread_scores[:, u * P:(u + 1) * P], rows[:, u, 2 * D:2 * D + 1], 0.0,
                                       ALU.is_gt, ALU.add, accum_out=higher[:, u, 1:2]))
                dve.sem_inc(s["bank_read"], 1)

            def ties(u):
                done(dve.scalar_tensor_tensor(tied, spread_scores[:, u * P:(u + 1) * P],
                                              rows[:, u, 2 * D:2 * D + 1], c(k, "earlier"), ALU.is_equal,
                                              ALU.mult, accum_out=higher[:, u, 0:1]))

            done(dve.memset(higher, 0.0))
            done(dve.memset(one, 1.0))
            for n in range(NB + 1):
                if n == 1:
                    for i in range(BT - 1):
                        residual(0, i)
                    inverse(1, 0)
                    inverse(1, 1)
                    residual(0, BT - 1)
                    inverse(1, 2)
                    inverse(1, 3)
                else:
                    for i in range(BT):
                        if n:
                            residual(n - 1, i)
                        if n < NB:
                            inverse(n, i)
                if n:
                    shifts(n - 1)
                    score(n - 1)
                if n >= 2:
                    compare(n - 2)
            compare(NB - 1)
            dve.wait_ge(compared_out["dve"], all_of("dve"))
            dve.wait_ge(compared_out["act"], all_of("act"))
            done(dve.tensor_reduce(ahead, higher, AX.X, ALU.add))
            dve.wait_ge(counted["dve"], all_of("dve"))
            dve.wait_ge(counted["act"], all_of("act"))
            done(dve.tensor_tensor(ahead[:, 1:NT], ahead[:, 1:NT], ps[:, 4, 1:NT], ALU.subtract))
            done(dve.scalar_tensor_tensor(ahead, c(k, "number")[:, 1:2 * NT:2], 1.0 * P, ahead, ALU.mult, ALU.add))
            dve.tensor_scalar(chosen, ahead, float(SEL), None, ALU.is_lt).then_inc(s["chosen"], 1)
            dve.wait_ge(s["chosen"], 1)
            done(dve.tensor_scalar(past, chosen, -1.0 * T, 1.0 * T, ALU.mult, ALU.add))
            dve.wait_ge(s["placed"], 1)
            done(dve.tensor_copy(total, ps[:, 5, NT:2 * NT]))
            done(dve.tensor_tensor_scan(place, c(k, "ones")[:, 0:NT], total, 0.0, ALU.mult, ALU.add))
            done(dve.tensor_tensor(place, place, total, ALU.subtract))
            done(dve.tensor_tensor(place, ps[:, 5, 0:NT], place, ALU.add))
            done(dve.tensor_tensor(place, place, past, ALU.add))
            for t in range(NT):
                if t >= 4:
                    dve.wait_ge(s["found"], t - 3)
                dve.tensor_scalar(onehot[t % 4], c(k, "slot"), place[:, t:t + 1], None,
                                  ALU.is_equal).then_inc(s["onehot_out"], 1)
            dve.wait_ge(s["found"], NT)
            for a in range(ST):
                ins = dve.tensor_copy(found[:, a:a + 1], ps[:, 6 + a, 0:1])
            done(ins)
            for a in range(ST):
                ins = dve.scalar_tensor_tensor(found[:, a:a + 1], ps[:, 6 + a, 1:2], float(P), found[:, a:a + 1],
                                               ALU.mult, ALU.add)
            done(ins)
            done(dve.tensor_copy(k.token, found))


def plan_stream():
    order = [("k", i) for i in range(4)] + [("q", 0)] + [("v", i) for i in range(4)]
    for step in range(1, NHK + 4):
        if step < NHK:
            order.append(("q", step))
        if step >= 4:
            order.append(("wo", step - 4))
    for step in range(NHK + 1):
        if step < NHK:
            order += [("gate", step), ("up", step)]
        if step:
            order.append(("down", step - 1))
    return order


CHUNKS = plan_stream()
CH = 1024
SLOTS = 8


def hidden_of(sel, j):
    return sel[:, j, D:2 * D]


def residual_of(sel, j):
    return sel[:, j, 0:D]


def selected_layer(k):
    nc, io, ps = k.nc, k.io, k.ps
    put = Place(k.arena, 0, k.arena_size)
    sel, xs, ht, kt = put(ST, ROW), put(ST, D), put(KT, SEL), put(NHK, SEL)
    v, b_v, raw, qt = put(ST, NHK * HD), put(NHK * HD), put(2, 2, SEL), put(2, 2, SEL)
    turn, cosine, t1, t2 = put(ST, 2 * P), put(2, SEL), put(2, SEL), put(2, SEL)
    prob, prob_t, attn = [put(2, 3 * P) for _ in range(2)], put(2, 3 * P), put(4, SEL)
    silu, hid = put(2, 2, SEL), put(3, 2, SEL)
    x1, x1s, rest, fin, junk = put(ST, D), put(ST, D), put(ST, D), put(ST, D), put(D)
    tiny = Place(k.small, 0, k.token_at)
    ss, ms, rstd, gate, left = tiny(ST), tiny(ST), tiny(ST), tiny(ST), tiny(ST)
    token = k.token
    top, total, inv = tiny(4, 2), tiny(4, 2), tiny(4, 2)
    ln1, ln2, b_q, b_k = tiny(KT), tiny(KT), tiny(NHQ), tiny(NHK)
    slots = [k.xnt[:, i * CH:(i + 1) * CH] for i in range(SLOTS)]

    def chunk(what, i):
        a = slots[CHUNKS.index((what, i)) % SLOTS]
        return a.rearrange("p (a b) -> p a b", b=D if what in ("wo", "down") else 2 * P)

    tasks = [("xT", a) for a in range(2)] + [("turnT",)] + [("k", i) for i in range(4)]
    tasks += [("q", 0)] + [("v", i) for i in range(4)]
    for step in range(1, NHK + 4):
        if step < NHK:
            tasks.append(("q", step))
        if step <= NHK:
            tasks += [("S", step - 1, hh) for hh in range(2)]
        if 3 <= step <= NHK + 2:
            tasks += [("PV", step - 3, hh) for hh in range(2)]
        if 2 <= step <= NHK + 1:
            tasks += [("PT", step - 2, hh) for hh in range(2)]
    tasks += [("x1T", a) for a in range(2)]
    for i in range(NHK):
        tasks += [("gate", i), ("up", i)]
    ring = Ring(k.sem, "last", [2, 3, 4, 5, 6, 7], tasks)
    s = sems(k, "last", """rows_in small_in rms_in rms_out xs_out ht_out turns_in turn_out raw_out roped
             v_out masked exp_out prob_out pt_out attn_out wo_done x1_out rms2_in rms2_out x1s_out h2_out silu_out
             hid_out down_done fin_out out_stored kt_out gate_out""")
    chunk_in = [k.sem(f"chunk_in{i}") for i in range(SLOTS)]
    dve_done, act_done, pool_done = k.chain["dve"], k.chain["act"], k.chain["pool"]
    scale = float(HD) ** -0.5

    def bank(task):
        return ps[:, ring.bank(task), :]

    def two(a, n=SEL):
        return a.rearrange("p (a b) -> p a b", b=n)

    with nc.Block() as block:

        @block.sync
        def _(sp):
            for to, what in ((ln1, "ln1"), (ln2, "ln2"), (b_q, "bq"), (b_k, "bk")):
                sp.dma_start(to, io[what]).then_inc(s["small_in"], 16)
            sp.dma_start(b_v, io["bv"].partition_broadcast(P)).then_inc(s["small_in"], 16)
            for n, (what, i) in enumerate(CHUNKS):
                if n >= SLOTS:
                    before, j = CHUNKS[n - SLOTS]
                    if before in ("wo", "down"):
                        sp.wait_ge(s[f"{before}_done"], j + 1)
                    else:
                        sp.wait_ge(ring.filled, ring.at[(before, j)] + 1)
                sp.dma_start(slots[n % SLOTS], io["chunks"][n]).then_inc(chunk_in[n % SLOTS], 16)

        @block.gpsimd
        def _(pool):
            def rsqrt(count, ready, out):
                pool.wait_ge(ready, count)
                pool_done(pool, pool.tensor_scalar(ms, ss, 1.0 / D, 1e-6, ALU.mult, ALU.add))
                pool.tensor_tensor(rstd, ms, c(k, "neghalf")[:, 0:ST], ALU.pow).then_inc(out, 1)

            pool.wait_ge(k.rows_stored, 16 * NB)
            for j in range(ST):
                pool.indirect_dma_start(
                    out=sel[:, j, :], out_offset=None, in_=k.kept[:, :],
                    in_offset=bass.IndirectOffsetOnAxis(ap=token[:, j:j + 1], axis=0), bounds_check=T - 1,
                    oob_is_err=False).then_inc(s["rows_in"], 16)
            for j in range(ST):
                pool.indirect_dma_start(
                    out=turn[:, j, :], out_offset=None, in_=io["turns"],
                    in_offset=bass.IndirectOffsetOnAxis(ap=token[:, j:j + 1], axis=0), bounds_check=T - 1,
                    oob_is_err=False).then_inc(s["turns_in"], 16)
            rsqrt(1, s["rms_in"], s["rms_out"])
            rsqrt(1, s["rms2_in"], s["rms2_out"])
            for i in range(2):
                pool.wait_ge(k.base_in[i], 16 * (NT // 2))
            for j in range(ST):
                pool.wait_ge(s["fin_out"], j + 1)
                pool.indirect_dma_start(
                    out=io["out"], out_offset=bass.IndirectOffsetOnAxis(ap=token[:, j:j + 1], axis=0),
                    in_=fin[:, j, :], in_offset=None, bounds_check=T - 1,
                    oob_is_err=False).then_inc(s["out_stored"], 16)
            pool.wait_ge(s["out_stored"], 16 * ST)

        @block.scalar
        def _(act):
            def spread(task, ln, out):
                a = task[1]
                ring.full(act, task)
                for b in range(2):
                    m = a * 2 + b
                    ins = act.activation(ht[:, m, :], bank(task)[:, b * SEL:(b + 1) * SEL], ACT.Copy,
                                         scale=ln[:, m:m + 1])
                ins.then_inc(out, 1)
                act.wait_ge(out, a + 1)
                act.sem_inc(ring.empty(task), 1)

            def biased(task, bias, r):
                if r >= 2:
                    act.wait_ge(s["roped"], r - 1)
                ring.full(act, task)
                for hh in range(2):
                    h = 2 * task[1] + hh
                    ins = act.activation(raw[:, r % 2, hh, :], bank(task)[:, hh * SEL:(hh + 1) * SEL],
                                         ACT.Identity, bias=bias[:, h:h + 1])
                ins.then_inc(s["raw_out"], 1)
                act.wait_ge(s["raw_out"], r + 1)
                act.sem_inc(ring.empty(task), 1)

            act.wait_ge(s["rows_in"], 16 * ST)
            act.activation(gate, sel[:, :, 2 * D], ACT.Sigmoid).then_inc(s["gate_out"], 1)
            act.wait_ge(s["small_in"], 16 * 5)
            for a in range(2):
                spread(("xT", a), ln1, s["ht_out"])
            ring.full(act, ("turnT",))
            act.activation(cosine, two(bank(("turnT",))), ACT.Copy).then_inc(s["turn_out"], 1)
            act.wait_ge(s["turn_out"], 1)
            act.sem_inc(ring.empty(("turnT",)), 1)
            for i in range(4):
                biased(("k", i), b_k, i)
            biased(("q", 0), b_q, 4)
            for step in range(1, NHK + 4):
                if step < NHK:
                    biased(("q", step), b_q, 4 + step)
                if step <= NHK:
                    i = step - 1
                    for hh in range(2):
                        h = 2 * i + hh
                        act.wait_ge(s["masked"], h + 1)
                        for part, cols in enumerate((slice(0, P), slice(P, 3 * P))):
                            ins = act.activation(prob[i % 2][:, hh, cols], prob[i % 2][:, hh, cols], ACT.Exp,
                                                 bias=top[:, h % 4, part:part + 1], scale=scale,
                                                 accum_out=total[:, h % 4, part:part + 1])
                        ins.then_inc(s["exp_out"], 1)
                if 3 <= step <= NHK + 2:
                    i = step - 3
                    for hh in range(2):
                        if i >= 2:
                            act.wait_ge(s["wo_done"], i - 1)
                        ring.full(act, ("PV", i, hh))
                        act.activation(attn[:, (2 * i + hh) % 4, :], bank(("PV", i, hh))[:, 0:SEL],
                                       ACT.Copy).then_inc(s["attn_out"], 1)
                        act.wait_ge(s["attn_out"], 2 * i + hh + 1)
                        act.sem_inc(ring.empty(("PV", i, hh)), 1)
                if 2 <= step <= NHK + 1:
                    i = step - 2
                    for hh in range(2):
                        ring.full(act, ("PT", i, hh))
                        act.activation(prob_t[:, hh, :], bank(("PT", i, hh))[:, 0:3 * P],
                                       ACT.Copy).then_inc(s["pt_out"], 1)
                        act.wait_ge(s["pt_out"], 2 * i + hh + 1)
                        act.sem_inc(ring.empty(("PT", i, hh)), 1)
            for a in range(2):
                spread(("x1T", a), ln2, s["h2_out"])
            for i in range(NHK):
                if i >= 2:
                    act.wait_ge(s["hid_out"], i - 1)
                ring.full(act, ("gate", i))
                act.activation(silu[:, i % 2, :, :], two(bank(("gate", i))), ACT.Silu).then_inc(s["silu_out"], 1)
                act.wait_ge(s["silu_out"], i + 1)
                act.sem_inc(ring.empty(("gate", i)), 1)

        @block.tensor
        def _(pe):
            ident = c(k, "ident")

            def arrived(what, i):
                n = CHUNKS.index((what, i))
                pe.wait_ge(chunk_in[n % SLOTS], 16 * (n // SLOTS + 1))

            def turn_rows(name, x):
                for a in range(2):
                    ring.free(pe, (name, a))
                    for b in range(2):
                        m = a * 2 + b
                        for j in range(ST):
                            mm = pe.transpose(bank((name, a))[:, b * SEL + j * P:b * SEL + (j + 1) * P],
                                              x[:, j, m * P:(m + 1) * P], ident)
                    mm.then_inc(ring.filled, 1)

            def features(what, i):
                arrived(what, i)
                ring.free(pe, (what, i))
                for hh in range(2):
                    for j in range(KT):
                        mm = pe.matmul(bank((what, i))[:, hh * SEL:(hh + 1) * SEL],
                                       chunk(what, i)[:, j, hh * P:(hh + 1) * P], ht[:, j, :],
                                       start=(j == 0), stop=(j == KT - 1))
                mm.then_inc(ring.filled, 1)

            pe.wait_ge(s["xs_out"], 1)
            turn_rows("xT", xs)
            pe.wait_ge(s["turns_in"], 16 * ST)
            ring.free(pe, ("turnT",))
            for b in range(2):
                for j in range(ST):
                    mm = pe.transpose(bank(("turnT",))[:, b * SEL + j * P:b * SEL + (j + 1) * P],
                                      turn[:, j, b * P:(b + 1) * P], ident)
            mm.then_inc(ring.filled, 1)
            pe.wait_ge(s["ht_out"], 2)
            for i in range(4):
                features("k", i)
            features("q", 0)
            for i in range(4):
                arrived("v", i)
                ring.free(pe, ("v", i))
                for a in range(ST):
                    for j in range(KT):
                        mm = pe.matmul(bank(("v", i))[:, a * 2 * P:(a + 1) * 2 * P], ht[:, j, a * P:(a + 1) * P],
                                       chunk("v", i)[:, j, :], start=(j == 0), stop=(j == KT - 1))
                mm.then_inc(ring.filled, 1)
            for step in range(1, NHK + 4):
                if step < NHK:
                    features("q", step)
                if step <= NHK:
                    i = step - 1
                    pe.wait_ge(s["roped"], 4 + i + 1)
                    for hh in range(2):
                        ring.free(pe, ("S", i, hh))
                        b = bank(("S", i, hh))
                        pe.matmul(b[:, 0:P], qt[:, i % 2, hh, 0:P], kt[:, i, 0:P], start=True, stop=True)
                        pe.matmul(b[:, P:3 * P], qt[:, i % 2, hh, P:2 * P], kt[:, i, :],
                                  start=True, stop=True).then_inc(ring.filled, 1)
                if step >= 4:
                    i = step - 4
                    arrived("wo", i)
                    pe.wait_ge(s["attn_out"], 2 * i + 2)
                    for hh in range(2):
                        for j in range(ST):
                            mm = pe.matmul(ps[:, j, :], attn[:, (2 * i + hh) % 4, j * P:(j + 1) * P],
                                           chunk("wo", i)[:, hh, :], start=(i == 0 and hh == 0),
                                           stop=(i == NHK - 1 and hh == 1), skip_group_check=True)
                    mm.then_inc(s["wo_done"], 1)
                if 3 <= step <= NHK + 2:
                    i = step - 3
                    if i == 0:
                        pe.wait_ge(s["v_out"], 4)
                    for hh in range(2):
                        pe.wait_ge(s["pt_out"], 2 * i + hh + 1)
                        ring.free(pe, ("PV", i, hh))
                        b = bank(("PV", i, hh))
                        vh = slice(i * HD, (i + 1) * HD)
                        pe.matmul(b[:, 0:SEL], v[:, 0, vh], prob_t[:, hh, 0:2 * P], start=True, stop=True)
                        pe.matmul(b[:, P:2 * P], v[:, 1, vh], prob_t[:, hh, 2 * P:3 * P], start=False,
                                  stop=True, skip_group_check=True).then_inc(ring.filled, 1)
                if 2 <= step <= NHK + 1:
                    i = step - 2
                    for hh in range(2):
                        pe.wait_ge(s["prob_out"], 2 * i + hh + 1)
                        ring.free(pe, ("PT", i, hh))
                        for part in range(3):
                            r = slice(part * P, (part + 1) * P)
                            mm = pe.transpose(bank(("PT", i, hh))[:, r], prob[i % 2][:, hh, r], ident)
                        mm.then_inc(ring.filled, 1)
            pe.wait_ge(s["x1s_out"], 1)
            turn_rows("x1T", x1s)
            pe.wait_ge(s["h2_out"], 2)
            for step in range(NHK + 1):
                if step < NHK:
                    features("gate", step)
                    features("up", step)
                if step:
                    i = step - 1
                    arrived("down", i)
                    pe.wait_ge(s["hid_out"], i + 1)
                    for b in range(2):
                        for j in range(ST):
                            mm = pe.matmul(ps[:, j, :], hid[:, i % 3, b, j * P:(j + 1) * P],
                                           chunk("down", i)[:, b, :], start=(i == 0 and b == 0),
                                           stop=(i == NHK - 1 and b == 1), skip_group_check=True)
                    mm.then_inc(s["down_done"], 1)

        @block.vector
        def _(dve):
            def done(ins):
                dve_done(dve, ins)

            def rope(r, out, out_sem):
                dve.wait_ge(s["raw_out"], r + 1)
                if r:
                    dve.wait_ge(s["roped"], r)
                x = raw[:, r % 2, :, :]
                lo, hi = slice(0, 64), slice(64, 128)
                co = cosine[:, 0, :].unsqueeze(1).to_broadcast((P, 2, SEL))
                si = cosine[:, 1, :].unsqueeze(1).to_broadcast((P, 2, SEL))
                dve.tensor_tensor(t1, x, co, ALU.mult)
                dve.tensor_tensor(t2[lo], x[hi], si[hi], ALU.mult)
                done(dve.tensor_tensor(t2[hi], x[lo], si[lo], ALU.mult))
                dve.tensor_tensor(out, t1, t2, ALU.add).then_inc(s["roped"], 1)

            def square_mean(x, ready):
                for j in range(ST):
                    ins = dve.tensor_tensor_reduce(junk, x(j), x(j), 1.0, 0.0, ALU.mult, ALU.add,
                                                   ss[:, j:j + 1])
                    if j == 0:
                        done(ins)
                ins.then_inc(ready, 1)

            dve.wait_ge(s["rows_in"], 16 * ST)
            square_mean(lambda j: hidden_of(sel, j), s["rms_in"])
            dve.wait_ge(s["rms_out"], 1)
            for j in range(ST):
                ins = dve.tensor_scalar(xs[:, j, :], hidden_of(sel, j), rstd[:, j:j + 1], None, ALU.mult)
            ins.then_inc(s["xs_out"], 1)
            dve.wait_ge(s["gate_out"], 1)
            dve.tensor_scalar(left, gate, -1.0, 1.0, ALU.mult, ALU.add)
            dve.wait_ge(s["turn_out"], 1)
            for i in range(4):
                rope(i, kt[:, 2 * i:2 * i + 2, :], s["kt_out"])
            rope(4, qt[:, 0, :, :], None)
            dve.wait_ge(s["small_in"], 16 * 5)
            for i in range(4):
                r = slice(i * 2 * P, (i + 1) * 2 * P)
                ring.full(dve, ("v", i))
                dve.tensor_tensor(v[:, :, r], two(bank(("v", i))), b_v[:, r].unsqueeze(1).to_broadcast((P, ST, 2 * P)),
                                  ALU.add).then_inc(s["v_out"], 1)
                dve.wait_ge(s["v_out"], i + 1)
                dve.sem_inc(ring.empty(("v", i)), 1)
            for step in range(1, NHK + 1):
                if step < NHK:
                    rope(4 + step, qt[:, step % 2, :, :], None)
                i = step - 1
                for hh in range(2):
                    h = 2 * i + hh
                    p, most = prob[i % 2][:, hh, :], top[:, h % 4, :]
                    ring.full(dve, ("S", i, hh))
                    if i >= 2:
                        ring.full(dve, ("PT", i - 2, hh))
                    dve.tensor_tensor(p, bank(("S", i, hh))[:, 0:3 * P], c(k, "addmask"),
                                      ALU.add).then_inc(ring.empty(("S", i, hh)), 1)
                    dve.wait_ge(ring.empty(("S", i, hh)), ring.at[("S", i, hh)] // 6 + 1)
                    dve.tensor_reduce(most[:, 0:1], p[:, 0:P], AX.X, ALU.max)
                    done(dve.tensor_reduce(most[:, 1:2], p[:, P:3 * P], AX.X, ALU.max))
                    dve.tensor_scalar(most, most, -scale, None, ALU.mult).then_inc(s["masked"], 1)
                for hh in range(2):
                    h = 2 * i + hh
                    p, by = prob[i % 2][:, hh, :], inv[:, h % 4, :]
                    dve.wait_ge(s["exp_out"], h + 1)
                    done(dve.reciprocal(by, total[:, h % 4, :]))
                    dve.tensor_scalar(p[:, 0:P], p[:, 0:P], by[:, 0:1], None, ALU.mult)
                    dve.tensor_scalar(p[:, P:3 * P], p[:, P:3 * P], by[:, 1:2], None,
                                      ALU.mult).then_inc(s["prob_out"], 1)
            dve.wait_ge(s["wo_done"], NHK)
            for j in range(ST):
                ins = dve.tensor_tensor(x1[:, j, :], ps[:, j, :], hidden_of(sel, j),
                                        ALU.add)
            done(ins)
            square_mean(lambda j: x1[:, j, :], s["rms2_in"])
            dve.wait_ge(s["rms2_out"], 1)
            for j in range(ST):
                ins = dve.tensor_scalar(x1s[:, j, :], x1[:, j, :], rstd[:, j:j + 1], None, ALU.mult)
            ins.then_inc(s["x1s_out"], 1)
            for j in range(ST):
                done(dve.scalar_tensor_tensor(rest[:, j, :], hidden_of(sel, j), left[:, j:j + 1],
                                              residual_of(sel, j), ALU.mult, ALU.add))
                done(dve.scalar_tensor_tensor(rest[:, j, :], x1[:, j, :], gate[:, j:j + 1], rest[:, j, :],
                                              ALU.mult, ALU.add))
            for i in range(NHK):
                ring.full(dve, ("up", i))
                dve.wait_ge(s["silu_out"], i + 1)
                if i >= 3:
                    dve.wait_ge(s["down_done"], i - 2)
                dve.tensor_tensor(hid[:, i % 3, :, :], two(bank(("up", i))), silu[:, i % 2, :, :],
                                  ALU.mult).then_inc(s["hid_out"], 1)
                dve.wait_ge(s["hid_out"], i + 1)
                dve.sem_inc(ring.empty(("up", i)), 1)
            dve.wait_ge(s["down_done"], NHK)
            for j in range(ST):
                dve.scalar_tensor_tensor(fin[:, j, :], ps[:, j, :], gate[:, j:j + 1], rest[:, j, :], ALU.mult,
                                         ALU.add).then_inc(s["fin_out"], 1)


def build(nc, io):
    with ExitStack() as ctx:
        ctx.enter_context(nc.allow_non_contiguous_dma("weights in tiles"))
        k = setup(nc, ctx, io)
        k.expert_in = nc.dram_tensor("expert_in", (NE * CAP, D), F32, kind="Internal").ap()
        k.expert_out = nc.dram_tensor("expert_out", (NE * CAP, D), F32, kind="Internal").ap()
        k.given = k.sem("rows_given")
        k.kept = nc.dram_tensor("rows_kept", (T, ROW), F32, kind="Internal").ap()
        k.attention_in = k.sem("attention_weights_in")
        k.w_in, k.xe_in = ([k.sem(f"{n}{p}") for p in range(2)] for n in ("w_expert_in", "rows_in"))
        k.base_in = [k.sem(f"base_stored{i}") for i in range(2)]
        k.wo_in = k.sem("wo_in")
        k.x2nt = [k.xnt[:, n * KT * BW:(n + 1) * KT * BW].rearrange("p (a b) -> p a b", b=BW) for n in range(NB)]
        k.gate_in = k.sem("gate_in")
        k.gate_w = k.arena[:, k.arena_size - KT * NE:k.arena_size].rearrange("p (a b) -> p a b", b=NE)
        k.w_shared = k.arena[:, 0:KT * 2 * FI + FM * D]
        k.s_shared = k.sem("shared_in")
        k.y_stored = [k.sem(f"y_stored{p}") for p in range(2)]
        k.phase_sems.clear()
        gated_linear_attention(k)
        expert_memory(k)
        route_and_shared(k)
        recycle(k)
        attention_memory(k)
        experts(k)
        linear_attention_sums(k)
        linear_attention(k)
        selected_layer(k)


def layout(inputs):
    f = {n: np.asarray(a) for n, a in inputs.items()}

    def rows_first(w):
        return np.ascontiguousarray(w.reshape(-1, P, w.shape[1]).transpose(1, 0, 2))

    def expert(w1, w3, w2):
        up = np.concatenate([rows_first(w1.T), rows_first(w3.T)], axis=2).reshape(P, -1)
        w2t = np.concatenate([w2.T, np.zeros((FM * P - FI, D), np.float32)], axis=0)
        return np.concatenate([up, rows_first(w2t).reshape(P, -1)], axis=1)

    out = {"consts": constants(), "x": np.ascontiguousarray(f["L0_attn_hidden_states"].reshape(T, D))}
    out["w_qk"] = rows_first(np.concatenate([f["L0_attn_Wq"].T] * 4 + [f["L0_attn_Wk"].T] * 4, axis=1))
    out["w_ig"] = rows_first(f["L0_attn_Wig"].T)
    out["w_og"] = rows_first(f["L0_attn_Wog"].T)
    out["g_weight"] = f["L0_attn_g_weight"]
    out["w_shared"] = expert(f["L0_ffn_Ws1"], f["L0_ffn_Ws3"], f["L0_ffn_Ws2"])
    w = {n: f[f"L1_ffn_{n}"] for n in ("wq", "wk", "wv", "wo", "w_gate", "w_up", "w_down")}
    source = {"q": w["wq"], "k": w["wk"], "v": w["wv"], "wo": w["wo"], "gate": w["w_gate"], "up": w["w_up"],
              "down": w["w_down"]}
    chunks = []
    for what, i in CHUNKS:
        part = slice(i * 2 * P, (i + 1) * 2 * P)
        a = source[what][part, :] if what in ("wo", "down") else source[what][:, part]
        chunks.append(rows_first(a).reshape(P, CH))
    out["chunks"] = np.stack(chunks)
    for n, m in (("ln1", "ln1_w"), ("ln2", "ln2_w"), ("bq", "bq"), ("bk", "bk")):
        out[n] = np.ascontiguousarray(f[f"L1_ffn_{m}"].reshape(-1, P).T)
    out["bv"] = f["L1_ffn_bv"]
    out["turns"] = turns()
    out["w_attention"] = np.concatenate(
        [rows_first(f[f"L1_attn_W{n}"].T).reshape(P, -1) for n in "qkvo"], axis=1)
    for n in "kvo":
        out[f"b_{n}"] = f[f"L1_attn_b{n}"]
    out["b_q"] = np.ascontiguousarray(f["L1_attn_bq"].reshape(KT, P).T)
    out["decay_row"] = np.exp(-np.arange(T, dtype=np.float32) / np.float32(T))
    out["w_router"] = f["L1_ffn_w_router"]
    out["gate_w"] = rows_first(f["L0_ffn_gate_w"].T)
    out["gate_b"] = f["L0_ffn_gate_b"]
    out["w_expert"] = np.stack([expert(f["L0_ffn_W1"][e], f["L0_ffn_W3"][e], f["L0_ffn_W2"][e]) for e in range(NE)])
    return out


def kernel(**inputs):
    import concourse.bacc as _bacc
    from concourse.bass_utils import run_bass_kernel_spmd as _run

    nc = _bacc.Bacc("TRN2", target_bir_lowering=False, num_devices=1)
    arrays, io = {}, {}
    for name, a in layout(inputs).items():
        arrays[f"in_{name}_dram"] = a
        io[name] = nc.dram_tensor(f"in_{name}_dram", a.shape, mybir.dt.from_np(a.dtype), kind="ExternalInput").ap()
    io["out"] = nc.dram_tensor("out_0_dram", (T, D), F32, kind="ExternalOutput").ap()
    build(nc, io)
    r = _run(nc, [arrays], core_ids=[0])
    return r.results[0]["out_0_dram"].reshape(1, T, D)
```
